# Optimizing a Trainium2 kernel written in Bass

```python
import numpy as np
import jax
import jax.numpy as jnp

def _softmax(x, axis=-1):
    return jax.nn.softmax(x, axis=axis)

def _gelu(x):
    return jax.nn.gelu(x, approximate=True)

def _silu(x):
    return jax.nn.silu(x)

def _sigmoid(x):
    return jax.nn.sigmoid(x)

def _layernorm(x, axis=-1, eps=1e-05):
    m = jnp.mean(x, axis=axis, keepdims=True)
    v = jnp.var(x, axis=axis, keepdims=True)
    return (x - m) / jnp.sqrt(v + eps)

def _scatter_add(tgt, idx, src, axis=0):
    return tgt.at[idx].add(src)

def _segment_sum(src, seg, n):
    return jax.ops.segment_sum(src, seg, n)
kernel_name = 'mk_early_fusion_d1_tok_img768_r4_15b259'

def setup_inputs(seed: int=0):
    np.random.seed(seed)
    _w = jnp.asarray

    def _rec_inputs():
        import jax
        import jax.numpy as jnp
        _rk = jax.random.key(seed)
        x = -0.000356955 + 1 * jax.random.normal(jax.random.fold_in(_rk, 1), (32, 224, 224, 3), jnp.float32)
        txt = 0.00833714 + 1.14623 * jax.random.normal(jax.random.fold_in(_rk, 2), (32, 77, 192), jnp.float32)
        return (x, txt)
    x, txt = _rec_inputs()

    def _L0_tok_setup():
        import jax, jax.numpy as jnp
        import numpy as np
        PATCH = 16
        IMG = 224
        NP_SIDE = IMG // PATCH
        EMBED = 192

        def _patchify(batch_image):
            B = batch_image.shape[0]
            x = batch_image.reshape(B, NP_SIDE, PATCH, NP_SIDE, PATCH, 3)
            x = x.transpose(0, 1, 3, 5, 2, 4)
            return x.reshape(B, NP_SIDE * NP_SIDE, 3 * PATCH * PATCH)
        key = jax.random.key(seed)
        k1, k2, k3, k4, k5 = jax.random.split(key, 5)
        return {'batch_image': jax.random.normal(k1, (128, IMG, IMG, 3), dtype=jnp.float32), 'W': jax.random.normal(k2, (EMBED, 3 * PATCH * PATCH), dtype=jnp.float32) * 0.02, 'b': jax.random.normal(k3, (EMBED,), dtype=jnp.float32) * 0.02, 'cls_token': jax.random.normal(k4, (1, 1, EMBED), dtype=jnp.float32), 'pos_embed': jax.random.normal(k5, (1, NP_SIDE * NP_SIDE + 1, EMBED), dtype=jnp.float32)}
    _L0_tok_all = _L0_tok_setup()
    _L0_tok_in = {k: v for k, v in _L0_tok_all.items() if k in ('W', 'b', 'cls_token', 'pos_embed')}
    del _L0_tok_all

    def _L0_attn_setup():
        import jax, jax.numpy as jnp
        import numpy as np
        ROPE_THETA = 10000.0

        def rope(x):
            B, S, D = x.shape
            half = D // 2
            inv_freq = 1.0 / ROPE_THETA ** (jnp.arange(half, dtype=jnp.float32) * 2.0 / D)
            ang = jnp.arange(S, dtype=jnp.float32)[:, None] * inv_freq[None, :]
            cos, sin = (jnp.cos(ang), jnp.sin(ang))
            x1, x2 = (x[..., 0::2], x[..., 1::2])
            r1 = x1 * cos - x2 * sin
            r2 = x1 * sin + x2 * cos
            return jnp.stack([r1, r2], axis=-1).reshape(B, S, D)
        key = jax.random.key(seed)
        ks = jax.random.split(key, 9)
        B, S, D = (4, 512, 192)
        w = 0.02
        return {'X': jax.random.normal(ks[0], (B, S, D), dtype=jnp.float32), 'Wq': jax.random.normal(ks[1], (D, D), dtype=jnp.float32) * w, 'bq': jnp.zeros((D,), dtype=jnp.float32), 'Wk': jax.random.normal(ks[2], (D, D), dtype=jnp.float32) * w, 'bk': jnp.zeros((D,), dtype=jnp.float32), 'Wv': jax.random.normal(ks[3], (D, D), dtype=jnp.float32) * w, 'bv': jnp.zeros((D,), dtype=jnp.float32), 'Wo': jax.random.normal(ks[4], (D, D), dtype=jnp.float32) * w, 'bo': jnp.zeros((D,), dtype=jnp.float32)}
    _L0_attn_all = _L0_attn_setup()
    _L0_attn_in = {k: v for k, v in _L0_attn_all.items() if k in ('Wq', 'bq', 'Wk', 'bk', 'Wv', 'bv', 'Wo', 'bo')}
    del _L0_attn_all

    def _L0_ffn_setup():
        import jax, jax.numpy as jnp
        import numpy as np
        B, S, H, F = (4, 256, 192, 768)
        EC, EU = (4, 4)
        CAP_FACTOR = 1.0

        def _ffn(x, W1, b1, W2, b2):
            return jax.nn.gelu(x @ W1 + b1, approximate=False) @ W2 + b2

        def _expert_mix(h, route, W1, b1, W2, b2, n_exp):
            out = jnp.zeros_like(h)
            for e in range(n_exp):
                m = (route == e).astype(h.dtype)[:, None]
                out = out + m * _ffn(h, W1[e], b1[e], W2[e], b2[e])
            return out

        def _drop_mask(route, pmax, capacity):
            N = route.shape[0]
            order = jnp.lexsort((-jax.lax.stop_gradient(pmax), route))
            rs = route[order]
            starts = jnp.searchsorted(rs, rs, side='left')
            rank_sorted = jnp.arange(N) - starts
            rank = jnp.zeros((N,), jnp.int32).at[order].set(rank_sorted.astype(jnp.int32))
            return rank >= capacity
        key = jax.random.key(seed)
        ks = jax.random.split(key, 8)

        def w(k, shape, s=0.02):
            return jax.random.normal(k, shape, jnp.float32) * s
        return {'hidden_states': jax.random.normal(ks[0], (B, S, H), jnp.float32), 'Wsc': w(ks[1], (H, EC)), 'bsc': jnp.zeros((EC,), jnp.float32), 'W1c': w(ks[2], (EC, H, F)), 'b1c': jnp.zeros((EC, F), jnp.float32), 'W2c': w(ks[3], (EC, F, H)), 'b2c': jnp.zeros((EC, H), jnp.float32), 'Wsu': w(ks[4], (H, EU)), 'bsu': jnp.zeros((EU,), jnp.float32), 'W1u': w(ks[5], (EU, H, F)), 'b1u': jnp.zeros((EU, F), jnp.float32), 'W2u': w(ks[6], (EU, F, H)), 'b2u': jnp.zeros((EU, H), jnp.float32)}
    _L0_ffn_all = _L0_ffn_setup()
    _L0_ffn_in = {k: v for k, v in _L0_ffn_all.items() if k in ('Wsc', 'bsc', 'W1c', 'b1c', 'W2c', 'b2c', 'Wsu', 'bsu', 'W1u', 'b1u', 'W2u', 'b2u')}
    del _L0_ffn_all
    return {'x': x, 'txt': txt, 'L0_tok_W': _L0_tok_in['W'], 'L0_tok_b': _L0_tok_in['b'], 'L0_tok_cls_token': _L0_tok_in['cls_token'], 'L0_tok_pos_embed': _L0_tok_in['pos_embed'], 'L0_attn_Wq': _L0_attn_in['Wq'], 'L0_attn_bq': _L0_attn_in['bq'], 'L0_attn_Wk': _L0_attn_in['Wk'], 'L0_attn_bk': _L0_attn_in['bk'], 'L0_attn_Wv': _L0_attn_in['Wv'], 'L0_attn_bv': _L0_attn_in['bv'], 'L0_attn_Wo': _L0_attn_in['Wo'], 'L0_attn_bo': _L0_attn_in['bo'], 'L0_ffn_Wsc': _L0_ffn_in['Wsc'], 'L0_ffn_bsc': _L0_ffn_in['bsc'], 'L0_ffn_W1c': _L0_ffn_in['W1c'], 'L0_ffn_b1c': _L0_ffn_in['b1c'], 'L0_ffn_W2c': _L0_ffn_in['W2c'], 'L0_ffn_b2c': _L0_ffn_in['b2c'], 'L0_ffn_Wsu': _L0_ffn_in['Wsu'], 'L0_ffn_bsu': _L0_ffn_in['bsu'], 'L0_ffn_W1u': _L0_ffn_in['W1u'], 'L0_ffn_b1u': _L0_ffn_in['b1u'], 'L0_ffn_W2u': _L0_ffn_in['W2u'], 'L0_ffn_b2u': _L0_ffn_in['b2u']}

def reference(x, txt, L0_tok_W, L0_tok_b, L0_tok_cls_token, L0_tok_pos_embed, L0_attn_Wq, L0_attn_bq, L0_attn_Wk, L0_attn_bk, L0_attn_Wv, L0_attn_bv, L0_attn_Wo, L0_attn_bo, L0_ffn_Wsc, L0_ffn_bsc, L0_ffn_W1c, L0_ffn_b1c, L0_ffn_W2c, L0_ffn_b2c, L0_ffn_Wsu, L0_ffn_bsu, L0_ffn_W1u, L0_ffn_b1u, L0_ffn_W2u, L0_ffn_b2u):
    import jax
    import jax.numpy as jnp

    def _L0_tok_ref(batch_image, W, b, cls_token, pos_embed):
        import jax, jax.numpy as jnp
        import numpy as np
        PATCH = 16
        IMG = 224
        NP_SIDE = IMG // PATCH
        EMBED = 192

        def _patchify(batch_image):
            B = batch_image.shape[0]
            x = batch_image.reshape(B, NP_SIDE, PATCH, NP_SIDE, PATCH, 3)
            x = x.transpose(0, 1, 3, 5, 2, 4)
            return x.reshape(B, NP_SIDE * NP_SIDE, 3 * PATCH * PATCH)
        B = batch_image.shape[0]
        patches = _patchify(batch_image)
        Zp = jnp.einsum('bpd,ed->bpe', patches, W) + b
        Zcls = jnp.broadcast_to(cls_token, (B, 1, EMBED))
        Zcls_p = jnp.concatenate([Zcls, Zp], axis=1)
        return Zcls_p + pos_embed

    def _L0_attn_ref(X, Wq, bq, Wk, bk, Wv, bv, Wo, bo):
        import jax, jax.numpy as jnp
        import numpy as np
        ROPE_THETA = 10000.0

        def rope(x):
            B, S, D = x.shape
            half = D // 2
            inv_freq = 1.0 / ROPE_THETA ** (jnp.arange(half, dtype=jnp.float32) * 2.0 / D)
            ang = jnp.arange(S, dtype=jnp.float32)[:, None] * inv_freq[None, :]
            cos, sin = (jnp.cos(ang), jnp.sin(ang))
            x1, x2 = (x[..., 0::2], x[..., 1::2])
            r1 = x1 * cos - x2 * sin
            r2 = x1 * sin + x2 * cos
            return jnp.stack([r1, r2], axis=-1).reshape(B, S, D)
        NUM_HEADS = 12
        B, S, D = X.shape
        hd = D // NUM_HEADS
        q = rope(X @ Wq + bq)
        k = rope(X @ Wk + bk)
        v = X @ Wv + bv
        qh = q.reshape(B, S, NUM_HEADS, hd)
        kh = k.reshape(B, S, NUM_HEADS, hd)
        vh = v.reshape(B, S, NUM_HEADS, hd)
        scores = jnp.einsum('bqhd,bkhd->bhqk', qh, kh) / jnp.sqrt(jnp.float32(hd))
        causal = jnp.tril(jnp.ones((S, S), dtype=bool))
        scores = jnp.where(causal[None, None, :, :], scores, -jnp.inf)
        weights = jax.nn.softmax(scores, axis=-1)
        out = jnp.einsum('bhqk,bkhd->bqhd', weights, vh).reshape(B, S, D)
        return out @ Wo + bo

    def _L0_ffn_ref(hidden_states, Wsc, bsc, W1c, b1c, W2c, b2c, Wsu, bsu, W1u, b1u, W2u, b2u):
        import jax, jax.numpy as jnp
        import numpy as np
        B, S, H, F = (4, 256, 192, 768)
        EC, EU = (4, 4)
        CAP_FACTOR = 1.0

        def _ffn(x, W1, b1, W2, b2):
            return jax.nn.gelu(x @ W1 + b1, approximate=False) @ W2 + b2

        def _expert_mix(h, route, W1, b1, W2, b2, n_exp):
            out = jnp.zeros_like(h)
            for e in range(n_exp):
                m = (route == e).astype(h.dtype)[:, None]
                out = out + m * _ffn(h, W1[e], b1[e], W2[e], b2[e])
            return out

        def _drop_mask(route, pmax, capacity):
            N = route.shape[0]
            order = jnp.lexsort((-jax.lax.stop_gradient(pmax), route))
            rs = route[order]
            starts = jnp.searchsorted(rs, rs, side='left')
            rank_sorted = jnp.arange(N) - starts
            rank = jnp.zeros((N,), jnp.int32).at[order].set(rank_sorted.astype(jnp.int32))
            return rank >= capacity
        shp = hidden_states.shape
        h = hidden_states.reshape(-1, shp[-1])
        N = h.shape[0]
        capacity = int(CAP_FACTOR * N / EC)
        pc = jax.nn.softmax(h @ Wsc + bsc, axis=-1)
        pmax_c = jnp.max(pc, axis=-1)
        route_c = jnp.argmax(pc, axis=-1)
        dropped = _drop_mask(route_c, pmax_c, capacity)
        scale_c = (pmax_c / jax.lax.stop_gradient(pmax_c))[:, None]
        common = _expert_mix(h, route_c, W1c, b1c, W2c, b2c, EC) * scale_c
        pu = jax.nn.softmax(h @ Wsu + bsu, axis=-1)
        pmax_u = jnp.max(pu, axis=-1)
        route_u = jnp.argmax(pu, axis=-1)
        scale_u = (pmax_u / jax.lax.stop_gradient(pmax_u))[:, None]
        unique = _expert_mix(h, route_u, W1u, b1u, W2u, b2u, EU) * scale_u
        out = common + dropped[:, None].astype(h.dtype) * unique
        return out.reshape(shp)
    h = _L0_tok_ref(x, L0_tok_W, L0_tok_b, L0_tok_cls_token, L0_tok_pos_embed)
    h = jnp.concatenate([h, txt], axis=1)
    h = h + _L0_attn_ref(_layernorm(h, axis=-1), L0_attn_Wq, L0_attn_bq, L0_attn_Wk, L0_attn_bk, L0_attn_Wv, L0_attn_bv, L0_attn_Wo, L0_attn_bo)
    h = h + _L0_ffn_ref(_layernorm(h, axis=-1), L0_ffn_Wsc, L0_ffn_bsc, L0_ffn_W1c, L0_ffn_b1c, L0_ffn_W2c, L0_ffn_b2c, L0_ffn_Wsu, L0_ffn_bsu, L0_ffn_W1u, L0_ffn_b1u, L0_ffn_W2u, L0_ffn_b2u)
    return h

_drawn_inputs = setup_inputs


def setup_inputs(seed=0):
    import zlib

    import numpy as np

    out = dict(_drawn_inputs(seed))
    spreads = {'L0_attn_bq': (0.0, 0.8),
     'L0_attn_bk': (0.0, 0.8),
     'L0_attn_bv': (0.0, 0.1),
     'L0_attn_bo': (0.0, 0.1),
     'L0_ffn_bsc': (0.0, 0.1),
     'L0_ffn_b1c': (0.0, 0.319),
     'L0_ffn_b2c': (0.0, 0.1),
     'L0_ffn_bsu': (0.0, 0.466),
     'L0_ffn_b1u': (0.0, 0.799),
     'L0_ffn_b2u': (0.0, 0.1)}
    factors = {'L0_tok_b': 3.266, 'L0_attn_Wq': 8.0, 'L0_attn_Wk': 8.0, 'L0_attn_Wv': 3.318}
    for name, (base, spread) in spreads.items():
        noise = np.random.default_rng([zlib.crc32(name.encode()), seed]).standard_normal(out[name].shape)
        drawn = base * np.exp(spread * noise) if base else spread * noise
        out[name] = jnp.asarray(drawn.astype(out[name].dtype))
    for name, factor in factors.items():
        out[name] = (out[name] * factor).astype(out[name].dtype)
    return out
```

```python
from contextlib import ExitStack

import numpy as np
import concourse.bass as bass
from concourse import mybir

F32 = mybir.dt.float32
BF16 = mybir.dt.bfloat16
U32 = mybir.dt.uint32
ALU = mybir.AluOpType
ACT = mybir.ActivationFunctionType
AX = mybir.AxisListType

P = 128
B = 32
D = 192
NPATCH, NTXT = 196, 77
S = 1 + NPATCH + NTXT
HEADS, HD = 12, 16
GROUPS, GH = 3, 4
TT = 3
TOFF = [0, 128, 256]
TLEN = [128, 128, S - 256]
IMG1 = 1 + NPATCH - 128
KC = 96
EC = 6
EPS = 1e-5
BIG = -1e30
PARTS = 6
KS_ROWS = PARTS * HD
KROWS = KS_ROWS + 3
SCALE = 0.25
Q2 = S - 32
NE = 8

FREE = 1

PREP_EMB = ["emb0", "emb1"]
MAXS = ["mq0", "mq1", "mq2"]
XNT = ["xnT0", "xnT1"]
QKV = ["qk0", "v0", "qk1", "v1", "qk2", "v2"]
STEADY = (PREP_EMB + MAXS + XNT + ["mT"] + QKV + ["t0", "t1", "t2", "t3", "t4", "t5", "t6"]
          + ["ut0", "ut1", "ut2", "at0", "at1", "t7", "o0", "o1", "x20", "x21", "r"])
FIRST = PREP_EMB + XNT + QKV + [f"t{u}" for u in range(8)]
LAST = MAXS + ["mT"] + ["ut0", "ut1", "ut2", "at0", "at1", "o0", "o1", "x20", "x21", "r"]
assert len(STEADY) % 2 == 0 and len(FIRST) % 2 == 0 and len(LAST) % 2 == 0


class Batch:

    def __init__(self, half, par):
        self.half, self.par, self.n = half, par, half * 2 + par

    def next(self):
        return Batch(self.half + self.par, 1 - self.par)


class Turn:

    def __init__(self, at, pre):
        self.at, self.pre = at, pre
        self.uses = STEADY if at and pre else FIRST if pre else LAST

    def bank(self, use):
        return self.uses.index(use) % 2

    def before(self, use=None):
        k = self.uses.index(use) // 2 if use else 0
        return k if self.at is None else self.at.n * (len(STEADY) // 2) + (len(FIRST) // 2 + k)


def rounds(eng, body):
    body(Turn(None, Batch(0, 0)))
    with eng.Fori(0, B // 2 - 1) as half:
        for par in range(2):
            b = Batch(half, par)
            body(Turn(b, b.next()))
    b = Batch(B // 2 - 1, 0)
    body(Turn(b, b.next()))
    body(Turn(b.next(), None))


class Steps:

    def __init__(self, eng, sem, first, steady):
        self.eng, self.sem, self.first, self.steady = eng, sem, first, steady

    def begin(self, turn):
        self.k, self.turn = 0, turn
        self.base = 0 if turn.at is None else turn.at.n * self.steady + self.first

    def done(self, ins):
        ins.then_inc(self.sem, 1)
        self.k += 1
        return self.k

    def need(self, k):
        self.eng.wait_ge(self.sem, self.base + k)

    def end(self):
        want = self.first if self.turn.at is None else self.steady
        assert self.turn.pre is None or self.k == want, (self.k, want)


def attention(nc, A, logits, h2_d, xn2_d):
    ctx = ExitStack()
    with ctx:
        def sb(name, shape, dt=F32):
            return ctx.enter_context(nc.sbuf_tensor(name, shape, dt))

        def ps(name, shape, dt=F32):
            return ctx.enter_context(nc.psum_tensor(name, shape, dt))

        def sem(name):
            return ctx.enter_context(nc.semaphore(name))

        ident = sb("ident", [P, P])
        identb = sb("identb", [P, P], BF16)
        masks = sb("masks_f", [P, 2, P])
        mask_qk = sb("mask_qk", [P, P], BF16)
        mask_kq = sb("mask_kq", [P, P], BF16)
        cosw = sb("cosw", [P, TT, 2 * D])
        sinw = sb("sinw", [P, TT, 2 * D])
        base = sb("base", [P, 2, D])
        biasb = sb("biasb", [P, 2, D])
        w_emb = sb("w_emb", [P, EC, D])
        w_qkv = sb("w_qkv", [KC + 1, 2, 3 * D])
        w_o = sb("w_o", [KC + 1, 2, D])
        w_r = sb("w_r", [KC + 1, 2, NE])
        xT = [sb(f"xT{i}", [P, EC, NPATCH + 1]) for i in range(2)]
        h = [sb(f"h{i}", [P, TT, D]) for i in range(2)]
        stat = sb("stat", [P, 2, TT, 6])
        mv = sb("mv", [P, 2, TT, 2])
        veps = sb("veps", [P, 2, TT])
        rstd = sb("rstd", [P, 2, TT])
        minus_half = sb("minus_half", [P, TT])
        xn = sb("xn", [P, TT, D])
        xnT = sb("xnT", [KC + 1, 2, S])
        ropeA = sb("ropeA", [P, TT, 2 * D])
        ropeB = sb("ropeB", [P, TT, 2 * D])
        rr = sb("rr", [P, TT, 2 * D])
        d1 = sb("d1", [P, TT, 2 * D])
        stk = sb("stk", [P, TT, 2 * HEADS, PARTS, HD], BF16)
        QS = [sb(f"QS{i}", [P, HEADS, S], BF16) for i in range(2)]
        KS = [sb(f"KS{i}", [P, HEADS, S], BF16) for i in range(2)]
        V = [sb(f"V{i}", [P, TT, HEADS, 32]) for i in range(2)]
        NM = 2 * HEADS + GROUPS
        nm = sb("nm", [P, NM])
        nmd = sb("nmd", [P, NM])
        nmp = sb("nmp", [P, NM, 3], BF16)
        mT = sb("mT", [3 * NM, P], BF16)
        PT = [sb(f"PT{i}", [P, GH, 438]) for i in range(2)]
        Usb = sb("Usb", [P, GROUPS, S])
        rec = sb("rec", [P, TT, HEADS])
        att = sb("att", [P, TT, D])
        attT = sb("attT", [KC + 1, 2, S])
        h2 = [sb(f"hh{i}", [P, TT, D]) for i in range(2)]
        xn2 = [sb(f"xn2{i}", [P, TT, D]) for i in range(2)]
        xn2T = sb("xn2T", [KC + 1, 2, S])
        SP_ = [ps(f"scores{i}", [P, 512]) for i in range(3)]
        MP = [ps(f"maxs{i}", [P, 512]) for i in range(2)]
        UP = ps("attn", [P, 512])
        G = [ps(f"gen{i}", [P, 512]) for i in range(2)]
        Gb = [g[:, :].bitcast(BF16) for g in G]

        consts_in = sem("consts_in")
        consts_set = sem("consts_set")
        x_in = [sem(f"x_in{i}") for i in range(2)]
        txt_in = [sem(f"txt_in{i}") for i in range(2)]
        g_filled = [sem(f"g_filled{i}") for i in range(2)]
        g_emptied = [sem(f"g_emptied{i}") for i in range(2)]
        steps = sem("steps")
        xn_ready = sem("xn_ready")
        var_ready = [sem(f"var_ready{i}") for i in range(2)]
        veps_ready = [sem(f"veps_ready{i}") for i in range(2)]
        rstd_ready = [sem(f"rstd_ready{i}") for i in range(2)]
        rope_r = sem("rope_r")
        part0 = sem("part0")
        diff1 = sem("diff1")
        part1 = sem("part1")
        parts_ready = sem("parts_ready")
        m_filled = [sem(f"m_filled{i}") for i in range(2)]
        m_read = [sem(f"m_read{i}") for i in range(2)]
        nmax_ready = sem("nmax_ready")
        mrow_in = [sem(f"mrow_in{i}") for i in range(2)]
        s_filled = [sem(f"s_filled{i}") for i in range(3)]
        p_ready = sem("p_ready")
        u_filled = sem("u_filled")
        u_read = sem("u_read")
        xn2_ready = sem("xn2_ready")
        rows_out = [sem(f"rows_out{i}") for i in range(2)]
        apart = {e: sem(f"apart_{i}") for i, e in enumerate((nc.sync.engine, nc.gpsimd.engine, nc.vector.engine))}

        loads = ((ident, "ident"), (masks, "masks"),
                 (cosw, "cosw"), (sinw, "sinw"), (base, "base"), (biasb, "biasb"), (w_emb, "w_emb"),
                 (w_qkv, "w_qkv"), (w_o, "w_o"), (w_r, "w_r"))
        n_set = 14
        block = ctx.enter_context(nc.Block())

        def wait_apart(eng, semaphore, value):
            eng.wait_ge(semaphore, value)
            eng.sem_inc(apart[eng.engine], 1)

        @block.sync
        def _(sp):
            for e in rows_out:
                sp.sem_inc(e, FREE)
            for dst, src in loads:
                sp.dma_start(dst[:], A[src]).then_inc(consts_in, 16)

            def load_x(b):
                sp.dma_start(xT[b.par][:], A["xT"][b.n]).then_inc(x_in[b.par], 16)

            def load_txt(b):
                sp.dma_start(h[b.par][IMG1:P, 1, :], A["txt"][b.n, 0:P - IMG1, :]).then_inc(txt_in[b.par], 16)
                sp.dma_start(h[b.par][0:TLEN[2], 2, :], A["txt"][b.n, P - IMG1:NTXT, :]).then_inc(txt_in[b.par], 16)

            def body(t, more=True):
                if t.at is None:
                    for b in (t.pre, t.pre.next()):
                        load_x(b)
                        load_txt(b)
                    return
                b = t.at
                if more:
                    for e in g_emptied:
                        wait_apart(sp, e, t.before())
                    load_x(b.next().next())
                wait_apart(sp, g_emptied[t.bank("mT")], t.before("mT") + 1)
                for r in range(3):
                    row = QS[b.par][KS_ROWS + r:KS_ROWS + r + 1, :, :]
                    for k in range(2):
                        sp.dma_start(row[:, :, k * P:(k + 1) * P],
                                     mT[k * 3 * HEADS + r:(k + 1) * 3 * HEADS:3, :]).then_inc(mrow_in[b.par], 16)
                    for j in range(GROUPS):
                        m = 3 * (2 * HEADS + j) + r
                        sp.dma_start(row[:, GH * j:GH * j + GH, 2 * P:S],
                                     mT[m:m + 1, :].rearrange("a (g q) -> a g q", g=GH)[:, :, 32 - TLEN[2]:32]
                                     ).then_inc(mrow_in[b.par], 16)
                for use in ("o0", "o1"):
                    wait_apart(sp, g_emptied[t.bank(use)], t.before(use) + 1)
                if more:
                    load_txt(b.next().next())
                out_ = rows_out[b.par]
                sp.dma_start(h2_d[b.n, 0:2 * P, :].rearrange("(t p) d -> p t d", p=P), h2[b.par][:, 0:2, :]).then_inc(out_, 16)
                sp.dma_start(h2_d[b.n, 2 * P:S, :], h2[b.par][0:TLEN[2], 2, :]).then_inc(out_, 16)
                wait_apart(sp, xn2_ready, b.n + 1)
                sp.dma_start(xn2_d[b.n, 0:2 * P, :].rearrange("(t p) d -> p t d", p=P), xn2[b.par][:, 0:2, :]).then_inc(out_, 16)
                sp.dma_start(xn2_d[b.n, 2 * P:S, :], xn2[b.par][0:TLEN[2], 2, :]).then_inc(out_, 16)

            def plain(t):
                body(t, more=not (t.at is not None and isinstance(t.at.n, int)))

            rounds(sp, plain)
            sp.wait_ge(g_emptied[0], len(FIRST) // 2 + (B - 1) * len(STEADY) // 2 + len(LAST) // 2)
            sp.wait_ge(g_emptied[1], len(FIRST) // 2 + (B - 1) * len(STEADY) // 2 + len(LAST) // 2)
            for p in range(2):
                sp.wait_ge(rows_out[p], 64 * (B // 2) + FREE)

        @block.tensor
        def _(pe):
            pe.wait_ge(consts_in, 16 * len(loads))
            pe.wait_ge(consts_set, n_set)

            def fill(t, use):
                pe.wait_ge(g_emptied[t.bank(use)], t.before(use))
                return t.bank(use)

            def have(t, use):
                pe.wait_ge(g_emptied[t.bank(use)], t.before(use) + 1)

            def embed(t, k):
                b = t.pre
                if k == 0:
                    pe.wait_ge(x_in[b.par], b.half * 16 + 16)
                g = fill(t, f"emb{k}")
                cols, m = (slice(0, P), P) if k == 0 else (slice(P, NPATCH + 1), IMG1)
                for c in range(EC):
                    mm = pe.matmul(G[g][0:m, 0:D], xT[b.par][:, c, cols], w_emb[:, c, :], start=(c == 0), stop=(c == EC - 1))
                mm.then_inc(g_filled[g], 1)

            def maxs(t, head):
                b, i = t.at, head % 2
                if head == 0:
                    for e in g_emptied:
                        pe.wait_ge(e, t.before())
                pe.wait_ge(m_read[i], b.n * (HEADS // 2) + head // 2 + FREE)
                q, k, r = QS[b.par], KS[b.par], slice(0, KS_ROWS)
                pe.matmul(MP[i][:, 0:P], q[r, head, 0:P], k[r, head, 0:P], start=True, stop=False, skip_group_check=True)
                pe.matmul(MP[i][:, 0:P], identb[:], mask_qk[:], start=False, stop=True, skip_group_check=True)
                pe.matmul(MP[i][:, P:3 * P], q[r, head, P:2 * P], k[r, head, 0:2 * P], start=True, stop=False, skip_group_check=True)
                pe.matmul(MP[i][:, 2 * P:3 * P], identb[:], mask_qk[:], start=False, stop=True, skip_group_check=True).then_inc(m_filled[i], 1)

            def maxs2(t, j):
                b = t.at
                g = fill(t, f"mq{j}")
                q, k, r = QS[b.par], KS[b.par], slice(0, KS_ROWS)
                for i in range(GH):
                    head, rows = GH * j + i, slice(32 * i, 32 * i + 32)
                    pe.matmul(G[g][rows, 0:S], q[r, head, Q2:S], k[r, head, :], start=True, stop=False, skip_group_check=True)
                    mm = pe.matmul(G[g][rows, Q2:S], identb[0:32, 0:32], mask_qk[0:32, 0:32], start=False, stop=True,
                                   tile_position=(0, 32 * i), skip_group_check=True)
                mm.then_inc(g_filled[g], 1)

            def turn_tokens(t, src, use):
                c = int(use[-1])
                g = fill(t, use)
                for k in range(TT):
                    mm = pe.transpose(G[g][0:KC, TOFF[k]:TOFF[k] + TLEN[k]], src[0:TLEN[k], k, c * KC:(c + 1) * KC],
                                      ident[0:TLEN[k], 0:TLEN[k]])
                mm.then_inc(g_filled[g], 1)

            def turn_max(t):
                pe.wait_ge(nmax_ready, t.at.n + 1)
                g = fill(t, "mT")
                pe.transpose(Gb[g][0:3 * NM, 0:P], nmp[:, :, :].rearrange("p h r -> p (h r)"), identb[:]).then_inc(g_filled[g], 1)

            def qkv(t):
                have(t, "xnT0")
                have(t, "xnT1")
                for k in range(TT):
                    tok = slice(TOFF[k], TOFF[k] + TLEN[k])
                    for use, cols in ((f"qk{k}", slice(0, 2 * D)), (f"v{k}", slice(2 * D, 3 * D))):
                        g = fill(t, use)
                        o = G[g][0:TLEN[k], 0:cols.stop - cols.start]
                        pe.matmul(o, xnT[:, 0, tok], w_qkv[:, 0, cols], start=True, stop=False)
                        pe.matmul(o, xnT[0:KC, 1, tok], w_qkv[0:KC, 1, cols], start=False, stop=True).then_inc(g_filled[g], 1)

            def turn_parts(t, u):
                if u == 0:
                    pe.wait_ge(parts_ready, t.pre.n * TT + TT)
                g = fill(t, f"t{u}")
                for i in range(3):
                    for k in range(TT):
                        mm = pe.transpose(Gb[g][0:KS_ROWS, i * S + TOFF[k]:i * S + TOFF[k] + TLEN[k]],
                                          stk[0:TLEN[k], k, 3 * u + i, :, :].rearrange("p a d -> p (a d)"),
                                          identb[0:TLEN[k], 0:TLEN[k]])
                mm.then_inc(g_filled[g], 1)

            def scores(t, head):
                b, i = t.at, head % 3
                if head == 0:
                    pe.wait_ge(mrow_in[b.par], b.half * 240 + 240)
                if head < 3:
                    pe.wait_ge(p_ready, b.n * HEADS + FREE)
                else:
                    pe.wait_ge(p_ready, b.n * HEADS + head - 2 + FREE)
                q, k, s, n = QS[b.par], KS[b.par], SP_[i], TLEN[2]
                r = slice(0, KROWS)
                pe.matmul(s[:, 0:S], k[r, head, 0:P], q[r, head, :], start=True, stop=False, skip_group_check=True)
                pe.matmul(s[:, 0:P], identb[:], mask_kq[:], start=False, stop=True, skip_group_check=True)
                pe.matmul(s[:, S:S + 146], k[r, head, P:2 * P], q[r, head, P:S], start=True, stop=False, skip_group_check=True)
                pe.matmul(s[:, S:S + P], identb[:], mask_kq[:], start=False, stop=True, skip_group_check=True)
                pe.matmul(s[0:n, 420:438], k[r, head, 2 * P:S], q[r, head, 2 * P:S], start=True, stop=False, skip_group_check=True)
                pe.matmul(s[0:n, 420:438], identb[0:n, 0:n], mask_kq[0:n, 0:n], start=False, stop=True,
                          skip_group_check=True).then_inc(s_filled[i], 1)

            def values(t, j):
                b = t.at
                pt = PT[(3 * b.par + j) % 2]
                pe.wait_ge(p_ready, b.n * HEADS + GH * (j + 1) + FREE)
                pe.wait_ge(u_read, b.n * GROUPS + j + FREE)
                for k, (lo, n, at) in enumerate(((0, S, 0), (P, 146, S), (2 * P, TLEN[2], 420))):
                    for i in range(GH):
                        rows = TLEN[k]
                        mm = pe.matmul(UP[32 * i:32 * i + 32, lo:S], V[b.par][0:rows, k, GH * j + i, :],
                                       pt[0:rows, i, at:at + n], start=(k == 0), stop=(k == 2),
                                       tile_position=(0, 32 * i), skip_group_check=True)
                mm.then_inc(u_filled, 1)

            def turn_values(t, k):
                if k == 0:
                    pe.wait_ge(u_read, t.at.n * GROUPS + GROUPS + FREE)
                g = fill(t, f"ut{k}")
                for j in range(GROUPS):
                    mm = pe.transpose(G[g][0:TLEN[k], j * P:(j + 1) * P], Usb[:, j, TOFF[k]:TOFF[k] + TLEN[k]], ident[:])
                mm.then_inc(g_filled[g], 1)

            def project(t):
                have(t, "at0")
                have(t, "at1")
                for use, tiles in (("o0", (0, 1)), ("o1", (2,))):
                    g = fill(t, use)
                    for k in tiles:
                        tok = slice(TOFF[k], TOFF[k] + TLEN[k])
                        o = G[g][0:TLEN[k], (k % 2) * D:(k % 2) * D + D]
                        pe.matmul(o, attT[:, 0, tok], w_o[:, 0, :], start=True, stop=False)
                        mm = pe.matmul(o, attT[0:KC, 1, tok], w_o[0:KC, 1, :], start=False, stop=True)
                    mm.then_inc(g_filled[g], 1)

            def route(t):
                have(t, "x20")
                have(t, "x21")
                g = fill(t, "r")
                for k in range(TT):
                    tok = slice(TOFF[k], TOFF[k] + TLEN[k])
                    o = G[g][0:TLEN[k], k * NE:(k + 1) * NE]
                    pe.matmul(o, xn2T[:, 0, tok], w_r[:, 0, :], start=True, stop=False)
                    mm = pe.matmul(o, xn2T[0:KC, 1, tok], w_r[0:KC, 1, :], start=False, stop=True)
                mm.then_inc(g_filled[g], 1)

            def body(t):
                if t.pre:
                    embed(t, 0)
                    embed(t, 1)
                if t.at:
                    for j in range(GROUPS):
                        for head in range(GH * j, GH * j + GH):
                            maxs(t, head)
                        maxs2(t, j)
                if t.pre:
                    pe.wait_ge(xn_ready, t.pre.n + 1)
                    turn_tokens(t, xn, "xnT0")
                    turn_tokens(t, xn, "xnT1")
                if t.at:
                    turn_max(t)
                if t.pre:
                    qkv(t)
                after = {0: (0, 1, 2), 1: (3, 4, 5), 2: (6,)}
                for j in range(GROUPS):
                    if t.at:
                        for head in range(GH * j, GH * j + GH):
                            scores(t, head)
                    if t.pre:
                        for u in after[j]:
                            turn_parts(t, u)
                    if t.at:
                        values(t, j)
                if t.at:
                    for k in range(TT):
                        turn_values(t, k)
                    for k in range(TT):
                        have(t, f"ut{k}")
                    turn_tokens(t, att, "at0")
                    turn_tokens(t, att, "at1")
                if t.pre:
                    turn_parts(t, 7)
                if t.at:
                    project(t)
                    pe.wait_ge(xn2_ready, t.at.n + 1)
                    turn_tokens(t, xn2[t.at.par], "x20")
                    turn_tokens(t, xn2[t.at.par], "x21")
                    route(t)

            rounds(pe, body)

        def copy_parts(eng, t, u, g):
            dst = (QS if u < 4 else KS)[t.pre.par][0:KS_ROWS, 3 * (u % 4):3 * (u % 4) + 3, :]
            src = Gb[g][0:KS_ROWS, 0:3 * S].rearrange("p (h s) -> p h s", s=S)
            if eng is nc.scalar:
                return eng.activation(dst, src, ACT.Copy)
            return eng.tensor_copy(dst, src)

        @block.scalar
        def _(act):
            act = nc.scalar
            for e in (p_ready, u_read):
                act.sem_inc(e, FREE)

            def take(t, use):
                act.wait_ge(g_filled[t.bank(use)], t.before(use) + 1)
                return t.bank(use)

            def copy_tokens(t, use, dst):
                g, c = take(t, use), int(use[-1])
                act.activation(dst[0:KC, c, :], G[g][0:KC, 0:S], ACT.Copy).then_inc(g_emptied[g], 1)

            def pairs(t, k):
                act.wait_ge(rope_r, t.pre.n * TT + k + 1)
                n = TLEN[k]
                q = rr[0:n, k, 0:D].rearrange("p (h a d) -> p h a d", a=1, d=HD)
                kk = rr[0:n, k, D:2 * D].rearrange("p (h a d) -> p h a d", a=1, d=HD)
                act.activation(stk[0:n, k, 0:HEADS, 0:3, :], q.broadcast_to([n, HEADS, 3, HD]), ACT.Copy)
                act.activation(stk[0:n, k, HEADS:2 * HEADS, 0:4:3, :], kk.broadcast_to([n, HEADS, 2, HD]), ACT.Copy)
                act.activation(stk[0:n, k, HEADS:2 * HEADS, 5:6, :], kk, ACT.Copy).then_inc(part0, 1)

            def weights(t, j):
                b = t.at
                pt = PT[(3 * b.par + j) % 2]
                for i in range(GH):
                    head = GH * j + i
                    s, n = SP_[head % 3], TLEN[2]
                    act.wait_ge(s_filled[head % 3], b.n * (HEADS // 3) + head // 3 + 1)
                    act.activation(pt[0:n, i, 420:438], s[0:n, 420:438], ACT.Exp, scale=SCALE)
                    act.activation(pt[:, i, 0:420], s[:, 0:420], ACT.Exp, scale=SCALE).then_inc(p_ready, 1)

            def body(t):
                if t.pre:
                    copy_tokens(t, "xnT0", xnT)
                    copy_tokens(t, "xnT1", xnT)
                if t.at:
                    g = take(t, "mT")
                    act.activation(mT[:], Gb[g][0:3 * NM, 0:P], ACT.Copy).then_inc(g_emptied[g], 1)
                if t.pre:
                    for k in range(TT):
                        g = take(t, f"v{k}")
                        act.activation(V[t.pre.par][0:TLEN[k], k, :, 0:HD],
                                       G[g][0:TLEN[k], 0:D].rearrange("p (h d) -> p h d", d=HD), ACT.Copy).then_inc(g_emptied[g], 1)
                    for k in range(TT):
                        pairs(t, k)
                after = {0: (0, 2), 1: (4,), 2: (6,)}
                for j in range(GROUPS):
                    if t.at:
                        weights(t, j)
                    if t.pre:
                        for u in after[j]:
                            g = take(t, f"t{u}")
                            copy_parts(act, t, u, g).then_inc(g_emptied[g], 1)
                    if t.at:
                        act.wait_ge(u_filled, t.at.n * GROUPS + j + 1)
                        act.activation(Usb[:, j, :], UP[:, 0:S], ACT.Copy).then_inc(u_read, 1)
                if t.at:
                    copy_tokens(t, "at0", attT)
                    copy_tokens(t, "at1", attT)
                    copy_tokens(t, "x20", xn2T)
                    copy_tokens(t, "x21", xn2T)

            rounds(act, body)

        @block.gpsimd
        def _(pool):
            pool.wait_ge(consts_set, n_set)

            def root(which, b):
                wait_apart(pool, var_ready[which], b.n + 1)
                pool.tensor_scalar(veps[:, which, :], mv[:, which, :, 1], EPS, None, ALU.add).then_inc(veps_ready[which], 1)
                pool.wait_ge(veps_ready[which], b.n + 1)
                pool.tensor_tensor(rstd[:, which, :], veps[:, which, :], minus_half[:], ALU.pow).then_inc(rstd_ready[which], 1)

            def body(t):
                if t.pre:
                    root(0, t.pre)
                    for k in range(TT):
                        r = slice(0, TLEN[k])
                        pool.wait_ge(g_emptied[t.bank(f"qk{k}")], t.before(f"qk{k}") + 1)
                        pool.tensor_tensor(rr[r, k, :], ropeA[r, k, :], ropeB[r, k, :], ALU.add).then_inc(rope_r, 1)
                    for k in range(TT):
                        n = TLEN[k]
                        wait_apart(pool, diff1, t.pre.n * TT + k + 1)
                        q = d1[0:n, k, 0:D].rearrange("p (h a d) -> p h a d", a=1, d=HD)
                        kk = d1[0:n, k, D:2 * D].rearrange("p (h a d) -> p h a d", a=1, d=HD)
                        pool.tensor_copy(stk[0:n, k, 0:HEADS, 3:5, :], q.broadcast_to([n, HEADS, 2, HD]))
                        pool.tensor_copy(stk[0:n, k, HEADS:2 * HEADS, 1:5:3, :], kk.broadcast_to([n, HEADS, 2, HD])).then_inc(part1, 1)
                if t.at:
                    root(1, t.at)

            rounds(pool, body)

        @block.vector
        def _(dve):
            for e in m_read:
                dve.sem_inc(e, FREE)
            for p in range(2):
                dve.memset(KS[p][KS_ROWS:KROWS, :, :], 1.0).then_inc(consts_set, 1)
                dve.memset(V[p][:], 1.0).then_inc(consts_set, 1)
            for x in (xnT, attT, xn2T):
                dve.memset(x[KC:KC + 1, :, :], 1.0).then_inc(consts_set, 1)
            dve.memset(mv[:], 1.0).then_inc(consts_set, 1)
            dve.memset(logits[:, :, 2, :], 0.0).then_inc(consts_set, 1)
            dve.memset(minus_half[:], -0.5).then_inc(consts_set, 1)
            dve.wait_ge(consts_in, 16 * len(loads))
            dve.tensor_tensor(base[:], base[:], biasb[:], ALU.add).then_inc(consts_set, 1)
            dve.tensor_copy(identb[:], ident[:]).then_inc(consts_set, 1)
            dve.tensor_copy(mask_qk[:], masks[:, 0, :]).then_inc(consts_set, 1)
            dve.tensor_copy(mask_kq[:], masks[:, 1, :]).then_inc(consts_set, 1)
            dve.wait_ge(consts_set, n_set)
            st = Steps(dve, steps, 1, 8)

            def take(t, use):
                dve.wait_ge(g_filled[t.bank(use)], t.before(use) + 1)
                return t.bank(use)

            def norm(src, dst, which, ready, b):
                k = {}

                def stats():
                    for i in range(TT):
                        ins = dve.bn_stats(stat[0:TLEN[i], which, i, :], src[0:TLEN[i], i, :])
                    k["stats"] = st.done(ins)

                def aggr():
                    wait_apart(dve, steps, st.base + k["stats"])
                    for i in range(TT):
                        ins = dve.bn_aggr(mv[0:TLEN[i], which, i, :], stat[0:TLEN[i], which, i, :])
                    ins.then_inc(var_ready[which], 1)

                def scale():
                    dve.wait_ge(rstd_ready[which], b.n + 1)
                    for i in range(TT):
                        n = TLEN[i]
                        ins = dve.tensor_scalar(dst[0:n, i, :], src[0:n, i, :], mv[0:n, which, i, 0:1],
                                                rstd[0:n, which, i:i + 1], ALU.subtract, ALU.mult)
                    ins.then_inc(ready, 1)

                return [stats, aggr, scale]

            def body(t):
                st.begin(t)
                b, pre = t.at, t.pre
                todo = []
                if pre:
                    def emb(k):
                        g = take(t, f"emb{k}")
                        n = P if k == 0 else IMG1
                        ins = dve.tensor_tensor(h[pre.par][0:n, k, :], G[g][0:n, 0:D], base[0:n, k, :], ALU.add)
                        ins.then_inc(g_emptied[g], 1)

                    def text():
                        dve.wait_ge(txt_in[pre.par], pre.half * 32 + 32)
                        dve.wait_ge(g_emptied[t.bank("emb0")], t.before("emb0") + 1)
                        dve.wait_ge(g_emptied[t.bank("emb1")], t.before("emb1") + 1)

                    ln = norm(h[pre.par], xn, 0, xn_ready, pre)
                    todo = [lambda: emb(0), lambda: emb(1), lambda: (text(), ln[0]()), ln[1], ln[2]]
                if b:
                    if todo:
                        todo.pop(0)()
                        todo.pop(0)()
                    for j in range(GROUPS):
                        for head in range(GH * j, GH * j + GH):
                            i = head % 2
                            dve.wait_ge(m_filled[i], b.n * (HEADS // 2) + head // 2 + 1)
                            dve.tensor_reduce(nm[:, head:head + 1], MP[i][:, 0:P], AX.X, ALU.max, negate=True)
                            dve.tensor_reduce(nm[:, HEADS + head:HEADS + head + 1], MP[i][:, P:3 * P], AX.X, ALU.max,
                                              negate=True).then_inc(m_read[i], 1)
                            if todo and head % 2:
                                todo.pop(0)()
                        g = take(t, f"mq{j}")
                        dve.tensor_reduce(nm[:, 2 * HEADS + j:2 * HEADS + j + 1], G[g][:, 0:S], AX.X, ALU.max,
                                          negate=True).then_inc(g_emptied[g], 1)
                for f in todo:
                    f()
                if b:
                    dve.wait_ge(g_emptied[t.bank("mq2")], t.before("mq2") + 1)
                    a1 = st.done(dve.tensor_copy(nmp[:, :, 0], nm[:]))
                    st.need(a1)
                    a2 = st.done(dve.tensor_tensor(nmd[:], nm[:], nmp[:, :, 0], ALU.subtract))
                    st.need(a2)
                    a3 = st.done(dve.tensor_copy(nmp[:, :, 1], nmd[:]))
                    st.need(a3)
                    dve.tensor_tensor(nmp[:, :, 2], nmd[:], nmp[:, :, 1], ALU.subtract).then_inc(nmax_ready, 1)
                if pre:
                    def rotate(k):
                        g, n = take(t, f"qk{k}"), TLEN[k]
                        dve.tensor_tensor(ropeA[0:n, k, :], G[g][0:n, 0:2 * D], cosw[0:n, k, :], ALU.mult)
                        pair = lambda x: x.rearrange("p (m two) -> p m two", two=2)
                        dve.tensor_tensor(pair(ropeB[0:n, k, :]), pair(G[g][0:n, 0:2 * D])[:, :, ::-1],
                                          pair(sinw[0:n, k, :]), ALU.mult).then_inc(g_emptied[g], 1)

                    def second(k):
                        n = TLEN[k]
                        dve.wait_ge(part0, pre.n * TT + k + 1)
                        dve.tensor_tensor(d1[0:n, k, :].rearrange("p (h d) -> p h d", d=HD),
                                          rr[0:n, k, :].rearrange("p (h d) -> p h d", d=HD), stk[0:n, k, :, 0, :],
                                          ALU.subtract).then_inc(diff1, 1)

                    def third(k):
                        n = TLEN[k]
                        dve.wait_ge(part1, pre.n * TT + k + 1)
                        dd = d1[0:n, k, :].rearrange("p (h d) -> p h d", d=HD)
                        dve.tensor_tensor(stk[0:n, k, 0:HEADS, 5, :], dd[:, 0:HEADS], stk[0:n, k, 0:HEADS, 3, :], ALU.subtract)
                        dve.tensor_tensor(stk[0:n, k, HEADS:2 * HEADS, 2, :], dd[:, HEADS:2 * HEADS],
                                          stk[0:n, k, HEADS:2 * HEADS, 1, :], ALU.subtract).then_inc(parts_ready, 1)

                    for k in range(TT):
                        rotate(k)
                    for k in range(TT):
                        second(k)
                    for k in range(TT):
                        third(k)
                    for u in (1, 3, 5):
                        g = take(t, f"t{u}")
                        copy_parts(dve, t, u, g).then_inc(g_emptied[g], 1)
                if b:
                    for k in range(TT):
                        g, n = take(t, f"ut{k}"), TLEN[k]
                        heads = G[g][0:n, 0:GROUPS * P].rearrange("p (h c) -> p h c", c=32)
                        r = st.done(dve.reciprocal(rec[0:n, k, :], heads[:, :, HD]))
                        st.need(r)
                        dve.tensor_tensor(att[0:n, k, :].rearrange("p (h d) -> p h d", d=HD), heads[:, :, 0:HD],
                                          rec[0:n, k, :].rearrange("p (h a) -> p h a", a=1).broadcast_to([n, HEADS, HD]),
                                          ALU.mult).then_inc(g_emptied[g], 1)
                if pre:
                    g = take(t, "t7")
                    copy_parts(dve, t, 7, g).then_inc(g_emptied[g], 1)
                if b:
                    dve.wait_ge(rows_out[b.par], b.half * 64 + FREE)
                    g = take(t, "o0")
                    dve.tensor_tensor(h2[b.par][:, 0:2, :].rearrange("p t d -> p (t d)"), G[g][:, 0:2 * D],
                                      h[b.par][:, 0:2, :].rearrange("p t d -> p (t d)"), ALU.add).then_inc(g_emptied[g], 1)
                    g, n = take(t, "o1"), TLEN[2]
                    dve.tensor_tensor(h2[b.par][0:n, 2, :], G[g][0:n, 0:D], h[b.par][0:n, 2, :], ALU.add).then_inc(g_emptied[g], 1)
                    dve.wait_ge(g_emptied[t.bank("o0")], t.before("o0") + 1)
                    dve.wait_ge(g_emptied[t.bank("o1")], t.before("o1") + 1)
                    for f in norm(h2[b.par], xn2[b.par], 1, xn2_ready, b):
                        f()
                    g = take(t, "r")
                    dve.tensor_copy(logits[:, b.n, 0:2, :], G[g][:, 0:2 * NE].rearrange("p (t e) -> p t e", e=NE))
                    dve.tensor_copy(logits[0:n, b.n, 2, :], G[g][0:n, 2 * NE:3 * NE]).then_inc(g_emptied[g], 1)
                st.end()

            rounds(dve, body)


FF = 768
NX = 4
N = B * S
CAP = N // NX
COLS = B * TT
ROWS = 256
CT = (N + NX * (ROWS - 1)) // ROWS
UT = (N - CAP + NX * (ROWS - 1)) // ROWS
DEPTH = 4
TILES = -(-(CT + UT) // DEPTH) * DEPTH
ZROW = TILES * ROWS
FC = FF // P
W1O, W2O, B1O, B2O = 0, 2 * FF, 2 * FF + FC * D, 2 * FF + FC * D + FC
WCOLS = B2O + D
STEPS = 27
KTH = max(CT, UT) + 2
CONSTS = dict(valid=COLS, seg=NX * COLS, rank=NX, kth=KTH, tile=TILES, lane=1, one=NX)
CWIDTH = sum(CONSTS.values())


def route_tokens(nc, A, logits, pos, scale, wrow, xs_d, y_d):
    ctx = ExitStack()
    with ctx:
        def sb(name, shape, dt=F32):
            return ctx.enter_context(nc.sbuf_tensor(name, shape, dt))

        def sem(name):
            return ctx.enter_context(nc.semaphore(name))

        consts = sb("route_consts", [P, CWIDTH])
        C, at = {}, 0
        for name, n in CONSTS.items():
            C[name] = consts[:, at:at + n]
            at += n
        before = sb("before", [P, P])
        ones = sb("ones", [P, P])
        zeros = sb("zeros", [P, 8 * D])
        z = sb("z", [P, COLS, 2, NX])
        ez = sb("ez", [P, COLS, 2, NX])
        mx = sb("mx", [P, COLS, 2])
        total = sb("total", [P, COLS, 2])
        pmax = sb("pmax", [P, COLS, 2])
        OH = sb("OH", [P, 2, NX, COLS])
        key = sb("key", [P, NX, COLS])
        T = sb("T", [P, NX])
        cand = sb("cand", [P, NX])
        step = sb("step", [P, 1])
        gain = sb("gain", [P, NX])
        part = sb("part", [P, NX])
        need = sb("need", [P, NX])
        flag = sb("flag", [P, NX, COLS])
        tie = sb("tie", [P, NX, COLS])
        run_ = sb("run", [P, NX, COLS])
        rk = sb("rk", [P, NX, COLS])
        posf = sb("posf", [P, 2, COLS])
        drop = sb("drop", [P, COLS])
        more = sb("more", [P, NX, KTH])
        nt = sb("nt", [P, NX])
        first = sb("first", [P, NX])
        first_row = sb("first_row", [P, NX])
        tcmp = sb("tcmp", [P, TILES, NX - 1])
        tex = sb("tex", [P, TILES])
        cnt_ps = ctx.enter_context(nc.psum_tensor("cnt_ps", [P, 512], F32))
        in_col = ctx.enter_context(nc.psum_tensor("in_col", [P, 512], F32))
        of_col = ctx.enter_context(nc.psum_tensor("of_col", [P, 512], F32))

        r_in = sem("r_in")
        zero_set = sem("zero_set")
        zeroed = sem("zeroed")
        z_ready, e_ready = sem("z_ready"), sem("e_ready")
        v = sem("v_steps")
        part_ready, counted = sem("part_ready"), sem("counted")
        ranks_in, ranks_out = sem("ranks_in"), sem("ranks_out")
        block = ctx.enter_context(nc.Block())

        @block.sync
        def _(sp):
            sp.dma_start(consts[:], A["rconsts"]).then_inc(r_in, 16)
            sp.dma_start(before[:], A["before"]).then_inc(r_in, 16)
            sp.wait_ge(zero_set, 1)
            n = ZROW // P // 8
            assert n * P * 8 == ZROW
            for i in range(n):
                sp.dma_start(xs_d[i * P * 8:(i + 1) * P * 8, :].rearrange("(p t) d -> p (t d)", p=P), zeros[:]).then_inc(zeroed, 16)
            sp.dma_start(y_d[ZROW:ZROW + 1, :], zeros[0:1, 0:D]).then_inc(zeroed, 16)
            sp.wait_ge(zeroed, 16 * n + 16)

        @block.gpsimd
        def _(pool):
            pool.memset(zeros[:], 0.0).then_inc(zero_set, 1)

        @block.scalar
        def _(act):
            nc.scalar.wait_ge(z_ready, 1)
            nc.scalar.activation(ez[:], z[:], ACT.Exp).then_inc(e_ready, 1)

        @block.tensor
        def _(pe):
            pe.wait_ge(r_in, 32)

            def ranks(k, src):
                pe.wait_ge(ranks_in, k + 1)
                f = src.rearrange("p e c -> p (e c)")
                pe.matmul(in_col[:, 0:NX * COLS], before[:], f, start=True, stop=True)
                pe.matmul(of_col[:, 0:NX * COLS], ones[:], f, start=True, stop=True).then_inc(ranks_out, 1)

            def count(n):
                pe.wait_ge(part_ready, n + 1)
                pe.matmul(cnt_ps[:, 0:NX], ones[:], part[:], start=True, stop=True).then_inc(counted, 1)

            ranks(0, OH[:, 0])
            with pe.Fori(0, STEPS) as i:
                count(i)
            count(STEPS)
            ranks(1, tie)
            ranks(2, OH[:, 1])

        @block.vector
        def _(dve):
            made = 0

            def done(ins):
                nonlocal made
                made += 1
                ins.then_inc(v, 1)
                dve.wait_ge(v, made)

            bc = lambda x, shape: x.broadcast_to(shape)
            by_e = lambda x: bc(x.rearrange("p (e a) -> p e a", a=1), [P, NX, COLS])
            by_c = lambda x: bc(x.rearrange("p (a c) -> p a c", a=1), [P, NX, COLS])
            last = lambda x: bc(x.rearrange("p c (s a) -> p c s a", a=1), [P, COLS, 2, NX])
            order = bc(C["rank"].rearrange("p (a b e) -> p a b e", a=1, b=1), [P, COLS, 2, NX])
            over_e = lambda x: x.rearrange("p e c -> p c e")

            done(dve.memset(ones[:], 1.0))
            done(dve.memset(T[:], 0.0))
            done(dve.memset(step[:], 1.0))
            dve.wait_ge(r_in, 32)
            lg = logits[:].rearrange("p b t (s e) -> p (b t) s e", s=2)
            done(dve.tensor_reduce(mx[:], lg, AX.X, ALU.max))
            dve.tensor_tensor(z[:], lg, last(mx), ALU.subtract).then_inc(z_ready, 1)
            dve.wait_ge(e_ready, 1)
            done(dve.tensor_reduce(total[:], ez[:], AX.X, ALU.add))
            done(dve.reciprocal(mx[:], total[:]))
            done(dve.tensor_tensor(ez[:], ez[:], last(mx), ALU.mult))
            done(dve.tensor_reduce(pmax[:], ez[:], AX.X, ALU.max))
            done(dve.tensor_tensor(z[:], ez[:], last(pmax), ALU.is_equal))
            done(dve.tensor_tensor(z[:], z[:], order, ALU.mult))
            done(dve.tensor_reduce(total[:], z[:], AX.X, ALU.max))
            done(dve.tensor_tensor(OH[:].rearrange("p s e c -> p c s e"), last(total), order, ALU.is_equal))
            for s in range(2):
                done(dve.tensor_tensor(OH[:, s], OH[:, s], by_c(C["valid"]), ALU.mult))

            def column_ranks(k):
                dve.wait_ge(ranks_out, k + 1)
                flat = lambda x: x.rearrange("p e c -> p (e c)")
                n = NX * COLS
                done(dve.tensor_tensor_scan(flat(run_[:]), C["seg"], of_col[:, 0:n], 0.0, ALU.mult, ALU.add))
                done(dve.tensor_tensor(flat(rk[:]), flat(run_[:]), of_col[:, 0:n], ALU.subtract))
                done(dve.tensor_tensor(flat(rk[:]), flat(rk[:]), in_col[:, 0:n], ALU.add))

            def place(kind, tile0, last_tile):
                cnt = run_[:, :, COLS - 1]
                done(dve.tensor_tensor(more[:], bc(cnt.rearrange("p (e a) -> p e a", a=1), [P, NX, KTH]),
                                       bc(C["kth"].rearrange("p (a k) -> p a k", a=1), [P, NX, KTH]), ALU.is_gt))
                done(dve.tensor_reduce(nt[:], more[:], AX.X, ALU.add))
                done(dve.tensor_tensor_scan(first[:], C["one"], nt[:], float(tile0), ALU.mult, ALU.add))
                done(dve.tensor_tensor(first[:], first[:], nt[:], ALU.subtract))
                done(dve.tensor_scalar(first_row[:], first[:], float(ROWS), None, ALU.mult))
                done(dve.tensor_tensor(rk[:], rk[:], by_e(first_row[:]), ALU.add))
                done(dve.tensor_tensor(rk[:], rk[:], OH[:, kind], ALU.mult))
                done(dve.tensor_reduce(posf[:, kind, :], over_e(rk[:]), AX.X, ALU.add))
                n = last_tile - tile0
                tile = C["tile"][:, tile0:last_tile].rearrange("p (t a) -> p t a", a=1)
                done(dve.tensor_tensor(tcmp[:, 0:n, :], bc(tile, [P, n, NX - 1]),
                                       bc(first[:, 1:NX].rearrange("p (a e) -> p a e", a=1), [P, n, NX - 1]), ALU.is_ge))
                done(dve.tensor_reduce(tex[:, tile0:last_tile], tcmp[:, 0:n, :], AX.X, ALU.add))
                done(dve.tensor_scalar(tex[:, tile0:last_tile], tex[:, tile0:last_tile], float(NX * kind), float(P), ALU.add, ALU.mult))
                done(dve.tensor_scalar(wrow[:, tile0:last_tile], tex[:, tile0:last_tile], C["lane"], None, ALU.add))

            done(dve.tensor_tensor(key[:], OH[:, 0], by_c(pmax[:, :, 0]), ALU.mult))
            dve.sem_inc(ranks_in, 1)
            column_ranks(0)
            place(0, 0, CT)
            done(dve.tensor_copy(pos[:, :, 0], posf[:, 0, :]))

            with dve.Fori(0, STEPS) as i:
                own = made + 5 * i
                dve.tensor_scalar(cand[:], T[:], step[:, 0:1], None, ALU.add).then_inc(v, 1)
                dve.wait_ge(v, own + 1)
                dve.tensor_tensor(flag[:], key[:], by_e(cand[:]), ALU.is_ge).then_inc(v, 1)
                dve.wait_ge(v, own + 2)
                dve.tensor_reduce(part[:], flag[:], AX.X, ALU.add).then_inc(part_ready, 1)
                dve.wait_ge(counted, i + 1)
                dve.tensor_scalar(gain[:], cnt_ps[:, 0:NX], float(CAP), step[:, 0:1], ALU.is_ge, ALU.mult).then_inc(v, 1)
                dve.wait_ge(v, own + 3)
                dve.tensor_scalar(step[:], step[:], 0.5, None, ALU.mult).then_inc(v, 1)
                dve.tensor_tensor(T[:], T[:], gain[:], ALU.add).then_inc(v, 1)
                dve.wait_ge(v, own + 5)
            made += 5 * STEPS

            done(dve.tensor_tensor(flag[:], key[:], by_e(T[:]), ALU.is_gt))
            dve.tensor_reduce(part[:], flag[:], AX.X, ALU.add).then_inc(part_ready, 1)
            done(dve.tensor_tensor(tie[:], key[:], by_e(T[:]), ALU.is_equal))
            done(dve.tensor_tensor(tie[:], tie[:], OH[:, 0], ALU.mult))
            dve.sem_inc(ranks_in, 1)
            dve.wait_ge(counted, STEPS + 1)
            done(dve.tensor_scalar(need[:], cnt_ps[:, 0:NX], -1.0, float(CAP), ALU.mult, ALU.add))
            column_ranks(1)
            done(dve.tensor_tensor(rk[:], rk[:], by_e(need[:]), ALU.is_ge))
            done(dve.tensor_tensor(rk[:], rk[:], tie[:], ALU.mult))
            done(dve.tensor_tensor(flag[:], key[:], by_e(T[:]), ALU.is_lt))
            done(dve.tensor_tensor(flag[:], flag[:], OH[:, 0], ALU.mult))
            done(dve.tensor_tensor(flag[:], flag[:], rk[:], ALU.add))
            done(dve.tensor_reduce(drop[:], over_e(flag[:]), AX.X, ALU.add))

            done(dve.tensor_tensor(OH[:, 1], OH[:, 1], by_c(drop[:]), ALU.mult))
            dve.sem_inc(ranks_in, 1)
            done(dve.reciprocal(mx[:], pmax[:]))
            done(dve.tensor_tensor(scale[:], pmax[:], mx[:], ALU.mult))
            done(dve.tensor_tensor(scale[:, :, 1], scale[:, :, 1], drop[:], ALU.mult))
            column_ranks(2)
            place(1, CT, TILES)
            done(dve.tensor_scalar(drop[:], drop[:], -float(ZROW), float(ZROW), ALU.mult, ALU.add))
            done(dve.tensor_tensor(pos[:, :, 1], posf[:, 1, :], drop[:], ALU.add))


def run_experts(nc, A, pos, scale, wrow, h2_d, xn2_d, xs_d, y_d, out):
    ctx = ExitStack()
    with ctx:
        def sb(name, shape, dt=F32):
            return ctx.enter_context(nc.sbuf_tensor(name, shape, dt))

        def ps(name):
            return ctx.enter_context(nc.psum_tensor(name, [P, 512], F32))

        def sem(name):
            return ctx.enter_context(nc.semaphore(name))

        def sems(name, n=DEPTH):
            return [sem(f"{name}{i}") for i in range(n)]

        eye = sb("eye", [P, P])
        tok = [sb(f"tok{i}", [P, TT, D]) for i in range(2)]
        idx = [sb(f"idx{i}", [P, TT, 2], U32) for i in range(2)]
        widx = [sb(f"widx{i}", [P, 1], U32) for i in range(DEPTH)]
        W = [sb(f"W{i}", [P, WCOLS]) for i in range(DEPTH)]
        X = [sb(f"X{i}", [P, ROWS // P, D]) for i in range(DEPTH)]
        XT = [sb(f"XT{i}", [KC, 2, ROWS]) for i in range(2)]
        Gl = [sb(f"Gl{i}", [P, FC, ROWS]) for i in range(2)]
        Y = [sb(f"Y{i}", [P, ROWS // P, D]) for i in range(DEPTH)]
        yc = [sb(f"yc{i}", [P, TT, D]) for i in range(2)]
        yu = [sb(f"yu{i}", [P, TT, D]) for i in range(2)]
        xt_ps = [ps(f"xt_ps{i}") for i in range(2)]
        h_ps = [ps(f"h_ps{i}") for i in range(4)]
        y_ps = [ps(f"y_ps{i}") for i in range(2)]

        eye_in = sem("eye_in")
        tok_in = sems("tok_in", 2)
        idx_ready = sem("idx_ready")
        tok_out = sems("tok_out", 2)
        block1 = ctx.enter_context(ExitStack())
        block = block1.enter_context(nc.Block())
        apart = {e: sem(f"apart_x{i}") for i, e in enumerate((nc.sync.engine, nc.gpsimd.engine, nc.vector.engine))}

        def wait_apart(eng, semaphore, value):
            eng.wait_ge(semaphore, value)
            eng.sem_inc(apart[eng.engine], 1)

        @block.sync
        def _(sp):
            def load(par, n, half):
                if not isinstance(half, int):
                    wait_apart(sp, tok_out[par], half * (16 * 2 * TT))
                sp.dma_start(tok[par][:, 0:2, :], xn2_d[n, 0:2 * P, :].rearrange("(t p) d -> p t d", p=P)).then_inc(tok_in[par], 16)
                sp.dma_start(tok[par][0:TLEN[2], 2, :], xn2_d[n, 2 * P:S, :]).then_inc(tok_in[par], 16)

            sp.dma_start(eye[:], A["ident"]).then_inc(eye_in, 16)
            for par in range(2):
                load(par, par, 0)
            with sp.Fori(1, B // 2) as half:
                for par in range(2):
                    load(par, half * 2 + par, half)
            sp.wait_ge(eye_in, 16)

        @block.gpsimd
        def _(pool):
            def scatter(par, n, half):
                if not isinstance(half, int):
                    wait_apart(pool, tok_out[par], half * (16 * 2 * TT))
                pool.tensor_copy(idx[par][:], pos[:, bass.ds(n * TT, TT), :]).then_inc(idx_ready, 1)
                wait_apart(pool, idx_ready, n + 1)
                wait_apart(pool, tok_in[par], half * 32 + 32)
                for k in range(TT):
                    for kind in range(2):
                        r = slice(0, TLEN[k])
                        pool.indirect_dma_start(xs_d[:, :], bass.IndirectOffsetOnAxis(idx[par][r, k, kind:kind + 1], 0), tok[par][r, k, :],
                                                None, bounds_check=ZROW - 1, oob_is_err=False).then_inc(tok_out[par], 16)

            for par in range(2):
                scatter(par, par, 0)
            with pool.Fori(1, B // 2) as half:
                for par in range(2):
                    scatter(par, half * 2 + par, half)
            for par in range(2):
                pool.wait_ge(tok_out[par], B // 2 * 16 * 2 * TT)

        block1.close()
        w_in = sems("w_in")
        rows_in = sems("rows_in")
        widx_ready = sem("widx_ready")
        xt_filled = sem("xt_filled")
        xt_ready = sem("xt_ready")
        h_filled = sem("h_filled")
        g_ready = sem("g_ready")
        y_filled = sem("y_filled")
        y_ready = sem("y_ready")
        y_out = sems("y_out")
        block2 = ctx.enter_context(ExitStack())
        block = block2.enter_context(nc.Block())

        class Tile:

            def __init__(self, quad, i):
                self.quad, self.i, self.n = quad, i, quad * DEPTH + i
                self.par = i % 2

            def next(self):
                return Tile(self.quad + (self.i + 1) // DEPTH, (self.i + 1) % DEPTH)

            def prev(self):
                return Tile(self.quad, self.i - 1) if self.i else Tile(self.quad - 1, DEPTH - 1)

            def is_first(self):
                return isinstance(self.n, int) and self.n == 0

            def is_last(self):
                return isinstance(self.n, int) and self.n == TILES - 1

        def tiles(eng, body):
            for i in range(DEPTH):
                body(Tile(0, i))
            with eng.Fori(1, TILES // DEPTH - 1) as quad:
                for i in range(DEPTH):
                    body(Tile(quad, i))
            for i in range(DEPTH):
                body(Tile(TILES // DEPTH - 1, i))

        @block.sync
        def _(sp):
            def body(t):
                peeled = isinstance(t.n, int)
                if not (peeled and t.n < DEPTH):
                    wait_apart(sp, xt_filled, t.n - (DEPTH - 1))
                sp.dma_start(X[t.i][:], xs_d[bass.ds(t.n * ROWS, ROWS), :].rearrange("(t p) d -> p t d", p=P)).then_inc(rows_in[t.i], 16)
                if not (peeled and t.n < 2):
                    store(t.prev().prev())

            def store(t):
                wait_apart(sp, y_ready, t.n + 1)
                sp.dma_start(y_d[bass.ds(t.n * ROWS, ROWS), :].rearrange("(t p) d -> p t d", p=P), Y[t.i][:]).then_inc(y_out[t.i], 16)

            tiles(sp, body)
            t = Tile(TILES // DEPTH - 1, DEPTH - 1)
            store(t.prev())
            store(t)
            for s in y_out:
                sp.wait_ge(s, 16 * (TILES // DEPTH))

        @block.gpsimd
        def _(pool):
            def body(t):
                if not (isinstance(t.n, int) and t.n < DEPTH):
                    wait_apart(pool, y_ready, t.n - (DEPTH - 1))
                pool.tensor_copy(widx[t.i][:], wrow[:, bass.ds(t.n, 1)]).then_inc(widx_ready, 1)
                wait_apart(pool, widx_ready, t.n + 1)
                pool.indirect_dma_start(W[t.i][:, :], None, A["experts"], bass.IndirectOffsetOnAxis(widx[t.i][:, 0:1], 0)).then_inc(w_in[t.i], 16)

            tiles(pool, body)

        @block.tensor
        def _(pe):
            def turn(t):
                pe.wait_ge(rows_in[t.i], t.quad * 16 + 16)
                if not (isinstance(t.n, int) and t.n < 2):
                    pe.wait_ge(xt_ready, t.n - 1)
                for c in range(2):
                    for k in range(ROWS // P):
                        mm = pe.transpose(xt_ps[t.par][0:KC, c * ROWS + k * P:c * ROWS + (k + 1) * P],
                                          X[t.i][:, k, c * KC:(c + 1) * KC], eye[:])
                mm.then_inc(xt_filled, 1)

            def up(t):
                pe.wait_ge(w_in[t.i], t.quad * 16 + 16)
                pe.wait_ge(xt_ready, t.n + 1)
                for f in range(FC):
                    k = t.par * FC + f
                    bank = k % 4
                    if not (isinstance(t.n, int) and t.n * FC + f < 4):
                        pe.wait_ge(g_ready, t.n * FC + (f - 3))
                    for c in range(2):
                        mm = pe.matmul(h_ps[bank][:, 0:ROWS], W[t.i][0:KC, c * FF + f * P:c * FF + (f + 1) * P],
                                       XT[t.par][:, c, :], start=(c == 0), stop=(c == 1))
                    mm.then_inc(h_filled, 1)

            def down(t):
                pe.wait_ge(g_ready, t.n * FC + FC)
                if not (isinstance(t.n, int) and t.n < 2):
                    pe.wait_ge(y_ready, t.n - 1)
                for k in range(ROWS // P):
                    for f in range(FC):
                        mm = pe.matmul(y_ps[t.par][:, k * D:(k + 1) * D], Gl[t.par][:, f, k * P:(k + 1) * P],
                                       W[t.i][:, W2O + f * D:W2O + (f + 1) * D], start=(f == 0), stop=(f == FC - 1))
                mm.then_inc(y_filled, 1)

            def body(t):
                if t.is_first():
                    turn(t)
                if not t.is_last():
                    turn(t.next())
                up(t)
                if not t.is_first():
                    down(t.prev())
                if t.is_last():
                    down(t)

            pe.wait_ge(eye_in, 16)
            tiles(pe, body)

        @block.scalar
        def _(act):
            act = nc.scalar

            def body(t):
                act.wait_ge(w_in[t.i], t.quad * 16 + 16)
                if not (isinstance(t.n, int) and t.n < 2):
                    act.wait_ge(y_filled, t.n - 1)
                for f in range(FC):
                    bank = (t.par * FC + f) % 4
                    act.wait_ge(h_filled, t.n * FC + f + 1)
                    act.activation(Gl[t.par][:, f, :], h_ps[bank][:, 0:ROWS], ACT.Gelu,
                                   bias=W[t.i][:, B1O + f:B1O + f + 1]).then_inc(g_ready, 1)

            tiles(act, body)

        @block.vector
        def _(dve):
            def turned(t):
                dve.wait_ge(xt_filled, t.n + 1)
                if not (isinstance(t.n, int) and t.n < 2):
                    dve.wait_ge(h_filled, (t.n - 1) * FC)
                dve.tensor_copy(XT[t.par][:], xt_ps[t.par][0:KC, :].rearrange("p (c t) -> p c t", c=2)).then_inc(xt_ready, 1)

            def finish(t):
                dve.wait_ge(y_filled, t.n + 1)
                if not (isinstance(t.n, int) and t.n < DEPTH):
                    dve.wait_ge(y_out[t.i], t.quad * 16)
                b2 = W[t.i][:, B2O:B2O + D].rearrange("p (a d) -> p a d", a=1).broadcast_to([P, ROWS // P, D])
                dve.tensor_tensor(Y[t.i][:], y_ps[t.par][:, 0:ROWS // P * D].rearrange("p (t d) -> p t d", d=D), b2,
                                  ALU.add).then_inc(y_ready, 1)

            def body(t):
                if t.is_first():
                    turned(t)
                if not t.is_last():
                    turned(t.next())
                if not t.is_first():
                    finish(t.prev())
                if t.is_last():
                    finish(t)

            tiles(dve, body)

        block2.close()

        h_in = sems("h_in", 2)
        y_in = sems("y_in", 2)
        first_sum = sem("first_sum")
        sums = sem("sums")
        idx2 = sem("idx2")
        out_done = sems("out_done", 2)
        act_apart = sem("act_apart")
        block = ctx.enter_context(nc.Block())

        @block.sync
        def _(sp):
            def load(par, n, half):
                wait_apart(sp, out_done[par], half * 32 + FREE)
                sp.dma_start(tok[par][:, 0:2, :], h2_d[n, 0:2 * P, :].rearrange("(t p) d -> p t d", p=P)).then_inc(h_in[par], 16)
                sp.dma_start(tok[par][0:TLEN[2], 2, :], h2_d[n, 2 * P:S, :]).then_inc(h_in[par], 16)

            with sp.Fori(0, B // 2) as half:
                for par in range(2):
                    load(par, half * 2 + par, half)
            for s in out_done:
                sp.wait_ge(s, B // 2 * 32 + FREE)

        @block.scalar
        def _(act):
            for e in out_done:
                nc.scalar.sem_inc(e, FREE)
            with nc.scalar.Fori(0, B // 2) as half:
                for par in range(2):
                    n = half * 2 + par
                    nc.scalar.wait_ge(sums, n + 1)
                    nc.scalar.sem_inc(act_apart, 1)
                    nc.scalar.dma_start(out[n, 0:2 * P, :].rearrange("(t p) d -> p t d", p=P), tok[par][:, 0:2, :]).then_inc(out_done[par], 16)
                    nc.scalar.dma_start(out[n, 2 * P:S, :], tok[par][0:TLEN[2], 2, :]).then_inc(out_done[par], 16)

        @block.gpsimd
        def _(pool):
            with pool.Fori(0, B // 2) as half:
                for par in range(2):
                    n = half * 2 + par
                    wait_apart(pool, out_done[par], half * 32 + FREE)
                    pool.tensor_copy(idx[par][:], pos[:, bass.ds(n * TT, TT), :]).then_inc(idx2, 1)
                    wait_apart(pool, idx2, n + 1)
                    for k in range(TT):
                        r = slice(0, TLEN[k])
                        for kind, dst in enumerate((yc, yu)):
                            pool.indirect_dma_start(dst[par][r, k, :], None, y_d[:, :],
                                                    bass.IndirectOffsetOnAxis(idx[par][r, k, kind:kind + 1], 0)).then_inc(y_in[par], 16)

        @block.vector
        def _(dve):
            with dve.Fori(0, B // 2) as half:
                for par in range(2):
                    n = half * 2 + par
                    dve.wait_ge(h_in[par], half * 32 + 32)
                    dve.wait_ge(y_in[par], half * (32 * TT) + 32 * TT)
                    for kind, src in enumerate((yc, yu)):
                        for k in range(TT):
                            r = slice(0, TLEN[k])
                            ins = dve.scalar_tensor_tensor(tok[par][r, k, :], src[par][r, k, :],
                                                           scale[r, bass.ds(n * TT + k, 1), kind], tok[par][r, k, :], ALU.mult, ALU.add)
                        if kind == 0:
                            ins.then_inc(first_sum, 1)
                            dve.wait_ge(first_sum, n + 1)
                    ins.then_inc(sums, 1)


def build(nc, A, out):
    ctx = ExitStack()
    with ctx:
        def sb(name, shape, dt=F32):
            return ctx.enter_context(nc.sbuf_tensor(name, shape, dt))

        logits = sb("logits", [P, B, TT, NE])
        pos = sb("pos", [P, COLS, 2], U32)
        scale = sb("scale", [P, COLS, 2])
        wrow = sb("wrow", [P, TILES], U32)
        h2_d = nc.dram_tensor("h2_d", [B, S, D], F32).ap()
        xn2_d = nc.dram_tensor("xn2_d", [B, S, D], F32).ap()
        xs_d = nc.dram_tensor("xs_d", [ZROW, D], F32).ap()
        y_d = nc.dram_tensor("y_d", [ZROW + 1, D], F32).ap()
        attention(nc, A, logits, h2_d, xn2_d)
        route_tokens(nc, A, logits, pos, scale, wrow, xs_d, y_d)
        run_experts(nc, A, pos, scale, wrow, h2_d, xn2_d, xs_d, y_d, out)
    return nc


IN_NAMES = ["xT", "txt", "ident", "masks", "cosw", "sinw", "base", "biasb", "w_emb", "w_qkv", "w_o", "w_r", "rconsts", "before", "experts"]


def layout(I):
    a = {k: np.asarray(v) for k, v in I.items()}
    side, pp = 14, 16
    x = a["x"].reshape(B, side, pp, side, pp, 3).transpose(0, 5, 2, 4, 1, 3).reshape(B, EC, P, NPATCH)
    xT = np.zeros((B, P, EC, NPATCH + 1), np.float32)
    xT[:, :, :, 1:] = x.transpose(0, 2, 1, 3)
    o = {"xT": xT, "txt": a["txt"]}
    o["ident"] = np.eye(P, dtype=np.float32)
    i = np.arange(P)
    later = np.where(i[None, :] > i[:, None], BIG, 0.0)
    o["masks"] = np.stack([later, later.T], 1).astype(np.float32)
    inv = (1.0 / np.float32(10000.0) ** (np.arange(D // 2, dtype=np.float32) * np.float32(2.0) / np.float32(D))).astype(np.float32)
    ang = (np.arange(TT * P, dtype=np.float32)[:, None] * inv[None, :]).astype(np.float32)
    cos = np.repeat(np.cos(ang).astype(np.float32), 2, 1)
    sin = np.repeat(np.sin(ang).astype(np.float32), 2, 1) * np.tile(np.float32([-1, 1]), D // 2)
    tiles = lambda t: np.ascontiguousarray(np.tile(t, (1, 2)).reshape(TT, P, 2 * D).transpose(1, 0, 2)).astype(np.float32)
    o["cosw"], o["sinw"] = tiles(cos), tiles(sin)
    pos = np.zeros((2 * P, D), np.float32)
    pos[:NPATCH + 1] = a["L0_tok_pos_embed"][0]
    bias = np.tile(a["L0_tok_b"], (2 * P, 1))
    bias[0] = a["L0_tok_cls_token"][0, 0]
    o["base"] = np.ascontiguousarray(pos.reshape(2, P, D).transpose(1, 0, 2))
    o["biasb"] = np.ascontiguousarray(bias.reshape(2, P, D).transpose(1, 0, 2))
    o["w_emb"] = np.ascontiguousarray(a["L0_tok_W"].T.reshape(EC, P, D).transpose(1, 0, 2))

    def chunks(w, bias):
        c = np.zeros((KC + 1, 2, w.shape[1]), np.float32)
        c[:KC, 0], c[:KC, 1], c[KC, 0] = w[:KC], w[KC:], bias
        return c

    o["w_qkv"] = chunks(np.concatenate([a[f"L0_attn_W{k}"] for k in "qkv"], 1), np.concatenate([a[f"L0_attn_b{k}"] for k in "qkv"]))
    o["w_o"] = chunks(a["L0_attn_Wo"], a["L0_attn_bo"])
    o["w_r"] = chunks(np.concatenate([a["L0_ffn_Wsc"], a["L0_ffn_Wsu"]], 1), np.concatenate([a["L0_ffn_bsc"], a["L0_ffn_bsu"]]))
    lane, col = np.arange(P)[:, None], np.arange(COLS)[None, :]
    c = dict(valid=(TOFF[1] * (col % TT) + lane < S), seg=np.tile(col > 0, (P, NX)), rank=np.tile(NX - np.arange(NX), (P, 1)),
             kth=np.tile(ROWS * np.arange(KTH), (P, 1)), tile=np.tile(np.arange(TILES), (P, 1)), lane=lane, one=np.ones((P, NX)))
    o["rconsts"] = np.concatenate([c[k].astype(np.float32) for k in CONSTS], 1)
    o["before"] = (lane < np.arange(P)[None, :]).astype(np.float32)
    w = np.zeros((2, NX, P, WCOLS), np.float32)
    for i, kind in enumerate("cu"):
        w[i, :, :KC, W1O:W2O] = a[f"L0_ffn_W1{kind}"].reshape(NX, 2, KC, FF).transpose(0, 2, 1, 3).reshape(NX, KC, 2 * FF)
        w[i, :, :, W2O:B1O] = a[f"L0_ffn_W2{kind}"].reshape(NX, FC, P, D).transpose(0, 2, 1, 3).reshape(NX, P, FC * D)
        w[i, :, :, B1O:B2O] = a[f"L0_ffn_b1{kind}"].reshape(NX, FC, P).transpose(0, 2, 1)
        w[i, :, :, B2O:] = a[f"L0_ffn_b2{kind}"][:, None, :]
    o["experts"] = w.reshape(2 * NX * P, WCOLS)
    return o


def kernel(**inputs):
    import concourse.bacc as _bacc
    from concourse.bass_utils import run_bass_kernel_spmd as _run

    nc = _bacc.Bacc("TRN2", target_bir_lowering=False, num_devices=1)
    arrays, aps = {}, {}
    for name, array in layout(inputs).items():
        arrays[f"in_{name}_dram"] = np.ascontiguousarray(array)
        aps[name] = nc.dram_tensor(f"in_{name}_dram", array.shape, mybir.dt.from_np(array.dtype), kind="ExternalInput").ap()
    out = nc.dram_tensor("out_0_dram", (B, S, D), F32, kind="ExternalOutput").ap()
    build(nc, aps, out)
    r = _run(nc, [arrays], core_ids=[0])
    return r.results[0]["out_0_dram"]
```

```python
from contextlib import ExitStack

import numpy as np
import concourse.bass as bass
from concourse import mybir

F32 = mybir.dt.float32
BF16 = mybir.dt.bfloat16
U32 = mybir.dt.uint32
ALU = mybir.AluOpType
ACT = mybir.ActivationFunctionType
AX = mybir.AxisListType

P = 128
B = 32
D = 192
NPATCH, NTXT = 196, 77
S = 1 + NPATCH + NTXT
HEADS, HD = 12, 16
GROUPS, GH = 3, 4
TT = 3
TOFF = [0, 128, 256]
TLEN = [128, 128, S - 256]
IMG1 = 1 + NPATCH - 128
KC = 96
EC = 6
EPS = 1e-5
BIG = -1e30
PARTS = 6
KS_ROWS = PARTS * HD
KROWS = KS_ROWS + 3
SCALE = 0.25
Q2 = S - 32
NE = 8

PAD = 2
FREE = 1

FF = 768
NX = 4
N = B * S
CAP = N // NX
COLS = B * TT
ROWS = 256
CT = (N + NX * (ROWS - 1)) // ROWS
UT = (N - CAP + NX * (ROWS - 1)) // ROWS
DEPTH = 4
TILES = -(-(CT + UT) // DEPTH) * DEPTH
FC = FF // P
W1O, W2O, B1O, B2O = 0, 2 * FF, 2 * FF + FC * D, 2 * FF + FC * D + FC
WCOLS = B2O + D
RU, RC = D + 2, 2 * D + 2
NOWHERE = 2.0 ** 14
KTH = max(CT, UT) + 2
CONSTS = dict(valid=COLS, ids=COLS, seg=NX * COLS, rank=NX, kth=KTH, tile=TILES, lane=1, one=NX)
CWIDTH = sum(CONSTS.values())

PREP_EMB = ["emb0", "emb1"]
MAXS = ["mq0", "mq1", "mq2"]
XNT = ["xnT0", "xnT1"]
QKV = ["qk0", "v0", "qk1", "v1", "qk2", "v2"]
STEADY = (PREP_EMB + MAXS + ["mT"] + XNT + QKV
          + ["t0", "ut0", "ut1", "ut2", "t1", "at0", "at1", "t2", "o0", "o1", "t3", "t4", "t5", "t6", "x20", "x21", "t7", "r"])
FIRST = PREP_EMB + XNT + QKV + [f"t{u}" for u in range(8)]
LAST = MAXS + ["mT"] + ["ut0", "ut1", "ut2", "at0", "at1", "o0", "o1", "x20", "x21", "r"]
assert len(STEADY) % 2 == 0 and len(FIRST) % 2 == 0 and len(LAST) % 2 == 0


class Batch:

    def __init__(self, half, par):
        self.half, self.par, self.n = half, par, half * 2 + par

    def next(self):
        return Batch(self.half + self.par, 1 - self.par)


class Turn:

    def __init__(self, at, pre):
        self.at, self.pre = at, pre
        self.uses = STEADY if at and pre else FIRST if pre else LAST

    def bank(self, use):
        return self.uses.index(use) % 2

    def before(self, use=None):
        k = self.uses.index(use) // 2 if use else 0
        return k if self.at is None else self.at.n * (len(STEADY) // 2) + (len(FIRST) // 2 + k)


def rounds(eng, body):
    body(Turn(None, Batch(0, 0)))
    with eng.Fori(0, B // 2 - 1) as half:
        for par in range(2):
            b = Batch(half, par)
            body(Turn(b, b.next()))
    b = Batch(B // 2 - 1, 0)
    body(Turn(b, b.next()))
    body(Turn(b.next(), None))


class Steps:

    def __init__(self, eng, sem, first, steady):
        self.eng, self.sem, self.first, self.steady = eng, sem, first, steady

    def begin(self, turn):
        self.k, self.turn = 0, turn
        self.base = 0 if turn.at is None else turn.at.n * self.steady + self.first

    def done(self, ins):
        ins.then_inc(self.sem, 1)
        self.k += 1
        return self.k

    def need(self, k):
        self.eng.wait_ge(self.sem, self.base + k)

    def end(self):
        want = self.first if self.turn.at is None else self.steady
        assert self.turn.pre is None or self.k == want, (self.k, want)


def attention(nc, A, logits, h2_d, xn2_d, xc_d, xu_d):
    ctx = ExitStack()
    with ctx:
        def sb(name, shape, dt=F32):
            return ctx.enter_context(nc.sbuf_tensor(name, shape, dt))

        def ps(name, shape, dt=F32):
            return ctx.enter_context(nc.psum_tensor(name, shape, dt))

        def sem(name):
            return ctx.enter_context(nc.semaphore(name))

        ident = sb("ident", [P, P])
        identb = sb("identb", [P, P], BF16)
        masks = sb("masks_f", [P, 2, P])
        mask_qk = sb("mask_qk", [P, P], BF16)
        mask_kq = sb("mask_kq", [P, P], BF16)
        cosw = sb("cosw", [P, TT, 2 * D])
        sinw = sb("sinw", [P, TT, 2 * D])
        base = sb("base", [P, 2, D])
        biasb = sb("biasb", [P, 2, D])
        w_emb = sb("w_emb", [P, EC, D])
        w_qkv = sb("w_qkv", [KC + 1, 2, 3 * D])
        w_o = sb("w_o", [KC + 1, 2, D])
        w_r = sb("w_r", [KC + 1, 2, NE])
        xT = [sb(f"xT{i}", [P, EC, NPATCH + 1]) for i in range(2)]
        h = [sb(f"h{i}", [P, TT, D]) for i in range(2)]
        stat = sb("stat", [P, 2, TT, 6])
        mv = sb("mv", [P, 2, TT, 2])
        veps = sb("veps", [P, 2, TT])
        rstd = sb("rstd", [P, 2, TT])
        minus_half = sb("minus_half", [P, TT])
        xn = sb("xn", [P, TT, D])
        xnT = sb("xnT", [KC + 1, 2, S])
        ropeA = sb("ropeA", [P, TT, 2 * D])
        ropeB = sb("ropeB", [P, TT, 2 * D])
        rr = sb("rr", [P, TT, 2 * D])
        d1 = sb("d1", [P, TT, 2 * D])
        stk = sb("stk", [P, TT, 2 * HEADS, PARTS, HD], BF16)
        QS = [sb(f"QS{i}", [P, HEADS, S], BF16) for i in range(2)]
        KS = [sb(f"KS{i}", [P, HEADS, S], BF16) for i in range(2)]
        V = [sb(f"V{i}", [P, TT, HEADS, 32]) for i in range(2)]
        NM = 2 * HEADS + GROUPS
        nm3 = sb("nm3", [P, HEADS, 3])
        nm = sb("nm", [P, NM])
        nmd = sb("nmd", [P, NM])
        nmp = sb("nmp", [P, TT, HEADS, 3], BF16)
        mT = sb("mT", [3 * HEADS, TT, P], BF16)
        PT = [sb(f"PT{i}", [P, GH, 438]) for i in range(2)]
        Usb = sb("Usb", [P, GROUPS, S])
        rec = sb("rec", [P, TT, HEADS])
        att = sb("att", [P, TT, D])
        attT = sb("attT", [KC + 1, 2, S])
        h2 = [sb(f"hh{i}", [P, TT, D]) for i in range(2)]
        xn2 = [sb(f"xn2{i}", [P, TT, D]) for i in range(2)]
        xn2T = sb("xn2T", [KC + 1, 2, S])
        padding = sb("padding", [P, PAD, RC])
        SP_ = [ps(f"scores{i}", [P, 512]) for i in range(3)]
        MP = [ps(f"maxs{i}", [P, 512]) for i in range(2)]
        UP = ps("attn", [P, 512])
        G = [ps(f"gen{i}", [P, 512]) for i in range(2)]
        Gb = [g[:, :].bitcast(BF16) for g in G]

        consts_in = sem("consts_in")
        consts_set = sem("consts_set")
        x_in = [sem(f"x_in{i}") for i in range(2)]
        txt_in = [sem(f"txt_in{i}") for i in range(2)]
        g_filled = [sem(f"g_filled{i}") for i in range(2)]
        g_emptied = [sem(f"g_emptied{i}") for i in range(2)]
        steps = sem("steps")
        xn_ready = sem("xn_ready")
        var_ready = [sem(f"var_ready{i}") for i in range(2)]
        veps_ready = [sem(f"veps_ready{i}") for i in range(2)]
        rstd_ready = [sem(f"rstd_ready{i}") for i in range(2)]
        rope_r = sem("rope_r")
        part0 = sem("part0")
        diff1 = sem("diff1")
        part1 = sem("part1")
        parts_ready = sem("parts_ready")
        m_filled = [sem(f"m_filled{i}") for i in range(2)]
        m_read = [sem(f"m_read{i}") for i in range(2)]
        nmax_ready = sem("nmax_ready")
        mrow_in = [sem(f"mrow_in{i}") for i in range(2)]
        s_filled = [sem(f"s_filled{i}") for i in range(3)]
        p_ready = sem("p_ready")
        u_filled = sem("u_filled")
        u_read = sem("u_read")
        xn2_ready = sem("xn2_ready")
        rows_out = [sem(f"rows_out{i}") for i in range(2)]
        padding_set, padded = sem("padding_set"), sem("padded")
        apart = {e: sem(f"apart_{i}") for i, e in enumerate((nc.sync.engine, nc.gpsimd.engine, nc.vector.engine, nc.tensor.engine))}

        loads = ((ident, "ident"), (masks, "masks"),
                 (cosw, "cosw"), (sinw, "sinw"), (base, "base"), (biasb, "biasb"), (w_emb, "w_emb"),
                 (w_qkv, "w_qkv"), (w_o, "w_o"), (w_r, "w_r"))
        n_set = 15
        block = ctx.enter_context(nc.Block())

        def wait_apart(eng, semaphore, value):
            eng.wait_ge(semaphore, value)
            eng.sem_inc(apart[eng.engine], 1)

        @block.sync
        def _(sp):
            for e in rows_out:
                sp.sem_inc(e, FREE)
            for dst, src in loads:
                sp.dma_start(dst[:], A[src]).then_inc(consts_in, 16)

            def load_x(b):
                sp.dma_start(xT[b.par][:], A["xT"][b.n]).then_inc(x_in[b.par], 16)

            def load_txt(b):
                sp.dma_start(h[b.par][IMG1:P, 1, :], A["txt"][b.n, 0:P - IMG1, :]).then_inc(txt_in[b.par], 16)
                sp.dma_start(h[b.par][0:TLEN[2], 2, :], A["txt"][b.n, P - IMG1:NTXT, :]).then_inc(txt_in[b.par], 16)

            def body(t, more=True):
                if t.at is None:
                    for b in (t.pre, t.pre.next()):
                        load_x(b)
                        load_txt(b)
                    return
                b = t.at
                if more:
                    for e in g_emptied:
                        wait_apart(sp, e, t.before())
                    load_x(b.next().next())
                wait_apart(sp, g_emptied[t.bank("mT")], t.before("mT") + 1)
                for r in range(3):
                    row = QS[b.par][KS_ROWS + r:KS_ROWS + r + 1, :, :]
                    sp.dma_start(row[:, :, 0:2 * P], mT[r:3 * HEADS:3, 0:2, :].rearrange("h t q -> h (t q)")).then_inc(mrow_in[b.par], 16)
                    sp.dma_start(row[:, :, 2 * P:S],
                                 mT[r:3 * GROUPS:3, 2, :].rearrange("j (g q) -> j g q", g=GH)[:, :, 32 - TLEN[2]:32]
                                 ).then_inc(mrow_in[b.par], 16)
                for use in ("o0", "o1"):
                    wait_apart(sp, g_emptied[t.bank(use)], t.before(use) + 1)
                if more:
                    load_txt(b.next().next())
                out_ = rows_out[b.par]
                sp.dma_start(h2_d[b.n, 0:2 * P, :].rearrange("(t p) d -> p t d", p=P), h2[b.par][:, 0:2, :]).then_inc(out_, 16)
                sp.dma_start(h2_d[b.n, 2 * P:S, :], h2[b.par][0:TLEN[2], 2, :]).then_inc(out_, 16)
                wait_apart(sp, xn2_ready, b.n + 1)
                sp.dma_start(xn2_d[b.n, 0:2 * P, :].rearrange("(t p) d -> p t d", p=P), xn2[b.par][:, 0:2, :]).then_inc(out_, 16)
                sp.dma_start(xn2_d[b.n, 2 * P:S, :], xn2[b.par][0:TLEN[2], 2, :]).then_inc(out_, 16)

            def plain(t):
                body(t, more=not (t.at is not None and isinstance(t.at.n, int)))

            rounds(sp, plain)
            sp.wait_ge(g_emptied[0], len(FIRST) // 2 + (B - 1) * len(STEADY) // 2 + len(LAST) // 2)
            sp.wait_ge(g_emptied[1], len(FIRST) // 2 + (B - 1) * len(STEADY) // 2 + len(LAST) // 2)
            for p in range(2):
                sp.wait_ge(rows_out[p], 64 * (B // 2) + FREE)

        @block.tensor
        def _(pe):
            pe.wait_ge(consts_in, 16 * len(loads))
            pe.wait_ge(consts_set, n_set)

            def fill(t, use):
                pe.wait_ge(g_emptied[t.bank(use)], t.before(use))
                return t.bank(use)

            def have(t, use):
                pe.wait_ge(g_emptied[t.bank(use)], t.before(use) + 1)

            def embed(t, k):
                b = t.pre
                if k == 0:
                    pe.wait_ge(x_in[b.par], b.half * 16 + 16)
                g = fill(t, f"emb{k}")
                cols, m = (slice(0, P), P) if k == 0 else (slice(P, NPATCH + 1), IMG1)
                for c in range(EC):
                    mm = pe.matmul(G[g][0:m, 0:D], xT[b.par][:, c, cols], w_emb[:, c, :], start=(c == 0), stop=(c == EC - 1))
                mm.then_inc(g_filled[g], 1)

            def maxs(t, head):
                b, i = t.at, head % 2
                if head == 0:
                    for e in g_emptied:
                        pe.wait_ge(e, t.before())
                pe.wait_ge(m_read[i], b.n * (HEADS // 2) + head // 2 + FREE)
                q, k, r = QS[b.par], KS[b.par], slice(0, KS_ROWS)
                pe.matmul(MP[i][:, 0:P], q[r, head, 0:P], k[r, head, 0:P], start=True, stop=False, skip_group_check=True)
                pe.matmul(MP[i][:, 0:P], identb[:], mask_qk[:], start=False, stop=True, skip_group_check=True)
                pe.matmul(MP[i][:, P:3 * P], q[r, head, P:2 * P], k[r, head, 0:2 * P], start=True, stop=False, skip_group_check=True)
                pe.matmul(MP[i][:, 2 * P:3 * P], identb[:], mask_qk[:], start=False, stop=True, skip_group_check=True).then_inc(m_filled[i], 1)

            def maxs2(t, j):
                b = t.at
                g = fill(t, f"mq{j}")
                q, k, r = QS[b.par], KS[b.par], slice(0, KS_ROWS)
                for i in range(GH):
                    head, rows = GH * j + i, slice(32 * i, 32 * i + 32)
                    pe.matmul(G[g][rows, 0:S], q[r, head, Q2:S], k[r, head, :], start=True, stop=False, skip_group_check=True)
                    mm = pe.matmul(G[g][rows, Q2:S], identb[0:32, 0:32], mask_qk[0:32, 0:32], start=False, stop=True,
                                   tile_position=(0, 32 * i), skip_group_check=True)
                mm.then_inc(g_filled[g], 1)

            def turn_tokens(t, src, use):
                c = int(use[-1])
                g = fill(t, use)
                for k in range(TT):
                    mm = pe.transpose(G[g][0:KC, TOFF[k]:TOFF[k] + TLEN[k]], src[0:TLEN[k], k, c * KC:(c + 1) * KC],
                                      ident[0:TLEN[k], 0:TLEN[k]])
                mm.then_inc(g_filled[g], 1)

            def turn_max(t):
                pe.wait_ge(nmax_ready, t.at.n + 1)
                g = fill(t, "mT")
                pe.sem_inc(apart[pe.engine], 1)
                for k in range(TT):
                    mm = pe.transpose(Gb[g][0:3 * HEADS, k * P:(k + 1) * P], nmp[:, k].rearrange("p h r -> p (h r)"), identb[:])
                mm.then_inc(g_filled[g], 1)

            def qkv(t):
                have(t, "xnT0")
                have(t, "xnT1")
                for k in range(TT):
                    tok = slice(TOFF[k], TOFF[k] + TLEN[k])
                    for use, cols in ((f"qk{k}", slice(0, 2 * D)), (f"v{k}", slice(2 * D, 3 * D))):
                        g = fill(t, use)
                        o = G[g][0:TLEN[k], 0:cols.stop - cols.start]
                        pe.matmul(o, xnT[:, 0, tok], w_qkv[:, 0, cols], start=True, stop=False)
                        pe.matmul(o, xnT[0:KC, 1, tok], w_qkv[0:KC, 1, cols], start=False, stop=True).then_inc(g_filled[g], 1)

            def turn_parts(t, u):
                if u == 0:
                    pe.wait_ge(parts_ready, t.pre.n * TT + TT)
                g = fill(t, f"t{u}")
                for i in range(3):
                    for k in range(TT):
                        mm = pe.transpose(Gb[g][0:KS_ROWS, i * S + TOFF[k]:i * S + TOFF[k] + TLEN[k]],
                                          stk[0:TLEN[k], k, 3 * u + i, :, :].rearrange("p a d -> p (a d)"),
                                          identb[0:TLEN[k], 0:TLEN[k]])
                mm.then_inc(g_filled[g], 1)

            def scores(t, head):
                b, i = t.at, head % 3
                if head == 0:
                    pe.wait_ge(mrow_in[b.par], b.half * 96 + 96)
                if head < 3:
                    pe.wait_ge(p_ready, b.n * HEADS + FREE)
                else:
                    pe.wait_ge(p_ready, b.n * HEADS + head - 2 + FREE)
                q, k, s, n = QS[b.par], KS[b.par], SP_[i], TLEN[2]
                r = slice(0, KROWS)
                pe.matmul(s[:, 0:S], k[r, head, 0:P], q[r, head, :], start=True, stop=False, skip_group_check=True)
                pe.matmul(s[:, 0:P], identb[:], mask_kq[:], start=False, stop=True, skip_group_check=True)
                pe.matmul(s[:, S:S + 146], k[r, head, P:2 * P], q[r, head, P:S], start=True, stop=False, skip_group_check=True)
                pe.matmul(s[:, S:S + P], identb[:], mask_kq[:], start=False, stop=True, skip_group_check=True)
                pe.matmul(s[0:n, 420:438], k[r, head, 2 * P:S], q[r, head, 2 * P:S], start=True, stop=False, skip_group_check=True)
                pe.matmul(s[0:n, 420:438], identb[0:n, 0:n], mask_kq[0:n, 0:n], start=False, stop=True,
                          skip_group_check=True).then_inc(s_filled[i], 1)

            def values(t, j):
                b = t.at
                pt = PT[(3 * b.par + j) % 2]
                pe.wait_ge(p_ready, b.n * HEADS + GH * (j + 1) + FREE)
                pe.wait_ge(u_read, b.n * GROUPS + j + FREE)
                for k, (lo, n, at) in enumerate(((0, S, 0), (P, 146, S), (2 * P, TLEN[2], 420))):
                    for i in range(GH):
                        rows = TLEN[k]
                        mm = pe.matmul(UP[32 * i:32 * i + 32, lo:S], V[b.par][0:rows, k, GH * j + i, :],
                                       pt[0:rows, i, at:at + n], start=(k == 0), stop=(k == 2),
                                       tile_position=(0, 32 * i), skip_group_check=True)
                mm.then_inc(u_filled, 1)

            def turn_values(t, k):
                if k == 0:
                    pe.wait_ge(u_read, t.at.n * GROUPS + GROUPS + FREE)
                g = fill(t, f"ut{k}")
                for j in range(GROUPS):
                    mm = pe.transpose(G[g][0:TLEN[k], j * P:(j + 1) * P], Usb[:, j, TOFF[k]:TOFF[k] + TLEN[k]], ident[:])
                mm.then_inc(g_filled[g], 1)

            def project(t):
                have(t, "at0")
                have(t, "at1")
                for use, tiles in (("o0", (0, 1)), ("o1", (2,))):
                    g = fill(t, use)
                    for k in tiles:
                        tok = slice(TOFF[k], TOFF[k] + TLEN[k])
                        o = G[g][0:TLEN[k], (k % 2) * D:(k % 2) * D + D]
                        pe.matmul(o, attT[:, 0, tok], w_o[:, 0, :], start=True, stop=False)
                        mm = pe.matmul(o, attT[0:KC, 1, tok], w_o[0:KC, 1, :], start=False, stop=True)
                    mm.then_inc(g_filled[g], 1)

            def route(t):
                have(t, "x20")
                have(t, "x21")
                g = fill(t, "r")
                for k in range(TT):
                    tok = slice(TOFF[k], TOFF[k] + TLEN[k])
                    o = G[g][0:TLEN[k], k * NE:(k + 1) * NE]
                    pe.matmul(o, xn2T[:, 0, tok], w_r[:, 0, :], start=True, stop=False)
                    mm = pe.matmul(o, xn2T[0:KC, 1, tok], w_r[0:KC, 1, :], start=False, stop=True)
                mm.then_inc(g_filled[g], 1)

            def body(t):
                def part(*us):
                    if t.pre:
                        for u in us:
                            turn_parts(t, u)

                emb = [0, 1] if t.pre else []
                if t.at:
                    for j in range(GROUPS):
                        for head in range(GH * j, GH * j + GH):
                            maxs(t, head)
                            if emb and head % 2:
                                embed(t, emb.pop(0))
                        maxs2(t, j)
                    turn_max(t)
                for k in emb:
                    embed(t, k)
                if t.pre:
                    pe.wait_ge(xn_ready, t.pre.n + 1)
                    turn_tokens(t, xn, "xnT0")
                    turn_tokens(t, xn, "xnT1")
                    qkv(t)
                if t.at:
                    for head in range(HEADS):
                        scores(t, head)
                        if head % GH == 1 and head > GH:
                            values(t, head // GH - 1)
                if t.at:
                    values(t, GROUPS - 1)
                part(0)
                if t.at:
                    for k in range(TT):
                        turn_values(t, k)
                    part(1)
                    for k in range(TT):
                        have(t, f"ut{k}")
                    turn_tokens(t, att, "at0")
                    turn_tokens(t, att, "at1")
                    part(2)
                    project(t)
                    part(3, 4, 5, 6)
                    pe.wait_ge(xn2_ready, t.at.n + 1)
                    turn_tokens(t, xn2[t.at.par], "x20")
                    turn_tokens(t, xn2[t.at.par], "x21")
                    part(7)
                    route(t)
                else:
                    part(1, 2, 3, 4, 5, 6, 7)

            rounds(pe, body)

        def copy_parts(eng, t, u, g):
            dst = (QS if u < 4 else KS)[t.pre.par][0:KS_ROWS, 3 * (u % 4):3 * (u % 4) + 3, :]
            src = Gb[g][0:KS_ROWS, 0:3 * S].rearrange("p (h s) -> p h s", s=S)
            if eng is nc.scalar:
                return eng.activation(dst, src, ACT.Copy)
            return eng.tensor_copy(dst, src)

        @block.scalar
        def _(act):
            act = nc.scalar
            for e in (p_ready, u_read):
                act.sem_inc(e, FREE)

            def take(t, use):
                act.wait_ge(g_filled[t.bank(use)], t.before(use) + 1)
                return t.bank(use)

            def copy_tokens(t, use, dst):
                g, c = take(t, use), int(use[-1])
                act.activation(dst[0:KC, c, :], G[g][0:KC, 0:S], ACT.Copy).then_inc(g_emptied[g], 1)

            def pairs(t, k):
                act.wait_ge(rope_r, t.pre.n * TT + k + 1)
                n = TLEN[k]
                q = rr[0:n, k, 0:D].rearrange("p (h a d) -> p h a d", a=1, d=HD)
                kk = rr[0:n, k, D:2 * D].rearrange("p (h a d) -> p h a d", a=1, d=HD)
                act.activation(stk[0:n, k, 0:HEADS, 0:3, :], q.broadcast_to([n, HEADS, 3, HD]), ACT.Copy)
                act.activation(stk[0:n, k, HEADS:2 * HEADS, 0:4:3, :], kk.broadcast_to([n, HEADS, 2, HD]), ACT.Copy)
                act.activation(stk[0:n, k, HEADS:2 * HEADS, 5:6, :], kk, ACT.Copy).then_inc(part0, 1)

            def weights(t, j):
                b = t.at
                pt = PT[(3 * b.par + j) % 2]
                for i in range(GH):
                    head = GH * j + i
                    s, n = SP_[head % 3], TLEN[2]
                    act.wait_ge(s_filled[head % 3], b.n * (HEADS // 3) + head // 3 + 1)
                    act.activation(pt[0:n, i, 420:438], s[0:n, 420:438], ACT.Exp, scale=SCALE)
                    act.activation(pt[:, i, 0:420], s[:, 0:420], ACT.Exp, scale=SCALE).then_inc(p_ready, 1)

            def attended(t, j):
                act.wait_ge(u_filled, t.at.n * GROUPS + j + 1)
                act.activation(Usb[:, j, :], UP[:, 0:S], ACT.Copy).then_inc(u_read, 1)

            def body(t):
                def parts(*us):
                    if t.pre:
                        for u in us:
                            g = take(t, f"t{u}")
                            copy_parts(act, t, u, g).then_inc(g_emptied[g], 1)

                if t.at:
                    g = take(t, "mT")
                    act.activation(mT[:], Gb[g][0:3 * HEADS, 0:TT * P].rearrange("p (t q) -> p t q", q=P), ACT.Copy).then_inc(g_emptied[g], 1)
                if t.pre:
                    copy_tokens(t, "xnT0", xnT)
                    copy_tokens(t, "xnT1", xnT)
                    for k in range(TT):
                        g = take(t, f"v{k}")
                        act.activation(V[t.pre.par][0:TLEN[k], k, :, 0:HD],
                                       G[g][0:TLEN[k], 0:D].rearrange("p (h d) -> p h d", d=HD), ACT.Copy).then_inc(g_emptied[g], 1)
                        if k:
                            pairs(t, k - 1)
                for j in range(GROUPS):
                    if t.at:
                        weights(t, j)
                    if t.pre and j == 0:
                        pairs(t, 2)
                    if t.at and j:
                        attended(t, j - 1)
                if t.at:
                    attended(t, GROUPS - 1)
                parts(0, 1)
                if t.at:
                    copy_tokens(t, "at0", attT)
                    copy_tokens(t, "at1", attT)
                parts(3, 4, 6)
                if t.at:
                    copy_tokens(t, "x20", xn2T)
                    copy_tokens(t, "x21", xn2T)

            rounds(act, body)

        @block.gpsimd
        def _(pool):
            pool.memset(padding[:], 0.0).then_inc(padding_set, 1)
            pool.wait_ge(padding_set, 1)
            pool.memset(padding[:, :, D + 1:D + 2], NOWHERE).then_inc(padding_set, 1)
            pool.wait_ge(padding_set, 2)
            for rows, width in ((xc_d, RC), (xu_d, RU)):
                for i in range(rows.shape[0] // (P * PAD)):
                    dst = rows[i * P * PAD:(i + 1) * P * PAD, :].rearrange("(p t) d -> p t d", p=P)
                    pool.dma_start(dst, padding[:, :, 0:width]).then_inc(padded, 16)
            pool.wait_ge(consts_set, n_set)

            def root(which, b):
                wait_apart(pool, var_ready[which], b.n + 1)
                pool.tensor_scalar(veps[:, which, :], mv[:, which, :, 1], EPS, None, ALU.add).then_inc(veps_ready[which], 1)
                pool.wait_ge(veps_ready[which], b.n + 1)
                pool.tensor_tensor(rstd[:, which, :], veps[:, which, :], minus_half[:], ALU.pow).then_inc(rstd_ready[which], 1)

            def body(t):
                if t.pre:
                    root(0, t.pre)
                    wait_apart(pool, rstd_ready[0], t.pre.n + 1)
                    for k in range(TT):
                        r = slice(0, TLEN[k])
                        ins = pool.tensor_scalar(xn[r, k, :], h[t.pre.par][r, k, :], mv[r, 0, k, 0:1], rstd[r, 0, k:k + 1],
                                                 ALU.subtract, ALU.mult)
                    ins.then_inc(xn_ready, 1)
                    for k in range(TT):
                        r = slice(0, TLEN[k])
                        pool.wait_ge(g_emptied[t.bank(f"qk{k}")], t.before(f"qk{k}") + 1)
                        pool.tensor_tensor(rr[r, k, :], ropeA[r, k, :], ropeB[r, k, :], ALU.add).then_inc(rope_r, 1)
                    for k in range(TT):
                        n = TLEN[k]
                        wait_apart(pool, diff1, t.pre.n * TT + k + 1)
                        q = d1[0:n, k, 0:D].rearrange("p (h a d) -> p h a d", a=1, d=HD)
                        kk = d1[0:n, k, D:2 * D].rearrange("p (h a d) -> p h a d", a=1, d=HD)
                        pool.tensor_copy(stk[0:n, k, 0:HEADS, 3:5, :], q.broadcast_to([n, HEADS, 2, HD]))
                        pool.tensor_copy(stk[0:n, k, HEADS:2 * HEADS, 1:5:3, :], kk.broadcast_to([n, HEADS, 2, HD])).then_inc(part1, 1)
                if t.at:
                    root(1, t.at)

            rounds(pool, body)
            pool.wait_ge(padded, 16 * TILES * ROWS // (P * PAD))

        @block.vector
        def _(dve):
            for e in m_read:
                dve.sem_inc(e, FREE)
            for p in range(2):
                dve.memset(KS[p][KS_ROWS:KROWS, :, :], 1.0).then_inc(consts_set, 1)
                dve.memset(V[p][:], 1.0).then_inc(consts_set, 1)
            for x in (xnT, attT, xn2T):
                dve.memset(x[KC:KC + 1, :, :], 1.0).then_inc(consts_set, 1)
            dve.memset(mv[:], 1.0).then_inc(consts_set, 1)
            dve.memset(nmp[:], 0.0).then_inc(consts_set, 1)
            dve.memset(logits[:, :, 2, :], 0.0).then_inc(consts_set, 1)
            dve.memset(minus_half[:], -0.5).then_inc(consts_set, 1)
            dve.wait_ge(consts_in, 16 * len(loads))
            dve.tensor_tensor(base[:], base[:], biasb[:], ALU.add).then_inc(consts_set, 1)
            dve.tensor_copy(identb[:], ident[:]).then_inc(consts_set, 1)
            dve.tensor_copy(mask_qk[:], masks[:, 0, :]).then_inc(consts_set, 1)
            dve.tensor_copy(mask_kq[:], masks[:, 1, :]).then_inc(consts_set, 1)
            dve.wait_ge(consts_set, n_set)
            st = Steps(dve, steps, 1, 9)

            def take(t, use):
                dve.wait_ge(g_filled[t.bank(use)], t.before(use) + 1)
                return t.bank(use)

            def norm(src, dst, which, ready, b):
                k = {}

                def stats():
                    for i in range(TT):
                        ins = dve.bn_stats(stat[0:TLEN[i], which, i, :], src[0:TLEN[i], i, :])
                    k["stats"] = st.done(ins)

                def aggr():
                    wait_apart(dve, steps, st.base + k["stats"])
                    for i in range(TT):
                        ins = dve.bn_aggr(mv[0:TLEN[i], which, i, :], stat[0:TLEN[i], which, i, :])
                    ins.then_inc(var_ready[which], 1)

                def scale():
                    dve.wait_ge(rstd_ready[which], b.n + 1)
                    for i in range(TT):
                        n = TLEN[i]
                        ins = dve.tensor_scalar(dst[0:n, i, :], src[0:n, i, :], mv[0:n, which, i, 0:1],
                                                rstd[0:n, which, i:i + 1], ALU.subtract, ALU.mult)
                    ins.then_inc(ready, 1)

                return [stats, aggr, scale]

            def body(t):
                st.begin(t)
                b, pre = t.at, t.pre
                todo = []
                if pre:
                    def emb(k):
                        g = take(t, f"emb{k}")
                        n = P if k == 0 else IMG1
                        ins = dve.tensor_tensor(h[pre.par][0:n, k, :], G[g][0:n, 0:D], base[0:n, k, :], ALU.add)
                        ins.then_inc(g_emptied[g], 1)

                    def text():
                        dve.wait_ge(txt_in[pre.par], pre.half * 32 + 32)
                        dve.wait_ge(g_emptied[t.bank("emb0")], t.before("emb0") + 1)
                        dve.wait_ge(g_emptied[t.bank("emb1")], t.before("emb1") + 1)

                    ln = norm(h[pre.par], xn, 0, xn_ready, pre)
                    todo = [lambda: emb(0), lambda: emb(1), lambda: (text(), ln[0]()), ln[1]]
                if b:
                    for j in range(GROUPS):
                        for head in range(GH * j, GH * j + GH):
                            i = head % 2
                            dve.wait_ge(m_filled[i], b.n * (HEADS // 2) + head // 2 + 1)
                            dve.tensor_reduce(nm3[:, head, :], MP[i][:, 0:3 * P].rearrange("p (t k) -> p t k", k=P), AX.X, ALU.max,
                                              negate=True).then_inc(m_read[i], 1)
                            if todo and (head % 2 or head > 3):
                                todo.pop(0)()
                        g = take(t, f"mq{j}")
                        dve.tensor_reduce(nm[:, 2 * HEADS + j:2 * HEADS + j + 1], G[g][:, 0:S], AX.X, ALU.max,
                                          negate=True).then_inc(g_emptied[g], 1)
                for f in todo:
                    f()
                if b:
                    dve.wait_ge(g_emptied[t.bank("mq2")], t.before("mq2") + 1)
                    dve.tensor_copy(nm[:, 0:HEADS], nm3[:, :, 0])
                    a0 = st.done(dve.tensor_tensor(nm[:, HEADS:2 * HEADS], nm3[:, :, 1], nm3[:, :, 2], ALU.min))
                    st.need(a0)
                    p0, p1, p2 = (nmp[:].rearrange("p t h r -> p (t h) r")[:, 0:NM, r] for r in range(3))
                    a1 = st.done(dve.tensor_copy(p0, nm[:]))
                    st.need(a1)
                    a2 = st.done(dve.tensor_tensor(nmd[:], nm[:], p0, ALU.subtract))
                    st.need(a2)
                    a3 = st.done(dve.tensor_copy(p1, nmd[:]))
                    st.need(a3)
                    dve.tensor_tensor(p2, nmd[:], p1, ALU.subtract).then_inc(nmax_ready, 1)
                if pre:
                    def rotate(k):
                        g, n = take(t, f"qk{k}"), TLEN[k]
                        dve.tensor_tensor(ropeA[0:n, k, :], G[g][0:n, 0:2 * D], cosw[0:n, k, :], ALU.mult)
                        pair = lambda x: x.rearrange("p (m two) -> p m two", two=2)
                        dve.tensor_tensor(pair(ropeB[0:n, k, :]), pair(G[g][0:n, 0:2 * D])[:, :, ::-1],
                                          pair(sinw[0:n, k, :]), ALU.mult).then_inc(g_emptied[g], 1)

                    def second(k):
                        n = TLEN[k]
                        dve.wait_ge(part0, pre.n * TT + k + 1)
                        dve.tensor_tensor(d1[0:n, k, :].rearrange("p (h d) -> p h d", d=HD),
                                          rr[0:n, k, :].rearrange("p (h d) -> p h d", d=HD), stk[0:n, k, :, 0, :],
                                          ALU.subtract).then_inc(diff1, 1)

                    def third(k):
                        n = TLEN[k]
                        dve.wait_ge(part1, pre.n * TT + k + 1)
                        dd = d1[0:n, k, :].rearrange("p (h d) -> p h d", d=HD)
                        dve.tensor_tensor(stk[0:n, k, 0:HEADS, 5, :], dd[:, 0:HEADS], stk[0:n, k, 0:HEADS, 3, :], ALU.subtract)
                        dve.tensor_tensor(stk[0:n, k, HEADS:2 * HEADS, 2, :], dd[:, HEADS:2 * HEADS],
                                          stk[0:n, k, HEADS:2 * HEADS, 1, :], ALU.subtract).then_inc(parts_ready, 1)

                    for f in (rotate, second, third):
                        for k in range(TT):
                            f(k)

                def parts(*us):
                    if pre:
                        for u in us:
                            g = take(t, f"t{u}")
                            copy_parts(dve, t, u, g).then_inc(g_emptied[g], 1)

                if b:
                    for k in range(TT):
                        g, n = take(t, f"ut{k}"), TLEN[k]
                        heads = G[g][0:n, 0:GROUPS * P].rearrange("p (h c) -> p h c", c=32)
                        r = st.done(dve.reciprocal(rec[0:n, k, :], heads[:, :, HD]))
                        st.need(r)
                        dve.tensor_tensor(att[0:n, k, :].rearrange("p (h d) -> p h d", d=HD), heads[:, :, 0:HD],
                                          rec[0:n, k, :].rearrange("p (h a) -> p h a", a=1).broadcast_to([n, HEADS, HD]),
                                          ALU.mult).then_inc(g_emptied[g], 1)
                parts(2)
                if b:
                    dve.wait_ge(rows_out[b.par], b.half * 64 + FREE)
                    g = take(t, "o0")
                    dve.tensor_tensor(h2[b.par][:, 0:2, :].rearrange("p t d -> p (t d)"), G[g][:, 0:2 * D],
                                      h[b.par][:, 0:2, :].rearrange("p t d -> p (t d)"), ALU.add).then_inc(g_emptied[g], 1)
                    g, n = take(t, "o1"), TLEN[2]
                    dve.tensor_tensor(h2[b.par][0:n, 2, :], G[g][0:n, 0:D], h[b.par][0:n, 2, :], ALU.add).then_inc(g_emptied[g], 1)
                    dve.wait_ge(g_emptied[t.bank("o0")], t.before("o0") + 1)
                    dve.wait_ge(g_emptied[t.bank("o1")], t.before("o1") + 1)
                    stats, aggr, scale = norm(h2[b.par], xn2[b.par], 1, xn2_ready, b)
                    stats()
                    aggr()
                    parts(5)
                    scale()
                    parts(7)
                    g = take(t, "r")
                    dve.tensor_copy(logits[:, b.n, 0:2, :], G[g][:, 0:2 * NE].rearrange("p (t e) -> p t e", e=NE))
                    dve.tensor_copy(logits[0:n, b.n, 2, :], G[g][0:n, 2 * NE:3 * NE]).then_inc(g_emptied[g], 1)
                else:
                    parts(5, 7)
                st.end()

            rounds(dve, body)


class Tile:

    def __init__(self, quad, i, search=False, settle=False, spread=False, unique=False):
        self.quad, self.i, self.n = quad, i, quad * DEPTH + i
        self.par = i % 2
        self.search, self.settle, self.spread = search, settle, spread
        self.unique = self.n >= CT if isinstance(quad, int) else unique
        self.number = self.n if isinstance(quad, int) else None

    def before(self, k):
        quad, i = (self.quad, self.i - k) if self.i >= k else (self.quad - 1, self.i - k + DEPTH)
        return Tile(quad, i, unique=self.unique)

    def next(self):
        return Tile(self.quad + (self.i + 1) // DEPTH, (self.i + 1) % DEPTH)

    def at_least(self, n):
        return self.number is None or self.number >= n


SEARCH, SETTLE, SPREAD, SWITCH = 4, 4, 5, CT // DEPTH
SPREAD_END = SPREAD + B // 2 // DEPTH
LAST_QUAD = TILES // DEPTH - 1
assert SPREAD_END <= SWITCH
assert 2 * DEPTH * SEARCH >= 27


def tiles(eng, body):
    def straight(quad, **kind):
        for i in range(DEPTH):
            body(Tile(quad, i, **kind))

    def loop(a, b, **kind):
        with eng.Fori(a, b) as quad:
            for i in range(DEPTH):
                body(Tile(quad, i, **kind))

    straight(0, search=True)
    loop(1, SEARCH, search=True)
    straight(SETTLE, settle=True)
    straight(SPREAD, spread=True)
    loop(SPREAD + 1, SPREAD_END, spread=True)
    for quad in range(SPREAD_END, SWITCH + 1):
        straight(quad)
    loop(SWITCH + 1, LAST_QUAD, unique=True)
    straight(LAST_QUAD)


def experts(nc, A, logits, h2_d, xn2_d, xc_d, xu_d, out):
    ctx = ExitStack()
    with ctx:
        def sb(name, shape, dt=F32):
            return ctx.enter_context(nc.sbuf_tensor(name, shape, dt))

        def ps(name):
            return ctx.enter_context(nc.psum_tensor(name, [P, 512], F32))

        def sem(name):
            return ctx.enter_context(nc.semaphore(name))

        def sems(name, n=DEPTH):
            return [sem(f"{name}{i}") for i in range(n)]

        consts = sb("route_consts", [P, CWIDTH])
        C, at = {}, 0
        for name, n in CONSTS.items():
            C[name] = consts[:, at:at + n]
            at += n
        before = sb("before", [P, P])
        ones = sb("ones", [P, P])
        eye = sb("eye", [P, P])
        z = sb("z", [P, COLS, 2, NX])
        ez = sb("ez", [P, COLS, 2, NX])
        mx = sb("mx", [P, COLS, 2])
        total = sb("total", [P, COLS, 2])
        pmax = sb("pmax", [P, COLS, 2])
        OH = sb("OH", [P, 2, NX, COLS])
        key = sb("key", [P, NX, COLS])
        T = sb("T", [P, NX])
        cand = sb("cand", [P, NX])
        step = sb("step", [P, 1])
        gain = sb("gain", [P, NX])
        part = sb("part", [P, NX])
        need = sb("need", [P, NX])
        flag = sb("flag", [P, NX, COLS])
        tie = sb("tie", [P, NX, COLS])
        run_ = sb("run", [P, NX, COLS])
        rk = sb("rk", [P, NX, COLS])
        posf = sb("posf", [P, COLS])
        drop = sb("drop", [P, COLS])
        more = sb("more", [P, NX, KTH])
        nt = sb("nt", [P, NX])
        first = sb("first", [P, NX])
        first_row = sb("first_row", [P, NX])
        tcmp = sb("tcmp", [P, TILES, NX - 1])
        tex = sb("tex", [P, TILES])
        pos = sb("pos", [P, 2, COLS], U32)
        meta = sb("meta", [P, 2, COLS, 2])
        wrow = sb("wrow", [P, TILES], U32)
        tok = sb("tok", [P, 4, TT, RC])
        idx = sb("idx", [P, 4, TT], U32)
        widx = [sb(f"widx{i}", [P, 1], U32) for i in range(DEPTH)]
        ids = [sb(f"ids{i}", [P, ROWS // P], U32) for i in range(DEPTH)]
        W = [sb(f"W{i}", [P, WCOLS]) for i in range(DEPTH)]
        X = [sb(f"X{i}", [P, ROWS // P, RC]) for i in range(DEPTH)]
        XT = [sb(f"XT{i}", [KC, 2, ROWS]) for i in range(2)]
        Gl = [sb(f"Gl{i}", [P, FC, ROWS]) for i in range(2)]
        base = [sb(f"base_rows{i}", [P, ROWS // P, D]) for i in range(DEPTH)]
        Yb = sb("Yb", [P, ROWS // P, D])
        Y = [sb(f"Y{i}", [P, ROWS // P, D]) for i in range(DEPTH)]
        xt_ps, y_ps, cnt_ps, in_col, of_col = (ps(f"{x}_ps") for x in ("xt", "y", "cnt", "in_col", "of_col"))
        h_ps = [ps(f"h_ps{i}") for i in range(3)]

        r_in = sem("r_in")
        z_ready, e_ready = sem("z_ready"), sem("e_ready")
        v = sem("v_steps")
        part_ready, counted = sem("part_ready"), sem("counted")
        ranks_in, ranks_out = sem("ranks_in"), sem("ranks_out")
        placed = sem("placed")
        tok_in = sems("tok_in")
        idx_ready = sem("idx_ready")
        tok_out = sems("tok_out")
        apart = {e: sem(f"apart_x{i}") for i, e in enumerate((nc.sync.engine, nc.gpsimd.engine, nc.vector.engine))}

        def wait_apart(eng, semaphore, value):
            eng.wait_ge(semaphore, value)
            eng.sem_inc(apart[eng.engine], 1)

        made = 0

        def done(ins):
            nonlocal made
            made += 1
            ins.then_inc(v, 1)
            nc.vector.wait_ge(v, made)

        dve = nc.vector
        bc = lambda x, shape: x.broadcast_to(shape)
        by_e = lambda x: bc(x.rearrange("p (e a) -> p e a", a=1), [P, NX, COLS])
        by_c = lambda x: bc(x.rearrange("p (a c) -> p a c", a=1), [P, NX, COLS])
        over_e = lambda x: x.rearrange("p e c -> p c e")
        flat = lambda x: x.rearrange("p e c -> p (e c)")

        def column_ranks(k):
            n = NX * COLS

            def scan():
                dve.wait_ge(ranks_out, k + 1)
                done(dve.tensor_tensor_scan(flat(run_[:]), C["seg"], of_col[:, 0:n], 0.0, ALU.mult, ALU.add))

            return [scan,
                    lambda: done(dve.tensor_tensor(flat(rk[:]), flat(run_[:]), of_col[:, 0:n], ALU.subtract)),
                    lambda: done(dve.tensor_tensor(flat(rk[:]), flat(rk[:]), in_col[:, 0:n], ALU.add))]

        def place(kind, tile0, last_tile):
            cnt = run_[:, :, COLS - 1]
            n = last_tile - tile0
            tile = C["tile"][:, tile0:last_tile].rearrange("p (t a) -> p t a", a=1)
            mine = slice(tile0, last_tile)
            row0 = 0 if kind == 0 else CT
            return [
                lambda: done(dve.tensor_tensor(more[:], bc(cnt.rearrange("p (e a) -> p e a", a=1), [P, NX, KTH]),
                                               bc(C["kth"].rearrange("p (a k) -> p a k", a=1), [P, NX, KTH]), ALU.is_gt)),
                lambda: done(dve.tensor_reduce(nt[:], more[:], AX.X, ALU.add)),
                lambda: done(dve.tensor_tensor_scan(first[:], C["one"], nt[:], float(tile0), ALU.mult, ALU.add)),
                lambda: done(dve.tensor_tensor(first[:], first[:], nt[:], ALU.subtract)),
                lambda: done(dve.tensor_scalar(first_row[:], first[:], float(-row0), float(ROWS), ALU.add, ALU.mult)),
                lambda: done(dve.tensor_tensor(rk[:], rk[:], by_e(first_row[:]), ALU.add)),
                lambda: done(dve.tensor_tensor(rk[:], rk[:], OH[:, kind], ALU.mult)),
                lambda: done(dve.tensor_reduce(posf[:], over_e(rk[:]), AX.X, ALU.add)),
                lambda: done(dve.tensor_tensor(tcmp[:, 0:n, :], bc(tile, [P, n, NX - 1]),
                                               bc(first[:, 1:NX].rearrange("p (a e) -> p a e", a=1), [P, n, NX - 1]), ALU.is_ge)),
                lambda: done(dve.tensor_reduce(tex[:, mine], tcmp[:, 0:n, :], AX.X, ALU.add)),
                lambda: done(dve.tensor_scalar(tex[:, mine], tex[:, mine], float(NX * kind), float(P), ALU.add, ALU.mult)),
                lambda: done(dve.tensor_scalar(wrow[:, mine], tex[:, mine], C["lane"], None, ALU.add))]

        with nc.Block() as block:
            @block.sync
            def _(sp):
                sp.dma_start(consts[:], A["rconsts"]).then_inc(r_in, 16)
                sp.dma_start(before[:], A["before"]).then_inc(r_in, 16)
                sp.dma_start(eye[:], A["ident"]).then_inc(r_in, 16)

                def load(buf, n, quad):
                    if not isinstance(quad, int):
                        wait_apart(sp, tok_out[buf], quad * (16 * TT))
                    for src, c in ((xn2_d, 0), (h2_d, D + 2)):
                        sp.dma_start(tok[:, buf, 0:2, c:c + D], src[n, 0:2 * P, :].rearrange("(t p) d -> p t d", p=P)).then_inc(tok_in[buf], 16)
                        sp.dma_start(tok[0:TLEN[2], buf, 2, c:c + D], src[n, 2 * P:S, :]).then_inc(tok_in[buf], 16)

                for i in range(4):
                    load(i, i, 0)
                with sp.Fori(1, B // 4) as quad:
                    for i in range(4):
                        load(i, quad * 4 + i, quad)

            @block.gpsimd
            def _(pool):
                pool.wait_ge(placed, 1)

                def send(buf, n, quad):
                    if not isinstance(quad, int):
                        wait_apart(pool, tok_out[buf], quad * (16 * TT))
                    pool.tensor_copy(idx[:, buf, :], pos[:, 0, bass.ds(n * TT, TT)])
                    pool.tensor_copy(tok[:, buf, :, D:D + 2], meta[:, 0, bass.ds(n * TT, TT), :]).then_inc(idx_ready, 1)
                    wait_apart(pool, idx_ready, n + 1)
                    wait_apart(pool, tok_in[buf], quad * 64 + 64)
                    for k in range(TT):
                        r = slice(0, TLEN[k])
                        pool.indirect_dma_start(xc_d[:, :], bass.IndirectOffsetOnAxis(idx[r, buf, k:k + 1], 0), tok[r, buf, k, :],
                                                None, bounds_check=CT * ROWS - 1, oob_is_err=False).then_inc(tok_out[buf], 16)

                for i in range(4):
                    send(i, i, 0)
                with pool.Fori(1, B // 4) as quad:
                    for i in range(4):
                        send(i, quad * 4 + i, quad)
                for s in tok_out:
                    pool.wait_ge(s, B // 4 * 16 * TT)

            @block.scalar
            def _(act):
                nc.scalar.wait_ge(z_ready, 1)
                nc.scalar.activation(ez[:], z[:], ACT.Exp).then_inc(e_ready, 1)

            @block.tensor
            def _(pe):
                pe.wait_ge(r_in, 48)
                pe.wait_ge(ranks_in, 1)
                pe.matmul(in_col[:, 0:NX * COLS], before[:], flat(OH[:, 0]), start=True, stop=True)
                pe.matmul(of_col[:, 0:NX * COLS], ones[:], flat(OH[:, 0]), start=True, stop=True).then_inc(ranks_out, 1)

            @block.vector
            def _(dve):
                last = lambda x: bc(x.rearrange("p c (s a) -> p c s a", a=1), [P, COLS, 2, NX])
                order = bc(C["rank"].rearrange("p (a b e) -> p a b e", a=1, b=1), [P, COLS, 2, NX])
                for x, value in ((ones, 1.0), (T, 0.0), (step, 1.0)):
                    done(dve.memset(x[:], value))
                for x in base:
                    done(dve.memset(x[:], 0.0))
                dve.wait_ge(r_in, 48)
                lg = logits[:].rearrange("p b t (s e) -> p (b t) s e", s=2)
                done(dve.tensor_reduce(mx[:], lg, AX.X, ALU.max))
                dve.tensor_tensor(z[:], lg, last(mx), ALU.subtract).then_inc(z_ready, 1)
                dve.wait_ge(e_ready, 1)
                done(dve.tensor_reduce(total[:], ez[:], AX.X, ALU.add))
                done(dve.reciprocal(mx[:], total[:]))
                done(dve.tensor_tensor(ez[:], ez[:], last(mx), ALU.mult))
                done(dve.tensor_reduce(pmax[:], ez[:], AX.X, ALU.max))
                done(dve.tensor_tensor(z[:], ez[:], last(pmax), ALU.is_equal))
                done(dve.tensor_tensor(z[:], z[:], order, ALU.mult))
                done(dve.tensor_reduce(total[:], z[:], AX.X, ALU.max))
                done(dve.tensor_tensor(OH[:].rearrange("p s e c -> p c s e"), last(total), order, ALU.is_equal))
                done(dve.tensor_tensor(OH[:, 0], OH[:, 0], by_c(C["valid"]), ALU.mult))
                dve.sem_inc(ranks_in, 1)
                done(dve.tensor_tensor(OH[:, 1], OH[:, 1], by_c(C["valid"]), ALU.mult))
                done(dve.tensor_tensor(key[:], OH[:, 0], by_c(pmax[:, :, 0]), ALU.mult))
                done(dve.reciprocal(mx[:], pmax[:]))
                done(dve.tensor_tensor(meta[:, :, :, 0].rearrange("p s c -> p c s"), pmax[:], mx[:], ALU.mult))
                for kind in range(2):
                    done(dve.tensor_copy(meta[:, kind, :, 1], C["ids"]))
                for f in column_ranks(0) + place(0, 0, CT):
                    f()
                done(dve.tensor_copy(pos[:, 0, :], posf[:]))
                dve.sem_inc(placed, 1)

        w_in = sems("w_in")
        rows_in = sems("rows_in")
        widx_ready = sem("widx_ready")
        ids_ready = sem("ids_ready")
        base_in = sems("base_in")
        xt_filled, xt_ready = sem("xt_filled"), sem("xt_ready")
        h_filled, g_ready = sem("h_filled"), sem("g_ready")
        y_filled, yb_ready, y_ready = sem("y_filled"), sem("yb_ready"), sem("y_ready")
        y_out = sems("y_out")
        spread_in = sems("spread_in")
        spread_out = sems("spread_out")
        spread_ready = sem("spread_ready")
        block = ctx.enter_context(nc.Block())

        def spread_images(t):
            for u in range(2):
                k = 2 * t.i + u
                yield (t.quad - SPREAD) * (2 * DEPTH) + k, k % 4, (t.quad - SPREAD) * 2 + k // 4

        out_rows = out.rearrange("b s d -> (b s) d")
        unique_rows = (TILES - CT) * ROWS

        @block.sync
        def _(sp):
            def body(t):
                if t.spread:
                    for n, buf, use in spread_images(t):
                        if not (isinstance(use, int) and use == 0):
                            wait_apart(sp, spread_out[buf], use * (16 * TT))
                        sp.dma_start(tok[:, buf, 0:2, 0:D], xn2_d[n, 0:2 * P, :].rearrange("(t p) d -> p t d", p=P)).then_inc(spread_in[buf], 16)
                        sp.dma_start(tok[0:TLEN[2], buf, 2, 0:D], xn2_d[n, 2 * P:S, :]).then_inc(spread_in[buf], 16)
                if t.at_least(DEPTH):
                    wait_apart(sp, y_ready, t.n - (DEPTH - 1))
                if t.unique:
                    if t.number == CT:
                        for e in spread_out:
                            sp.wait_ge(e, B // 4 * 16 * TT)
                    sp.dma_start(X[t.i][:, :, 0:RU], xu_d[bass.ds((t.n - CT) * ROWS, ROWS), :].rearrange("(t p) d -> p t d", p=P)
                                 ).then_inc(rows_in[t.i], 16)
                else:
                    sp.dma_start(X[t.i][:], xc_d[bass.ds(t.n * ROWS, ROWS), :].rearrange("(t p) d -> p t d", p=P)).then_inc(rows_in[t.i], 16)

            tiles(sp, body)

        @block.gpsimd
        def _(pool):
            def send(t):
                for k in range(ROWS // P):
                    pool.indirect_dma_start(out_rows, bass.IndirectOffsetOnAxis(ids[t.i][:, k:k + 1], 0), Y[t.i][:, k, :],
                                            None, bounds_check=N - 1, oob_is_err=False).then_inc(y_out[t.i], 16)

            def numbers(t):
                if t.at_least(DEPTH):
                    wait_apart(pool, y_out[t.i], t.quad * 32)
                wait_apart(pool, rows_in[t.i], t.quad * 16 + 16)
                pool.tensor_copy(ids[t.i][:], X[t.i][:, :, D + 1]).then_inc(ids_ready, 1)
                if t.unique:
                    wait_apart(pool, ids_ready, t.n + 1)
                    if t.number == CT:
                        wait_apart(pool, y_ready, CT)
                        send(Tile((CT - 1) // DEPTH, (CT - 1) % DEPTH))
                        for i, e in enumerate(y_out):
                            pool.wait_ge(e, len(range(i, CT, DEPTH)) * 32)
                    for k in range(ROWS // P):
                        pool.indirect_dma_start(base[t.i][:, k, :], None, out_rows, bass.IndirectOffsetOnAxis(ids[t.i][:, k:k + 1], 0),
                                                bounds_check=N - 1, oob_is_err=False).then_inc(base_in[t.i], 16)

            def spread(t):
                for n, buf, use in spread_images(t):
                    if not (isinstance(use, int) and use == 0):
                        wait_apart(pool, spread_out[buf], use * (16 * TT))
                    pool.tensor_copy(idx[:, buf, :], pos[:, 1, bass.ds(n * TT, TT)])
                    pool.tensor_copy(tok[:, buf, :, D:D + 2], meta[:, 1, bass.ds(n * TT, TT), :]).then_inc(spread_ready, 1)
                    wait_apart(pool, spread_ready, n + 1)
                    wait_apart(pool, spread_in[buf], use * 32 + 32)
                    for k in range(TT):
                        r = slice(0, TLEN[k])
                        pool.indirect_dma_start(xu_d[:, :], bass.IndirectOffsetOnAxis(idx[r, buf, k:k + 1], 0), tok[r, buf, k, 0:RU],
                                                None, bounds_check=unique_rows - 1, oob_is_err=False).then_inc(spread_out[buf], 16)

            def body(t):
                if t.at_least(DEPTH):
                    wait_apart(pool, y_ready, t.n - (DEPTH - 1))
                pool.tensor_copy(widx[t.i][:], wrow[:, bass.ds(t.n, 1)]).then_inc(widx_ready, 1)
                wait_apart(pool, widx_ready, t.n + 1)
                pool.indirect_dma_start(W[t.i][:, :], None, A["experts"], bass.IndirectOffsetOnAxis(widx[t.i][:, 0:1], 0)).then_inc(w_in[t.i], 16)
                if t.at_least(DEPTH) and t.number != CT - 1 + DEPTH:
                    send(Tile(t.quad - 1, t.i))
                if t.at_least(2):
                    numbers(t.before(2))
                if t.number == SPREAD * DEPTH - 1:
                    pool.wait_ge(placed, 2)
                if t.spread:
                    spread(t)

            tiles(pool, body)
            for i in (2, 3):
                numbers(Tile(LAST_QUAD, i))
            for i in range(DEPTH):
                wait_apart(pool, y_ready, TILES - DEPTH + i + 1)
                send(Tile(LAST_QUAD, i))
            for e in y_out:
                pool.wait_ge(e, 32 * (LAST_QUAD + 1))

        @block.tensor
        def _(pe):
            def turn(t):
                pe.wait_ge(rows_in[t.i], t.quad * 16 + 16)
                if t.at_least(1):
                    pe.wait_ge(xt_ready, t.n)
                for c in range(2):
                    for k in range(ROWS // P):
                        mm = pe.transpose(xt_ps[0:KC, c * ROWS + k * P:c * ROWS + (k + 1) * P],
                                          X[t.i][:, k, c * KC:(c + 1) * KC], eye[:])
                mm.then_inc(xt_filled, 1)

            def up(t, chunks):
                for f in chunks:
                    if not (t.number == 0 and f < 3):
                        pe.wait_ge(g_ready, t.n * FC + (f - 2))
                    for c in range(2):
                        mm = pe.matmul(h_ps[f % 3][:, 0:ROWS], W[t.i][0:KC, c * FF + f * P:c * FF + (f + 1) * P],
                                       XT[t.par][:, c, :], start=(c == 0), stop=(c == 1))
                    mm.then_inc(h_filled, 1)

            def down(t):
                pe.wait_ge(g_ready, t.n * FC + FC)
                if t.at_least(1):
                    pe.wait_ge(y_ready, t.n)
                for k in range(ROWS // P):
                    for f in range(FC):
                        mm = pe.matmul(y_ps[:, k * D:(k + 1) * D], Gl[t.par][:, f, k * P:(k + 1) * P],
                                       W[t.i][:, W2O + f * D:W2O + (f + 1) * D], start=(f == 0), stop=(f == FC - 1))
                mm.then_inc(y_filled, 1)

            def ranks(k, src):
                pe.wait_ge(ranks_in, k + 1)
                pe.matmul(in_col[:, 0:NX * COLS], before[:], flat(src), start=True, stop=True)
                pe.matmul(of_col[:, 0:NX * COLS], ones[:], flat(src), start=True, stop=True).then_inc(ranks_out, 1)

            def count(n):
                pe.wait_ge(part_ready, n + 1)
                pe.matmul(cnt_ps[:, 0:NX], ones[:], part[:], start=True, stop=True).then_inc(counted, 1)

            def body(t):
                if t.number == 0:
                    turn(t)
                if t.number != TILES - 1:
                    turn(t.next())
                pe.wait_ge(w_in[t.i], t.quad * 16 + 16)
                pe.wait_ge(xt_ready, t.n + 1)
                up(t, range(3))
                if t.search or t.number == SETTLE * DEPTH:
                    count(t.n * 2)
                up(t, range(3, FC))
                if t.at_least(1):
                    down(t.before(1))
                if t.search:
                    count(t.n * 2 + 1)
                if t.number == SETTLE * DEPTH:
                    ranks(1, tie)
                if t.number == SETTLE * DEPTH + 1:
                    ranks(2, OH[:, 1])
                if t.number == TILES - 1:
                    down(t)

            tiles(pe, body)

        @block.scalar
        def _(act):
            act = nc.scalar

            def body(t):
                act.wait_ge(w_in[t.i], t.quad * 16 + 16)
                if t.at_least(2):
                    act.wait_ge(y_filled, t.n - 1)
                for f in range(FC):
                    act.wait_ge(h_filled, t.n * FC + f + 1)
                    act.activation(Gl[t.par][:, f, :], h_ps[f % 3][:, 0:ROWS], ACT.Gelu,
                                   bias=W[t.i][:, B1O + f:B1O + f + 1]).then_inc(g_ready, 1)

            tiles(act, body)

        @block.vector
        def _(dve):
            nonlocal made

            def turned(t):
                dve.wait_ge(xt_filled, t.n + 1)
                if t.at_least(2):
                    dve.wait_ge(h_filled, (t.n - 1) * FC)
                dve.tensor_copy(XT[t.par][:], xt_ps[0:KC, :].rearrange("p (c t) -> p c t", c=2)).then_inc(xt_ready, 1)

            def finish(t):
                dve.wait_ge(y_filled, t.n + 1)
                b2 = W[t.i][:, B2O:B2O + D].rearrange("p (a d) -> p a d", a=1).broadcast_to([P, ROWS // P, D])
                dve.tensor_tensor(Yb[:], y_ps[:, 0:ROWS // P * D].rearrange("p (t d) -> p t d", d=D), b2, ALU.add).then_inc(yb_ready, 1)
                dve.wait_ge(ids_ready, t.n + 1)
                if t.at_least(DEPTH):
                    dve.wait_ge(y_out[t.i], t.quad * 32)
                if t.unique:
                    first = SWITCH + (t.i < CT % DEPTH)
                    dve.wait_ge(base_in[t.i], (t.quad - first) * 32 + 32)
                dve.wait_ge(yb_ready, t.n + 1)
                for k in range(ROWS // P):
                    more_ = base[t.i][:, k, :] if t.unique else X[t.i][:, k, D + 2:RC]
                    ins = dve.scalar_tensor_tensor(Y[t.i][:, k, :], Yb[:, k, :], X[t.i][:, k, D:D + 1], more_, ALU.mult, ALU.add)
                ins.then_inc(y_ready, 1)

            start = made

            def test(k, step0):
                dve.tensor_scalar(cand[:], T[:], step[:, 0:1], None, ALU.add).then_inc(v, 1)
                dve.wait_ge(v, step0 + 1)
                dve.tensor_tensor(flag[:], key[:], by_e(cand[:]), ALU.is_ge).then_inc(v, 1)
                dve.wait_ge(v, step0 + 2)
                dve.tensor_reduce(part[:], flag[:], AX.X, ALU.add).then_inc(part_ready, 1)

            def take(k, step0):
                dve.wait_ge(counted, k + 1)
                dve.tensor_scalar(gain[:], cnt_ps[:, 0:NX], float(CAP), step[:, 0:1], ALU.is_ge, ALU.mult).then_inc(v, 1)
                dve.wait_ge(v, step0 + 3)
                dve.tensor_scalar(step[:], step[:], 0.5, None, ALU.mult).then_inc(v, 1)
                dve.tensor_tensor(T[:], T[:], gain[:], ALU.add).then_inc(v, 1)
                dve.wait_ge(v, step0 + 5)

            def ties():
                done(dve.tensor_tensor(flag[:], key[:], by_e(T[:]), ALU.is_gt))
                dve.tensor_reduce(part[:], flag[:], AX.X, ALU.add).then_inc(part_ready, 1)
                done(dve.tensor_tensor(tie[:], key[:], by_e(T[:]), ALU.is_equal))
                done(dve.tensor_tensor(tie[:], tie[:], OH[:, 0], ALU.mult))
                dve.sem_inc(ranks_in, 1)

            def drops():
                dve.wait_ge(counted, 2 * DEPTH * SEARCH + 1)
                done(dve.tensor_scalar(need[:], cnt_ps[:, 0:NX], -1.0, float(CAP), ALU.mult, ALU.add))
                for f in column_ranks(1):
                    f()
                done(dve.tensor_tensor(rk[:], rk[:], by_e(need[:]), ALU.is_ge))
                done(dve.tensor_tensor(rk[:], rk[:], tie[:], ALU.mult))
                done(dve.tensor_tensor(flag[:], key[:], by_e(T[:]), ALU.is_lt))
                done(dve.tensor_tensor(flag[:], flag[:], OH[:, 0], ALU.mult))
                done(dve.tensor_tensor(flag[:], flag[:], rk[:], ALU.add))
                done(dve.tensor_reduce(drop[:], over_e(flag[:]), AX.X, ALU.add))
                done(dve.tensor_tensor(OH[:, 1], OH[:, 1], by_c(drop[:]), ALU.mult))
                dve.sem_inc(ranks_in, 1)

            unique_place = column_ranks(2) + place(1, CT, TILES) + [
                lambda: done(dve.tensor_scalar(drop[:], drop[:], -float(unique_rows), float(unique_rows), ALU.mult, ALU.add)),
                lambda: done(dve.tensor_tensor(pos[:, 1, :], posf[:], drop[:], ALU.add)),
                lambda: dve.sem_inc(placed, 1)]

            def body(t):
                nonlocal made
                if t.number == 0:
                    turned(t)
                if t.number != TILES - 1:
                    turned(t.next())
                if t.search:
                    if t.number != 0:
                        take(t.n * 2 - 1, t.n * 10 + (start - 5))
                    test(t.n * 2, t.n * 10 + start)
                    take(t.n * 2, t.n * 10 + start)
                    test(t.n * 2 + 1, t.n * 10 + (start + 5))
                if t.number == SETTLE * DEPTH:
                    take(t.n * 2 - 1, t.n * 10 + (start - 5))
                    made = start + 10 * t.n
                    ties()
                if t.number == SETTLE * DEPTH + 1:
                    drops()
                if t.number == SETTLE * DEPTH + 2:
                    for f in unique_place[:8]:
                        f()
                if t.number == SETTLE * DEPTH + 3:
                    for f in unique_place[8:]:
                        f()
                if t.at_least(1):
                    finish(t.before(1))
                if t.number == TILES - 1:
                    finish(t)

            tiles(dve, body)


def build(nc, A, out):
    ctx = ExitStack()
    with ctx:
        def sb(name, shape, dt=F32):
            return ctx.enter_context(nc.sbuf_tensor(name, shape, dt))

        logits = sb("logits", [P, B, TT, NE])
        h2_d = nc.dram_tensor("h2_d", [B, S, D], F32).ap()
        xn2_d = nc.dram_tensor("xn2_d", [B, S, D], F32).ap()
        xc_d = nc.dram_tensor("xc_d", [CT * ROWS, RC], F32).ap()
        xu_d = nc.dram_tensor("xu_d", [(TILES - CT) * ROWS, RU], F32).ap()
        attention(nc, A, logits, h2_d, xn2_d, xc_d, xu_d)
        experts(nc, A, logits, h2_d, xn2_d, xc_d, xu_d, out)
    return nc


IN_NAMES = ["xT", "txt", "ident", "masks", "cosw", "sinw", "base", "biasb", "w_emb", "w_qkv", "w_o", "w_r", "rconsts", "before", "experts"]


def layout(I):
    a = {k: np.asarray(v) for k, v in I.items()}
    side, pp = 14, 16
    x = a["x"].reshape(B, side, pp, side, pp, 3).transpose(0, 5, 2, 4, 1, 3).reshape(B, EC, P, NPATCH)
    xT = np.zeros((B, P, EC, NPATCH + 1), np.float32)
    xT[:, :, :, 1:] = x.transpose(0, 2, 1, 3)
    o = {"xT": xT, "txt": a["txt"]}
    o["ident"] = np.eye(P, dtype=np.float32)
    i = np.arange(P)
    later = np.where(i[None, :] > i[:, None], BIG, 0.0)
    o["masks"] = np.stack([later, later.T], 1).astype(np.float32)
    inv = (1.0 / np.float32(10000.0) ** (np.arange(D // 2, dtype=np.float32) * np.float32(2.0) / np.float32(D))).astype(np.float32)
    ang = (np.arange(TT * P, dtype=np.float32)[:, None] * inv[None, :]).astype(np.float32)
    cos = np.repeat(np.cos(ang).astype(np.float32), 2, 1)
    sin = np.repeat(np.sin(ang).astype(np.float32), 2, 1) * np.tile(np.float32([-1, 1]), D // 2)
    tiles = lambda t: np.ascontiguousarray(np.tile(t, (1, 2)).reshape(TT, P, 2 * D).transpose(1, 0, 2)).astype(np.float32)
    o["cosw"], o["sinw"] = tiles(cos), tiles(sin)
    pos = np.zeros((2 * P, D), np.float32)
    pos[:NPATCH + 1] = a["L0_tok_pos_embed"][0]
    bias = np.tile(a["L0_tok_b"], (2 * P, 1))
    bias[0] = a["L0_tok_cls_token"][0, 0]
    o["base"] = np.ascontiguousarray(pos.reshape(2, P, D).transpose(1, 0, 2))
    o["biasb"] = np.ascontiguousarray(bias.reshape(2, P, D).transpose(1, 0, 2))
    o["w_emb"] = np.ascontiguousarray(a["L0_tok_W"].T.reshape(EC, P, D).transpose(1, 0, 2))

    def chunks(w, bias):
        c = np.zeros((KC + 1, 2, w.shape[1]), np.float32)
        c[:KC, 0], c[:KC, 1], c[KC, 0] = w[:KC], w[KC:], bias
        return c

    o["w_qkv"] = chunks(np.concatenate([a[f"L0_attn_W{k}"] for k in "qkv"], 1), np.concatenate([a[f"L0_attn_b{k}"] for k in "qkv"]))
    o["w_o"] = chunks(a["L0_attn_Wo"], a["L0_attn_bo"])
    o["w_r"] = chunks(np.concatenate([a["L0_ffn_Wsc"], a["L0_ffn_Wsu"]], 1), np.concatenate([a["L0_ffn_bsc"], a["L0_ffn_bsu"]]))
    lane, col = np.arange(P)[:, None], np.arange(COLS)[None, :]
    tok = P * (col % TT) + lane
    c = dict(valid=(tok < S), ids=(col // TT * S + tok), seg=np.tile(col > 0, (P, NX)), rank=np.tile(NX - np.arange(NX), (P, 1)),
             kth=np.tile(ROWS * np.arange(KTH), (P, 1)), tile=np.tile(np.arange(TILES), (P, 1)), lane=lane, one=np.ones((P, NX)))
    o["rconsts"] = np.concatenate([c[k].astype(np.float32) for k in CONSTS], 1)
    o["before"] = (lane < np.arange(P)[None, :]).astype(np.float32)
    w = np.zeros((2, NX, P, WCOLS), np.float32)
    for i, kind in enumerate("cu"):
        w[i, :, :KC, W1O:W2O] = a[f"L0_ffn_W1{kind}"].reshape(NX, 2, KC, FF).transpose(0, 2, 1, 3).reshape(NX, KC, 2 * FF)
        w[i, :, :, W2O:B1O] = a[f"L0_ffn_W2{kind}"].reshape(NX, FC, P, D).transpose(0, 2, 1, 3).reshape(NX, P, FC * D)
        w[i, :, :, B1O:B2O] = a[f"L0_ffn_b1{kind}"].reshape(NX, FC, P).transpose(0, 2, 1)
        w[i, :, :, B2O:] = a[f"L0_ffn_b2{kind}"][:, None, :]
    o["experts"] = w.reshape(2 * NX * P, WCOLS)
    return o


def kernel(**inputs):
    import concourse.bacc as _bacc
    from concourse.bass_utils import run_bass_kernel_spmd as _run

    nc = _bacc.Bacc("TRN2", target_bir_lowering=False, num_devices=1)
    arrays, aps = {}, {}
    for name, array in layout(inputs).items():
        arrays[f"in_{name}_dram"] = np.ascontiguousarray(array)
        aps[name] = nc.dram_tensor(f"in_{name}_dram", array.shape, mybir.dt.from_np(array.dtype), kind="ExternalInput").ap()
    out = nc.dram_tensor("out_0_dram", (B, S, D), F32, kind="ExternalOutput").ap()
    build(nc, aps, out)
    r = _run(nc, [arrays], core_ids=[0])
    return r.results[0]["out_0_dram"]
```

```python
from contextlib import ExitStack

import numpy as np
import concourse.bass as bass
from concourse import mybir

F32 = mybir.dt.float32
BF16 = mybir.dt.bfloat16
F32R = mybir.dt.float32r
U32 = mybir.dt.uint32
ALU = mybir.AluOpType
ACT = mybir.ActivationFunctionType
AX = mybir.AxisListType

P = 128
B = 32
D = 192
NPATCH, NTXT = 196, 77
S = 1 + NPATCH + NTXT
HEADS, HD = 12, 16
GROUPS, GH = 3, 4
TT = 3
TOFF = [0, 128, 256]
TLEN = [128, 128, S - 256]
IMG1 = 1 + NPATCH - 128
KC = 96
EC = 6
EPS = 1e-5
BIG = -1e30
PARTS = 6
KS_ROWS = PARTS * HD
KROWS = KS_ROWS + 3
SCALE = 0.25
Q2 = S - 32
NE = 8

FREE = 1

LOOPED = B - 4

FF = 768
NX = 4
N = B * S
CAP = N // NX
COLS = -(-N // P)
HALF = -(-COLS // 2)
CC = 3
CHUNKS = COLS // CC
LASTN = N - (COLS - 1) * P
assert CHUNKS * CC == COLS and CHUNKS % 4 == 3
ROWS = 256
CT = (N + NX * (ROWS - 1)) // ROWS
UT = (N - CAP + NX * (ROWS - 1)) // ROWS
DEPTH = 4
TILES = -(-(CT + UT) // DEPTH) * DEPTH
FC = FF // P
W1O, W2O, B1O, B2O = 0, 2 * FF, 2 * FF + FC * D, 2 * FF + FC * D + FC
WCOLS = B2O + D
RU, RC = D + 2, 2 * D + 2
NOWHERE = 2.0 ** 14
KTH = max(CT, UT) + 2
assert TILES - 2 * LOOPED <= 3 * (B - LOOPED)
CONSTS = dict(valid=COLS, ids=COLS, seg=NX * COLS, rank=NX, kth=KTH, tile=TILES, lane=1, one=NX)
CWIDTH = sum(CONSTS.values())

STEADY = ["mq0", "mq1", "mq2", "xnT0", "xnT1", "qk0", "v0", "at0", "at1", "mT", "qk1", "o0", "o1", "v1", "qk2", "v2",
          "emb0", "emb1", "x20", "x21", "t0", "t2", "t4", "t6"]
MID = {"mq0", "mq1", "mq2", "mT"}
AT = {"at0", "at1", "o0", "o1", "x20", "x21"}
NEW = {"emb0", "emb1"}
PRE = set(STEADY) - MID - AT - NEW
assert all(len(x) % 2 == 0 for x in (NEW, PRE, MID, AT))


class Batch:

    def __init__(self, half, par):
        self.half, self.par, self.n = half, par, half * 2 + par

    def next(self):
        return Batch(self.half + self.par, 1 - self.par)


class Turn:

    def __init__(self, at, mid, pre, new):
        self.at, self.mid, self.pre, self.new = at, mid, pre, new
        self.uses = [u for u in STEADY if (at and u in AT) or (mid and u in MID) or (pre and u in PRE) or (new and u in NEW)]
        self.ats = at.n if at else 0
        self.mids = mid.n if mid else at.n + 1 if at else 0
        self.pres = pre.n if pre else B if at else 0
        self.news = new.n if new else B

    def in_max_banks(self, u=None):
        return self.mids * (HEADS // 2) + self.pres * 2 + (0 if u is None else (HEADS // 2 if self.mid else 0) + u // 4)

    def bank(self, use):
        return self.uses.index(use) % 2

    def latest(self, *uses):
        return list({self.bank(u): u for u in uses}.values())

    def before(self, use=None):
        k = self.uses.index(use) // 2 if use else 0
        return self.ats * (len(AT) // 2) + self.mids * (len(MID) // 2) + self.pres * (len(PRE) // 2) + self.news * (len(NEW) // 2) + k


def rounds(eng, body):
    b = [Batch(n // 2, n % 2) for n in range(B)] + [None] * 3
    body(Turn(None, None, None, b[0]))
    body(Turn(None, None, b[0], b[1]))
    body(Turn(None, b[0], b[1], b[2]))
    with eng.Fori(0, B // 2 - 2) as half:
        for par in range(2):
            at = Batch(half, par)
            body(Turn(at, at.next(), at.next().next(), at.next().next().next()))
    for n in range(B - 4, B):
        body(Turn(*b[n:n + 4]))


class Steps:

    def __init__(self, eng, sem, at, mid, pre):
        self.eng, self.sem, self.at, self.mid, self.pre = eng, sem, at, mid, pre

    def begin(self, turn):
        self.k, self.turn = 0, turn
        self.base = turn.ats * self.at + turn.mids * self.mid + turn.pres * self.pre

    def done(self, ins):
        ins.then_inc(self.sem, 1)
        self.k += 1
        return self.k

    def need(self, k):
        self.eng.wait_ge(self.sem, self.base + k)

    def end(self):
        t = self.turn
        assert self.k == bool(t.at) * self.at + bool(t.mid) * self.mid + bool(t.pre) * self.pre, self.k


def attention(nc, A, logits, h2_d, xn2_d, xc_d, xu_d):
    ctx = ExitStack()
    with ctx:
        def sb(name, shape, dt=F32):
            return ctx.enter_context(nc.sbuf_tensor(name, shape, dt))

        def ps(name, shape, dt=F32):
            return ctx.enter_context(nc.psum_tensor(name, shape, dt))

        def sem(name):
            return ctx.enter_context(nc.semaphore(name))

        ident = sb("ident", [P, P])
        identb = sb("identb", [P, P], BF16)
        masks = sb("masks_f", [P, 2, P])
        mask_qk = sb("mask_qk", [P, P], BF16)
        mask_kq = sb("mask_kq", [P, P], BF16)
        cosw = sb("cosw", [P, TT, 2 * D])
        sinw = sb("sinw", [P, TT, 2 * D])
        base = sb("base", [P, 2, D])
        biasb = sb("biasb", [P, 2, D])
        w_emb = sb("w_emb", [P, EC, D])
        w_qkv = sb("w_qkv", [KC + 1, 2, 3 * D])
        w_o = sb("w_o", [KC + 1, 2, D])
        w_r = sb("w_r", [KC + 1, 2, NE])
        xT = [sb(f"xT{i}", [P, EC, NPATCH + 1]) for i in range(2)]
        h = [sb(f"h{i}", [P, TT, D]) for i in range(2)]
        stat = sb("stat", [P, 2, TT, 6])
        mv = sb("mv", [P, 2, TT, 2])
        veps = sb("veps", [P, 2, TT])
        rstd = sb("rstd", [P, 2, TT])
        minus_half = sb("minus_half", [P, TT])
        xn = sb("xn", [P, TT, D])
        xnT = sb("xnT", [KC + 1, 2, S])
        ropeA = sb("ropeA", [P, TT, 2 * D])
        ropeB = sb("ropeB", [P, TT, 2 * D])
        rr = sb("rr", [P, TT, 2 * D])
        d1 = sb("d1", [P, TT, 2 * D])
        stk = sb("stk", [P, TT, 2 * HEADS, PARTS, HD], BF16)
        QS = [sb(f"QS{i}", [P, HEADS, S], BF16) for i in range(2)]
        KS = [sb(f"KS{i}", [P, HEADS, S], BF16) for i in range(2)]
        V = [sb(f"V{i}", [P, TT, HEADS, 32]) for i in range(2)]
        NM = 2 * HEADS + GROUPS
        nm3 = sb("nm3", [P, HEADS, 3])
        nm = sb("nm", [P, NM])
        nmd = sb("nmd", [P, NM])
        nmp = sb("nmp", [P, TT, HEADS, 3], BF16)
        mT = sb("mT", [3 * HEADS, TT, P], BF16)
        PT = [sb(f"PT{i}", [P, GH, 438]) for i in range(2)]
        Usb = sb("Usb", [P, GROUPS, S])
        rec = sb("rec", [P, TT, HEADS])
        att = sb("att", [P, TT, D])
        attT = sb("attT", [KC + 1, 2, S])
        h2 = [sb(f"hh{i}", [P, TT, D]) for i in range(2)]
        xn2 = [sb(f"xn2{i}", [P, TT, D]) for i in range(2)]
        xn2T = sb("xn2T", [KC + 1, 2, S])
        padding = sb("padding", [P, ROWS // P, RC])
        SP_ = [ps(f"scores{i}", [P, 512]) for i in range(3)]
        MP = [ps(f"maxs{i}", [P, 512]) for i in range(2)]
        UP = ps("attn", [P, 512])
        G = [ps(f"gen{i}", [P, 512]) for i in range(2)]
        Gb = [g[:, :].bitcast(BF16) for g in G]
        Mb = [m[:, :].bitcast(BF16) for m in MP]

        consts_in = sem("consts_in")
        consts_set = sem("consts_set")
        x_in = [sem(f"x_in{i}") for i in range(2)]
        txt_in = [sem(f"txt_in{i}") for i in range(2)]
        g_filled = [sem(f"g_filled{i}") for i in range(2)]
        g_emptied = [sem(f"g_emptied{i}") for i in range(2)]
        steps = sem("steps")
        xn_ready = sem("xn_ready")
        var_ready = [sem(f"var_ready{i}") for i in range(2)]
        veps_ready = [sem(f"veps_ready{i}") for i in range(2)]
        rstd_ready = [sem(f"rstd_ready{i}") for i in range(2)]
        rope_r = sem("rope_r")
        part0 = sem("part0")
        diff1 = sem("diff1")
        part1 = sem("part1")
        parts_ready = sem("parts_ready")
        m_filled = [sem(f"m_filled{i}") for i in range(2)]
        m_read = [sem(f"m_read{i}") for i in range(2)]
        nmax_ready = sem("nmax_ready")
        mrow_in = [sem(f"mrow_in{i}") for i in range(2)]
        s_filled = [sem(f"s_filled{i}") for i in range(3)]
        p_ready = sem("p_ready")
        u_filled = sem("u_filled")
        u_read = sem("u_read")
        ut_filled = sem("ut_filled")
        att_ready = sem("att_ready")
        r_filled, r_read = sem("r_filled"), sem("r_read")
        xn2_ready = sem("xn2_ready")
        h_saved = sem("h_saved")
        rows_out = [sem(f"rows_out{i}") for i in range(2)]
        padding_set, padded = sem("padding_set"), sem("padded")
        apart = {e: sem(f"apart_{i}") for i, e in enumerate((nc.sync.engine, nc.gpsimd.engine, nc.vector.engine, nc.tensor.engine))}

        loads = ((ident, "ident"), (masks, "masks"),
                 (cosw, "cosw"), (sinw, "sinw"), (base, "base"), (biasb, "biasb"), (w_emb, "w_emb"),
                 (w_qkv, "w_qkv"), (w_o, "w_o"), (w_r, "w_r"))
        n_set = 14
        block = ctx.enter_context(nc.Block())

        def wait_apart(eng, semaphore, value):
            eng.wait_ge(semaphore, value)
            eng.sem_inc(apart[eng.engine], 1)

        @block.sync
        def _(sp):
            for e in rows_out:
                sp.sem_inc(e, FREE)
            for dst, src in loads:
                sp.dma_start(dst[:], A[src]).then_inc(consts_in, 16)

            def load_x(b):
                sp.dma_start(xT[b.par][:], A["xT"][b.n]).then_inc(x_in[b.par], 16)

            def load_txt(b):
                sp.dma_start(h[b.par][IMG1:P, 1, :], A["txt"][b.n, 0:P - IMG1, :]).then_inc(txt_in[b.par], 16)
                sp.dma_start(h[b.par][0:TLEN[2], 2, :], A["txt"][b.n, P - IMG1:NTXT, :]).then_inc(txt_in[b.par], 16)

            def body(t):
                if not t.pre and not t.at:
                    for b in (t.new, t.new.next()):
                        load_x(b)
                        load_txt(b)
                    return
                if t.new and not (isinstance(t.new.n, int) and t.new.n == B - 1):
                    for e in g_emptied:
                        wait_apart(sp, e, t.before())
                    load_x(t.new.next())
                if t.mid and t.new:
                    wait_apart(sp, h_saved, t.mid.n + 1)
                    load_txt(t.new)
                if t.mid:
                    b = t.mid
                    wait_apart(sp, g_emptied[t.bank("mT")], t.before("mT") + 1)
                    for r in range(3):
                        row = QS[b.par][KS_ROWS + r:KS_ROWS + r + 1, :, :]
                        sp.dma_start(row[:, :, 0:2 * P], mT[r:3 * HEADS:3, 0:2, :].rearrange("h t q -> h (t q)")).then_inc(mrow_in[b.par], 16)
                        sp.dma_start(row[:, :, 2 * P:S],
                                     mT[r:3 * GROUPS:3, 2, :].rearrange("j (g q) -> j g q", g=GH)[:, :, 32 - TLEN[2]:32]
                                     ).then_inc(mrow_in[b.par], 16)
                if t.at:
                    b = t.at
                    for use in ("o0", "o1"):
                        wait_apart(sp, g_emptied[t.bank(use)], t.before(use) + 1)
                    out_ = rows_out[b.par]
                    sp.dma_start(h2_d[b.n, 0:2 * P, :].rearrange("(t p) d -> p t d", p=P), h2[b.par][:, 0:2, :]).then_inc(out_, 16)
                    sp.dma_start(h2_d[b.n, 2 * P:S, :], h2[b.par][0:TLEN[2], 2, :]).then_inc(out_, 16)
                    wait_apart(sp, xn2_ready, b.n + 1)
                    sp.dma_start(xn2_d[b.n, 0:2 * P, :].rearrange("(t p) d -> p t d", p=P), xn2[b.par][:, 0:2, :]).then_inc(out_, 16)
                    sp.dma_start(xn2_d[b.n, 2 * P:S, :], xn2[b.par][0:TLEN[2], 2, :]).then_inc(out_, 16)

            rounds(sp, body)
            for e in g_emptied:
                sp.wait_ge(e, B * len(STEADY) // 2)
            for p in range(2):
                sp.wait_ge(rows_out[p], 64 * (B // 2) + FREE)

        @block.tensor
        def _(pe):
            pe.wait_ge(consts_in, 16 * len(loads))
            pe.wait_ge(consts_set, n_set)

            def fill(t, use):
                pe.wait_ge(g_emptied[t.bank(use)], t.before(use))
                return t.bank(use)

            def have(t, uses, then):
                for use in t.latest(*uses):
                    if t.bank(use) != t.bank(then):
                        pe.wait_ge(g_emptied[t.bank(use)], t.before(use) + 1)

            def embed(t, k):
                b = t.new
                if k == 0:
                    pe.wait_ge(x_in[b.par], b.half * 16 + 16)
                g = fill(t, f"emb{k}")
                cols, m = (slice(0, P), P) if k == 0 else (slice(P, NPATCH + 1), IMG1)
                for c in range(EC):
                    mm = pe.matmul(G[g][0:m, 0:D], xT[b.par][:, c, cols], w_emb[:, c, :], start=(c == 0), stop=(c == EC - 1))
                mm.then_inc(g_filled[g], 1)

            def maxs(t, head):
                b, i = t.mid, head % 2
                if head == 0:
                    for e in g_emptied:
                        pe.wait_ge(e, t.before())
                    pe.wait_ge(m_read[1], t.in_max_banks() + FREE)
                pe.wait_ge(m_read[i], t.in_max_banks() + (head // 2 + FREE))
                q, k, r = QS[b.par], KS[b.par], slice(0, KS_ROWS)
                pe.matmul(MP[i][:, 0:P], q[r, head, 0:P], k[r, head, 0:P], start=True, stop=False, skip_group_check=True)
                pe.matmul(MP[i][:, 0:P], identb[:], mask_qk[:], start=False, stop=True, skip_group_check=True)
                pe.matmul(MP[i][:, P:3 * P], q[r, head, P:2 * P], k[r, head, 0:2 * P], start=True, stop=False, skip_group_check=True)
                pe.matmul(MP[i][:, 2 * P:3 * P], identb[:], mask_qk[:], start=False, stop=True, skip_group_check=True).then_inc(m_filled[i], 1)

            def maxs2(t, j):
                b = t.mid
                g = fill(t, f"mq{j}")
                q, k, r = QS[b.par], KS[b.par], slice(0, KS_ROWS)
                for i in range(GH):
                    head, rows = GH * j + i, slice(32 * i, 32 * i + 32)
                    pe.matmul(G[g][rows, 0:S], q[r, head, Q2:S], k[r, head, :], start=True, stop=False, skip_group_check=True)
                    mm = pe.matmul(G[g][rows, Q2:S], identb[0:32, 0:32], mask_qk[0:32, 0:32], start=False, stop=True,
                                   tile_position=(0, 32 * i), skip_group_check=True)
                mm.then_inc(g_filled[g], 1)

            def turn_tokens(t, src, use):
                c = int(use[-1])
                g = fill(t, use)
                for k in range(TT):
                    mm = pe.transpose(G[g][0:KC, TOFF[k]:TOFF[k] + TLEN[k]], src[0:TLEN[k], k, c * KC:(c + 1) * KC],
                                      ident[0:TLEN[k], 0:TLEN[k]])
                mm.then_inc(g_filled[g], 1)

            def turn_max(t):
                pe.wait_ge(nmax_ready, t.mid.n + 1)
                g = fill(t, "mT")
                pe.sem_inc(apart[pe.engine], 1)
                for k in range(TT):
                    mm = pe.transpose(Gb[g][0:3 * HEADS, k * P:(k + 1) * P], nmp[:, k].rearrange("p h r -> p (h r)"), identb[:])
                mm.then_inc(g_filled[g], 1)

            def project_in(t, *uses):
                for use in uses:
                    k, cols = int(use[-1]), slice(0, 2 * D) if use[0] == "q" else slice(2 * D, 3 * D)
                    tok = slice(TOFF[k], TOFF[k] + TLEN[k])
                    g = fill(t, use)
                    o = G[g][0:TLEN[k], 0:cols.stop - cols.start]
                    pe.matmul(o, xnT[:, 0, tok], w_qkv[:, 0, cols], start=True, stop=False)
                    pe.matmul(o, xnT[0:KC, 1, tok], w_qkv[0:KC, 1, cols], start=False, stop=True).then_inc(g_filled[g], 1)

            def turn_parts(t, u):
                if u == 0:
                    pe.wait_ge(parts_ready, t.pre.n * TT + TT)
                if u % 2:
                    i = u // 2 % 2
                    pe.wait_ge(m_read[i], t.in_max_banks(u) + FREE)
                    bank, filled = Mb[i], m_filled[i]
                else:
                    g = fill(t, f"t{u}")
                    bank, filled = Gb[g], g_filled[g]
                for i in range(3):
                    for k in range(TT):
                        mm = pe.transpose(bank[0:KS_ROWS, i * S + TOFF[k]:i * S + TOFF[k] + TLEN[k]],
                                          stk[0:TLEN[k], k, 3 * u + i, :, :].rearrange("p a d -> p (a d)"),
                                          identb[0:TLEN[k], 0:TLEN[k]])
                mm.then_inc(filled, 1)

            def scores(t, head):
                b, i = t.at, head % 3
                if head == 0:
                    pe.wait_ge(mrow_in[b.par], b.half * 96 + 96)
                if head == 0:
                    pe.wait_ge(r_read, b.n + FREE)
                if head < 3:
                    pe.wait_ge(p_ready, b.n * HEADS + FREE)
                else:
                    pe.wait_ge(p_ready, b.n * HEADS + head - 2 + FREE)
                q, k, s, n = QS[b.par], KS[b.par], SP_[i], TLEN[2]
                r = slice(0, KROWS)
                pe.matmul(s[:, 0:S], k[r, head, 0:P], q[r, head, :], start=True, stop=False, skip_group_check=True)
                pe.matmul(s[:, 0:P], identb[:], mask_kq[:], start=False, stop=True, skip_group_check=True)
                pe.matmul(s[:, S:S + 146], k[r, head, P:2 * P], q[r, head, P:S], start=True, stop=False, skip_group_check=True)
                pe.matmul(s[:, S:S + P], identb[:], mask_kq[:], start=False, stop=True, skip_group_check=True)
                pe.matmul(s[0:n, 420:438], k[r, head, 2 * P:S], q[r, head, 2 * P:S], start=True, stop=False, skip_group_check=True)
                pe.matmul(s[0:n, 420:438], identb[0:n, 0:n], mask_kq[0:n, 0:n], start=False, stop=True,
                          skip_group_check=True).then_inc(s_filled[i], 1)

            def values(t, j):
                b = t.at
                pt = PT[(3 * b.par + j) % 2]
                pe.wait_ge(p_ready, b.n * HEADS + GH * (j + 1) + FREE)
                pe.wait_ge(u_read, b.n * GROUPS + j + FREE)
                for k, (lo, n, at) in enumerate(((0, S, 0), (P, 146, S), (2 * P, TLEN[2], 420))):
                    for i in range(GH):
                        rows = TLEN[k]
                        mm = pe.matmul(UP[32 * i:32 * i + 32, lo:S], V[b.par][0:rows, k, GH * j + i, :],
                                       pt[0:rows, i, at:at + n], start=(k == 0), stop=(k == 2),
                                       tile_position=(0, 32 * i), skip_group_check=True)
                mm.then_inc(u_filled, 1)

            def turn_values(t, k):
                if k == 0:
                    pe.wait_ge(u_read, t.at.n * GROUPS + GROUPS + FREE)
                for j in range(GROUPS):
                    mm = pe.transpose(SP_[k][0:TLEN[k], j * P:(j + 1) * P], Usb[:, j, TOFF[k]:TOFF[k] + TLEN[k]], ident[:])
                mm.then_inc(ut_filled, 1)

            def project(t):
                have(t, ("at0", "at1"), "o0")
                for use, tiles in (("o0", (0, 1)), ("o1", (2,))):
                    g = fill(t, use)
                    for k in tiles:
                        tok = slice(TOFF[k], TOFF[k] + TLEN[k])
                        o = G[g][0:TLEN[k], (k % 2) * D:(k % 2) * D + D]
                        pe.matmul(o, attT[:, 0, tok], w_o[:, 0, :], start=True, stop=False)
                        mm = pe.matmul(o, attT[0:KC, 1, tok], w_o[0:KC, 1, :], start=False, stop=True)
                    mm.then_inc(g_filled[g], 1)

            def route(t):
                for use in ("x20", "x21"):
                    pe.wait_ge(g_emptied[t.bank(use)], t.before(use) + 1)
                pe.matmul(SP_[0][0:NE, 0:S], w_r[:, 0, :], xn2T[:, 0, :], start=True, stop=False)
                pe.matmul(SP_[0][0:NE, 0:S], w_r[0:KC, 1, :], xn2T[0:KC, 1, :], start=False, stop=True).then_inc(r_filled, 1)

            def body(t):
                for head in range(HEADS):
                    if t.at:
                        scores(t, head)
                    if t.mid:
                        maxs(t, head)
                        if head % GH == 3:
                            maxs2(t, head // GH)
                    if t.at and head % GH == 1 and head > GH:
                        values(t, head // GH - 1)
                if t.at:
                    values(t, GROUPS - 1)
                if t.pre:
                    pe.wait_ge(xn_ready, t.pre.n + 1)
                    turn_tokens(t, xn, "xnT0")
                    turn_tokens(t, xn, "xnT1")
                if t.at:
                    for k in range(TT):
                        turn_values(t, k)
                if t.pre:
                    have(t, ("xnT0", "xnT1"), "qk0")
                    project_in(t, "qk0", "v0")
                if t.at:
                    pe.wait_ge(att_ready, t.at.n * TT + TT)
                    turn_tokens(t, att, "at0")
                    turn_tokens(t, att, "at1")
                if t.mid:
                    turn_max(t)
                if t.pre:
                    project_in(t, "qk1")
                if t.at:
                    project(t)
                if t.pre:
                    project_in(t, "v1", "qk2", "v2")
                if t.new:
                    embed(t, 0)
                    embed(t, 1)
                if t.at:
                    pe.wait_ge(xn2_ready, t.at.n + 1)
                    turn_tokens(t, xn2[t.at.par], "x20")
                    turn_tokens(t, xn2[t.at.par], "x21")
                    if not t.pre:
                        route(t)
                if t.pre:
                    turn_parts(t, 0)
                    if t.at:
                        route(t)
                    for u in (1, 2, 3, 4, 6, 5, 7):
                        turn_parts(t, u)

            rounds(pe, body)

        def copy_parts(eng, t, u, bank):
            dst = (QS if u < 4 else KS)[t.pre.par][0:KS_ROWS, 3 * (u % 4):3 * (u % 4) + 3, :]
            src = bank[0:KS_ROWS, 0:3 * S].rearrange("p (h s) -> p h s", s=S)
            if eng is nc.scalar:
                return eng.activation(dst, src, ACT.Copy)
            return eng.tensor_copy(dst, src)

        @block.scalar
        def _(act):
            act = nc.scalar
            for e in (p_ready, u_read):
                act.sem_inc(e, FREE)

            def take(t, use):
                act.wait_ge(g_filled[t.bank(use)], t.before(use) + 1)
                return t.bank(use)

            def copy_tokens(t, use, dst):
                g, c = take(t, use), int(use[-1])
                act.activation(dst[0:KC, c, :], G[g][0:KC, 0:S], ACT.Copy).then_inc(g_emptied[g], 1)

            def pairs(t, k):
                act.wait_ge(rope_r, t.pre.n * TT + k + 1)
                n = TLEN[k]
                q = rr[0:n, k, 0:D].rearrange("p (h a d) -> p h a d", a=1, d=HD)
                kk = rr[0:n, k, D:2 * D].rearrange("p (h a d) -> p h a d", a=1, d=HD)
                act.activation(stk[0:n, k, 0:HEADS, 0:3, :], q.broadcast_to([n, HEADS, 3, HD]), ACT.Copy)
                act.activation(stk[0:n, k, HEADS:2 * HEADS, 0:4:3, :], kk.broadcast_to([n, HEADS, 2, HD]), ACT.Copy)
                act.activation(stk[0:n, k, HEADS:2 * HEADS, 5:6, :], kk, ACT.Copy).then_inc(part0, 1)

            def pairs1(t, k):
                act.wait_ge(diff1, t.pre.n * TT + k + 1)
                n = TLEN[k]
                q = d1[0:n, k, 0:D].rearrange("p (h a d) -> p h a d", a=1, d=HD)
                kk = d1[0:n, k, D:2 * D].rearrange("p (h a d) -> p h a d", a=1, d=HD)
                act.activation(stk[0:n, k, 0:HEADS, 3:5, :], q.broadcast_to([n, HEADS, 2, HD]), ACT.Copy)
                act.activation(stk[0:n, k, HEADS:2 * HEADS, 1:5:3, :], kk.broadcast_to([n, HEADS, 2, HD]), ACT.Copy).then_inc(part1, 1)

            def weights(t, j):
                b = t.at
                pt = PT[(3 * b.par + j) % 2]
                for i in range(GH):
                    head = GH * j + i
                    s, n = SP_[head % 3], TLEN[2]
                    act.wait_ge(s_filled[head % 3], b.n * (HEADS // 3) + head // 3 + 1)
                    act.activation(pt[0:n, i, 420:438], s[0:n, 420:438], ACT.Exp, scale=SCALE)
                    act.activation(pt[:, i, 0:420], s[:, 0:420], ACT.Exp, scale=SCALE).then_inc(p_ready, 1)

            def attended(t, j):
                act.wait_ge(u_filled, t.at.n * GROUPS + j + 1)
                act.activation(Usb[:, j, :], UP[:, 0:S], ACT.Copy).then_inc(u_read, 1)

            def values_out(t, k):
                g = take(t, f"v{k}")
                act.activation(V[t.pre.par][0:TLEN[k], k, :, 0:HD],
                               G[g][0:TLEN[k], 0:D].rearrange("p (h d) -> p h d", d=HD), ACT.Copy).then_inc(g_emptied[g], 1)

            def body(t):
                if t.at:
                    for j in range(GROUPS):
                        weights(t, j)
                        if j:
                            attended(t, j - 1)
                    attended(t, GROUPS - 1)
                if t.pre:
                    copy_tokens(t, "xnT0", xnT)
                    copy_tokens(t, "xnT1", xnT)
                    values_out(t, 0)
                if t.at:
                    copy_tokens(t, "at0", attT)
                    copy_tokens(t, "at1", attT)
                if t.mid:
                    g = take(t, "mT")
                    act.activation(mT[:], Gb[g][0:3 * HEADS, 0:TT * P].rearrange("p (t q) -> p t q", q=P), ACT.Copy).then_inc(g_emptied[g], 1)
                if t.pre:
                    pairs(t, 0)
                    values_out(t, 1)
                    pairs(t, 1)
                    values_out(t, 2)
                    pairs(t, 2)
                    for k in range(TT):
                        pairs1(t, k)
                if t.at:
                    copy_tokens(t, "x20", xn2T)
                    copy_tokens(t, "x21", xn2T)
                if t.pre:
                    for u in (0, 2, 4, 6):
                        g = take(t, f"t{u}")
                        copy_parts(act, t, u, Gb[g]).then_inc(g_emptied[g], 1)

            rounds(act, body)

        @block.gpsimd
        def _(pool):
            pool.memset(padding[:], 0.0).then_inc(padding_set, 1)
            pool.wait_ge(padding_set, 1)
            pool.memset(padding[:, :, D + 1:D + 2], NOWHERE).then_inc(padding_set, 1)
            pool.wait_ge(padding_set, 2)

            def pad(rows, width, tile):
                dst = rows[bass.ds(tile * ROWS, ROWS), :].rearrange("(p t) d -> p t d", p=P)
                pool.dma_start(dst, padding[:, :, 0:width]).then_inc(padded, 16)

            pool.wait_ge(consts_set, n_set)

            def root(which, b):
                wait_apart(pool, var_ready[which], b.n + 1)
                pool.tensor_scalar(veps[:, which, :], mv[:, which, :, 1], EPS, None, ALU.add).then_inc(veps_ready[which], 1)
                pool.wait_ge(veps_ready[which], b.n + 1)
                pool.tensor_tensor(rstd[:, which, :], veps[:, which, :], minus_half[:], ALU.pow).then_inc(rstd_ready[which], 1)

            def body(t):
                if t.pre:
                    root(0, t.pre)
                if t.mid:
                    b = t.mid
                    if t.at:
                        wait_apart(pool, rows_out[b.par], b.half * 64 + FREE)
                    pool.tensor_copy(h2[b.par][:, 0:2, :], h[b.par][:, 0:2, :])
                    pool.tensor_copy(h2[b.par][0:TLEN[2], 2, :], h[b.par][0:TLEN[2], 2, :]).then_inc(h_saved, 1)
                if t.at:
                    root(1, t.at)
                    if isinstance(t.at.n, int):
                        k = t.at.n - (B - 4)
                        tiles_ = [LOOPED + 3 * k + i for i in range(3)]
                        for i in tiles_:
                            if i < CT:
                                pad(xc_d, RC, i)
                            elif i - CT + LOOPED < TILES - CT:
                                pad(xu_d, RU, i - CT + LOOPED)
                    else:
                        pad(xc_d, RC, t.at.n)
                        pad(xu_d, RU, t.at.n)

            rounds(pool, body)
            pool.wait_ge(padded, 16 * TILES)

        @block.vector
        def _(dve):
            for e in (*m_read, r_read):
                dve.sem_inc(e, FREE)
            for p in range(2):
                dve.memset(KS[p][KS_ROWS:KROWS, :, :], 1.0).then_inc(consts_set, 1)
                dve.memset(V[p][:], 1.0).then_inc(consts_set, 1)
            for x in (xnT, attT, xn2T):
                dve.memset(x[KC:KC + 1, :, :], 1.0).then_inc(consts_set, 1)
            dve.memset(mv[:], 1.0).then_inc(consts_set, 1)
            dve.memset(nmp[:], 0.0).then_inc(consts_set, 1)
            dve.memset(minus_half[:], -0.5).then_inc(consts_set, 1)
            dve.wait_ge(consts_in, 16 * len(loads))
            dve.tensor_tensor(base[:], base[:], biasb[:], ALU.add).then_inc(consts_set, 1)
            dve.tensor_copy(identb[:], ident[:]).then_inc(consts_set, 1)
            dve.tensor_copy(mask_qk[:], masks[:, 0, :]).then_inc(consts_set, 1)
            dve.tensor_copy(mask_kq[:], masks[:, 1, :]).then_inc(consts_set, 1)
            dve.wait_ge(consts_set, n_set)
            st = Steps(dve, steps, at=4, mid=4, pre=1)

            def take(t, use):
                dve.wait_ge(g_filled[t.bank(use)], t.before(use) + 1)
                return t.bank(use)

            def norm(src, dst, which, ready, b):
                k = {}

                def stats(i):
                    ins = dve.bn_stats(stat[0:TLEN[i], which, i, :], src[0:TLEN[i], i, :])
                    if i == TT - 1:
                        k["stats"] = st.done(ins)

                def aggr():
                    wait_apart(dve, steps, st.base + k["stats"])
                    for i in range(TT):
                        ins = dve.bn_aggr(mv[0:TLEN[i], which, i, :], stat[0:TLEN[i], which, i, :])
                    ins.then_inc(var_ready[which], 1)

                def scale(i):
                    if i == 0:
                        dve.wait_ge(rstd_ready[which], b.n + 1)
                    n = TLEN[i]
                    ins = dve.tensor_scalar(dst[0:n, i, :], src[0:n, i, :], mv[0:n, which, i, 0:1],
                                            rstd[0:n, which, i:i + 1], ALU.subtract, ALU.mult)
                    if i == TT - 1:
                        ins.then_inc(ready, 1)

                return stats, aggr, scale

            def embedded(t, k):
                g = take(t, f"emb{k}")
                if k == 0 and t.mid:
                    dve.wait_ge(h_saved, t.mid.n + 1)
                n = P if k == 0 else IMG1
                dve.tensor_tensor(h[t.new.par][0:n, k, :], G[g][0:n, 0:D], base[0:n, k, :], ALU.add).then_inc(g_emptied[g], 1)

            def text(t):
                dve.wait_ge(txt_in[t.pre.par], t.pre.half * 32 + 32)
                for e in g_emptied:
                    dve.wait_ge(e, t.before())

            def max_parts(t):
                dve.wait_ge(g_emptied[t.bank("mq2")], t.before("mq2") + 1)
                dve.tensor_copy(nm[:, 0:HEADS], nm3[:, :, 0])
                a0 = st.done(dve.tensor_tensor(nm[:, HEADS:2 * HEADS], nm3[:, :, 1], nm3[:, :, 2], ALU.min))
                st.need(a0)
                p0, p1, p2 = (nmp[:].rearrange("p t h r -> p (t h) r")[:, 0:NM, r] for r in range(3))
                a1 = st.done(dve.tensor_copy(p0, nm[:]))
                st.need(a1)
                a2 = st.done(dve.tensor_tensor(nmd[:], nm[:], p0, ALU.subtract))
                st.need(a2)
                a3 = st.done(dve.tensor_copy(p1, nmd[:]))
                st.need(a3)
                dve.tensor_tensor(p2, nmd[:], p1, ALU.subtract).then_inc(nmax_ready, 1)

            def rotate(t, k):
                g, n = take(t, f"qk{k}"), TLEN[k]
                dve.tensor_tensor(ropeA[0:n, k, :], G[g][0:n, 0:2 * D], cosw[0:n, k, :], ALU.mult)
                pair = lambda x: x.rearrange("p (m two) -> p m two", two=2)
                dve.tensor_tensor(pair(ropeB[0:n, k, :]), pair(G[g][0:n, 0:2 * D])[:, :, ::-1],
                                  pair(sinw[0:n, k, :]), ALU.mult).then_inc(g_emptied[g], 1)
                dve.wait_ge(g_emptied[g], t.before(f"qk{k}") + 1)
                dve.tensor_tensor(rr[0:n, k, :], ropeA[0:n, k, :], ropeB[0:n, k, :], ALU.add).then_inc(rope_r, 1)

            def second(t, k):
                n = TLEN[k]
                dve.wait_ge(part0, t.pre.n * TT + k + 1)
                dve.tensor_tensor(d1[0:n, k, :].rearrange("p (h d) -> p h d", d=HD),
                                  rr[0:n, k, :].rearrange("p (h d) -> p h d", d=HD), stk[0:n, k, :, 0, :],
                                  ALU.subtract).then_inc(diff1, 1)

            def third(t, k):
                n = TLEN[k]
                dve.wait_ge(part1, t.pre.n * TT + k + 1)
                dd = d1[0:n, k, :].rearrange("p (h d) -> p h d", d=HD)
                dve.tensor_tensor(stk[0:n, k, 0:HEADS, 5, :], dd[:, 0:HEADS], stk[0:n, k, 0:HEADS, 3, :], ALU.subtract)
                dve.tensor_tensor(stk[0:n, k, HEADS:2 * HEADS, 2, :], dd[:, HEADS:2 * HEADS],
                                  stk[0:n, k, HEADS:2 * HEADS, 1, :], ALU.subtract).then_inc(parts_ready, 1)

            def divide(t, k):
                n = TLEN[k]
                dve.wait_ge(ut_filled, t.at.n * TT + k + 1)
                heads = SP_[k][0:n, 0:GROUPS * P].rearrange("p (h c) -> p h c", c=32)
                r = st.done(dve.reciprocal(rec[0:n, k, :], heads[:, :, HD]))
                st.need(r)
                dve.tensor_tensor(att[0:n, k, :].rearrange("p (h d) -> p h d", d=HD), heads[:, :, 0:HD],
                                  rec[0:n, k, :].rearrange("p (h a) -> p h a", a=1).broadcast_to([n, HEADS, HD]),
                                  ALU.mult).then_inc(att_ready, 1)

            def add_attention(t):
                b, n = t.at, TLEN[2]
                if not t.new:
                    dve.wait_ge(h_saved, b.n + 1)
                g = take(t, "o0")
                h01 = h2[b.par][:, 0:2, :].rearrange("p t d -> p (t d)")
                dve.tensor_tensor(h01, G[g][:, 0:2 * D], h01, ALU.add).then_inc(g_emptied[g], 1)
                g = take(t, "o1")
                dve.tensor_tensor(h2[b.par][0:n, 2, :], G[g][0:n, 0:D], h2[b.par][0:n, 2, :], ALU.add).then_inc(g_emptied[g], 1)
                dve.wait_ge(g_emptied[t.bank("o0")], t.before("o0") + 1)
                dve.wait_ge(g_emptied[t.bank("o1")], t.before("o1") + 1)

            def body(t):
                st.begin(t)
                b, pre = t.at, t.pre
                todo = []
                if pre:
                    stats, aggr, scale = norm(h[pre.par], xn, 0, xn_ready, pre)
                    todo = [lambda: (text(t), stats(0)), lambda: stats(1), lambda: stats(2), aggr,
                            lambda: scale(0), lambda: scale(1), lambda: scale(2)]
                if t.mid:
                    for head in range(HEADS):
                        i = head % 2
                        dve.wait_ge(m_filled[i], t.in_max_banks() + (head // 2 + 1))
                        dve.tensor_reduce(nm3[:, head, :], MP[i][:, 0:3 * P].rearrange("p (t k) -> p t k", k=P), AX.X, ALU.max,
                                          negate=True).then_inc(m_read[i], 1)
                        if head % GH == 3:
                            j = head // GH
                            g = take(t, f"mq{j}")
                            dve.tensor_reduce(nm[:, 2 * HEADS + j:2 * HEADS + j + 1], G[g][:, 0:S], AX.X, ALU.max,
                                              negate=True).then_inc(g_emptied[g], 1)
                        if todo and head in (1, 2, 4, 5, 7, 8, 9):
                            todo.pop(0)()
                for f in todo:
                    f()
                if t.mid:
                    max_parts(t)
                if b:
                    for k in range(TT):
                        divide(t, k)
                if pre:
                    rotate(t, 0)
                    rotate(t, 1)
                if b:
                    add_attention(t)
                    stats, aggr, scale = norm(h2[b.par], xn2[b.par], 1, xn2_ready, b)
                    for k in range(TT):
                        stats(k)
                    aggr()
                if pre:
                    rotate(t, 2)
                if b:
                    for k in range(TT):
                        scale(k)
                if pre:
                    second(t, 0)
                    second(t, 1)
                if t.new:
                    embedded(t, 0)
                if pre:
                    second(t, 2)
                    third(t, 0)
                    third(t, 1)
                if t.new:
                    embedded(t, 1)
                if pre:
                    third(t, 2)
                if b:
                    dve.wait_ge(r_filled, b.n + 1)
                    dve.tensor_copy(logits[:, b.n, :], SP_[0][0:NE, 0:S]).then_inc(r_read, 1)
                if pre:
                    for u in (1, 3, 5, 7):
                        i = u // 2 % 2
                        dve.wait_ge(m_filled[i], t.in_max_banks(u) + 1)
                        copy_parts(dve, t, u, Mb[i]).then_inc(m_read[i], 1)
                st.end()

            rounds(dve, body)


class Tile:

    def __init__(self, quad, i, search=False, settle=False, spread=False, unique=False):
        self.opens = i == 0 and (unique or isinstance(quad, int) and quad == 0)
        self.closes = i == DEPTH - 1 and (unique or isinstance(quad, int) and quad == SWITCH)
        self.quad, self.i, self.n = quad, i, quad * DEPTH + i
        self.par = i % 2
        self.search, self.settle, self.spread = search, settle, spread
        self.unique = self.n >= CT if isinstance(quad, int) else unique
        self.number = self.n if isinstance(quad, int) else None

    def before(self, k):
        quad, i = (self.quad, self.i - k) if self.i >= k else (self.quad - 1, self.i - k + DEPTH)
        return Tile(quad, i, unique=self.unique)

    def next(self):
        return Tile(self.quad + (self.i + 1) // DEPTH, (self.i + 1) % DEPTH)

    def at_least(self, n):
        return self.number is None or self.number >= n


SEARCH, SETTLE, SPREAD, SWITCH = 4, 4, 5, CT // DEPTH
SPREAD_END = SPREAD + -(-CHUNKS // (2 * DEPTH))
LAST_QUAD = TILES // DEPTH - 1
assert SPREAD_END <= SWITCH
assert 2 * DEPTH * SEARCH >= 27


def tiles(eng, body, load_end):
    def straight(quad, **kind):
        for i in range(DEPTH):
            body(Tile(quad, i, **kind))

    def loop(a, b, **kind):
        with eng.Fori(a, b) as quad:
            for i in range(DEPTH):
                body(Tile(quad, i, **kind))

    straight(0, search=True)
    loop(1, SEARCH, search=True)
    straight(SETTLE, settle=True)
    for quad in range(SPREAD, SPREAD_END):
        straight(quad, spread=True)
    for quad in range(SPREAD_END, SWITCH + 1):
        straight(quad)
    end = load_end(eng)
    with eng.Fori(SWITCH + 1, LAST_QUAD + 1) as quad:
        with eng.If(quad * DEPTH < end):
            for i in range(DEPTH):
                body(Tile(quad, i, unique=True))
        with eng.Else():
            eng.nop()


def experts(nc, A, logits, h2_d, xn2_d, xc_d, xu_d, out):
    ctx = ExitStack()
    with ctx:
        def sb(name, shape, dt=F32):
            return ctx.enter_context(nc.sbuf_tensor(name, shape, dt))

        def ps(name):
            return ctx.enter_context(nc.psum_tensor(name, [P, 512], F32))

        def sem(name):
            return ctx.enter_context(nc.semaphore(name))

        def sems(name, n=DEPTH):
            return [sem(f"{name}{i}") for i in range(n)]

        consts = sb("route_consts", [P, CWIDTH])
        C, at = {}, 0
        for name, n in CONSTS.items():
            C[name] = consts[:, at:at + n]
            at += n
        by_token = sb("by_token", [P, COLS, NE])
        before = sb("before", [P, P])
        ones = sb("ones", [P, P])
        eye = sb("eye", [P, P])
        z = sb("z", [P, COLS, 2, NX])
        ez = sb("ez", [P, COLS, 2, NX])
        mx = sb("mx", [P, COLS, 2])
        total = sb("total", [P, COLS, 2])
        pmax = sb("pmax", [P, COLS, 2])
        OH = sb("OH", [P, 2, NX, COLS])
        key = sb("key", [P, NX, COLS])
        T = sb("T", [P, NX])
        cand = sb("cand", [P, NX])
        step = sb("step", [P, 1])
        gain = sb("gain", [P, NX])
        part = sb("part", [P, NX])
        need = sb("need", [P, NX])
        flag = sb("flag", [P, NX, COLS])
        tie = sb("tie", [P, NX, COLS])
        run_ = sb("run", [P, NX, COLS])
        rk = sb("rk", [P, NX, COLS])
        posf = sb("posf", [P, COLS])
        drop = sb("drop", [P, COLS])
        more = sb("more", [P, NX, KTH])
        nt = sb("nt", [P, NX])
        first = sb("first", [P, NX])
        first_row = sb("first_row", [P, NX])
        tcmp = sb("tcmp", [P, TILES, NX - 1])
        tex = sb("tex", [P, TILES])
        pos = sb("pos", [P, 2, COLS], U32)
        meta = sb("meta", [P, 2, COLS, 2])
        wrow = sb("wrow", [P, TILES], U32)
        end_tile = sb("end_tile", [1, 1], U32)
        end_stored = sb("end_stored", [1, 1], U32)
        end_f = sb("end_f", [1, 1])
        quads_f = sb("quads_f", [1, TILES // DEPTH])
        tok = sb("tok", [P, 4, CC, RC])
        idx = sb("idx", [P, 4, CC], U32)
        ids = [sb(f"ids{i}", [P, ROWS // P], U32) for i in range(DEPTH)]
        W = [sb(f"W{i}", [P, WCOLS]) for i in range(DEPTH)]
        X = [sb(f"X{i}", [P, ROWS // P, RC]) for i in range(DEPTH)]
        XTh = [sb(f"XTh{i}", [KC, 2, ROWS], F32R) for i in range(2)]
        XTl = [sb(f"XTl{i}", [KC, 2, ROWS], F32R) for i in range(2)]
        Wh = [sb(f"Wh{i}", [KC, 2 * FF], F32R) for i in range(2)]
        Wl = [sb(f"Wl{i}", [KC, 2 * FF], F32R) for i in range(2)]
        Gl = [sb(f"Gl{i}", [P, FC, ROWS]) for i in range(2)]
        base = [sb(f"base_rows{i}", [P, ROWS // P, D]) for i in range(DEPTH)]
        Yb = sb("Yb", [P, ROWS // P, D])
        Y = [sb(f"Y{i}", [P, ROWS // P, D]) for i in range(DEPTH)]
        xt_ps, y_ps, cnt_ps, in_col, of_col = (ps(f"{x}_ps") for x in ("xt", "y", "cnt", "in_col", "of_col"))
        h_ps = [ps(f"h_ps{i}") for i in range(3)]

        r_in = sem("r_in")
        z_ready, e_ready = sem("z_ready"), sem("e_ready")
        turned_in = sem("turned_in")
        v = sem("v_steps")
        part_ready, counted = sem("part_ready"), sem("counted")
        ranks_in, ranks_out = sem("ranks_in"), sem("ranks_out")
        placed = sem("placed")
        tok_in = sems("tok_in")
        idx_ready = sem("idx_ready")
        tok_out = sems("tok_out")
        apart = {e: sem(f"apart_x{i}") for i, e in enumerate((nc.sync.engine, nc.gpsimd.engine, nc.vector.engine))}

        def wait_apart(eng, semaphore, value):
            eng.wait_ge(semaphore, value)
            eng.sem_inc(apart[eng.engine], 1)

        def chunk_rows(c):
            if isinstance(c, int) and c == CHUNKS - 1:
                return ((0, CC - 1, P), (CC - 1, 1, LASTN))
            return ((0, CC, P),)

        def load_chunk(sp, src, c, buf, at, loaded):
            rows = src.rearrange("b s d -> (b s) d")
            for k, n, lanes in chunk_rows(c):
                sp.dma_start(tok[0:lanes, buf, k:k + n, at:at + D],
                             rows[bass.ds(c * (CC * P) + k * P, (n - 1) * P + lanes), :].rearrange("(t p) d -> p t d", p=lanes)
                             ).then_inc(loaded, 16)

        def send_chunk(pool, c, buf, kind, target, width, rows, ready, count, loaded, value, sent):
            pool.tensor_copy(idx[:, buf, :], pos[:, kind, bass.ds(c * CC, CC)])
            pool.tensor_copy(tok[:, buf, :, D:D + 2], meta[:, kind, bass.ds(c * CC, CC), :]).then_inc(ready, 1)
            wait_apart(pool, ready, count)
            wait_apart(pool, loaded, value)
            for k0, n, lanes in chunk_rows(c):
                for k in range(k0, k0 + n):
                    pool.indirect_dma_start(target[:, :], bass.IndirectOffsetOnAxis(idx[0:lanes, buf, k:k + 1], 0), tok[0:lanes, buf, k, 0:width],
                                            None, bounds_check=rows - 1, oob_is_err=False).then_inc(sent, 16)

        def uses(buf):
            return len(range(buf, CHUNKS, 4))

        made = 0

        def done(ins):
            nonlocal made
            made += 1
            ins.then_inc(v, 1)
            nc.vector.wait_ge(v, made)

        dve = nc.vector
        bc = lambda x, shape: x.broadcast_to(shape)
        by_e = lambda x: bc(x.rearrange("p (e a) -> p e a", a=1), [P, NX, COLS])
        by_c = lambda x: bc(x.rearrange("p (a c) -> p a c", a=1), [P, NX, COLS])
        over_e = lambda x: x.rearrange("p e c -> p c e")
        flat = lambda x: x.rearrange("p e c -> p (e c)")

        def column_ranks(k):
            n = NX * COLS

            def scan():
                dve.wait_ge(ranks_out, k + 1)
                done(dve.tensor_tensor_scan(flat(run_[:]), C["seg"], of_col[:, 0:n], 0.0, ALU.mult, ALU.add))

            return [scan,
                    lambda: done(dve.tensor_tensor(flat(rk[:]), flat(run_[:]), of_col[:, 0:n], ALU.subtract)),
                    lambda: done(dve.tensor_tensor(flat(rk[:]), flat(rk[:]), in_col[:, 0:n], ALU.add))]

        def place(kind, tile0, last_tile):
            cnt = run_[:, :, COLS - 1]
            n = last_tile - tile0
            tile = C["tile"][:, tile0:last_tile].rearrange("p (t a) -> p t a", a=1)
            mine = slice(tile0, last_tile)
            row0 = 0 if kind == 0 else CT
            steps_ = [
                lambda: done(dve.tensor_tensor(more[:], bc(cnt.rearrange("p (e a) -> p e a", a=1), [P, NX, KTH]),
                                               bc(C["kth"].rearrange("p (a k) -> p a k", a=1), [P, NX, KTH]), ALU.is_gt)),
                lambda: done(dve.tensor_reduce(nt[:], more[:], AX.X, ALU.add)),
                lambda: done(dve.tensor_tensor_scan(first[:], C["one"], nt[:], float(tile0), ALU.mult, ALU.add)),
                lambda: done(dve.tensor_tensor(first[:], first[:], nt[:], ALU.subtract)),
                lambda: done(dve.tensor_scalar(first_row[:], first[:], float(-row0), float(ROWS), ALU.add, ALU.mult)),
                lambda: done(dve.tensor_tensor(rk[:], rk[:], by_e(first_row[:]), ALU.add)),
                lambda: done(dve.tensor_tensor(rk[:], rk[:], OH[:, kind], ALU.mult)),
                lambda: done(dve.tensor_reduce(posf[:], over_e(rk[:]), AX.X, ALU.add)),
                lambda: done(dve.tensor_tensor(tcmp[:, 0:n, :], bc(tile, [P, n, NX - 1]),
                                               bc(first[:, 1:NX].rearrange("p (a e) -> p a e", a=1), [P, n, NX - 1]), ALU.is_ge)),
                lambda: done(dve.tensor_reduce(tex[:, mine], tcmp[:, 0:n, :], AX.X, ALU.add)),
                lambda: done(dve.tensor_scalar(tex[:, mine], tex[:, mine], float(NX * kind), float(P), ALU.add, ALU.mult)),
                lambda: done(dve.tensor_scalar(wrow[:, mine], tex[:, mine], C["lane"], None, ALU.add))]
            if kind == 1:
                quads = C["tile"][0:1, 0:TILES:DEPTH]
                steps_ += [
                    lambda: done(dve.tensor_tensor(end_f[:], first[0:1, NX - 1:NX], nt[0:1, NX - 1:NX], ALU.add)),
                    lambda: done(dve.tensor_copy(end_tile[:], end_f[:])),
                    lambda: done(dve.tensor_tensor(quads_f[:], quads, end_f[:].broadcast_to([1, TILES // DEPTH]), ALU.is_lt)),
                    lambda: done(dve.tensor_reduce(end_f[:], quads_f[:], AX.X, ALU.add)),
                    lambda: done(dve.tensor_scalar(end_stored[:], end_f[:], float(SWITCH + 1), 32.0, ALU.max, ALU.mult))]
            return steps_

        def chunks(eng, body):
            for c in range(4):
                body(c, c, 0)
            with eng.Fori(1, CHUNKS // 4) as quad:
                for buf in range(4):
                    body(buf, quad * 4 + buf, quad)
            for c in range(CHUNKS // 4 * 4, CHUNKS):
                body(c % 4, c, c // 4)

        with nc.Block() as block:
            @block.sync
            def _(sp):
                sp.dma_start(consts[:], A["rconsts"]).then_inc(r_in, 16)
                sp.dma_start(before[:], A["before"]).then_inc(r_in, 16)
                sp.dma_start(eye[:], A["ident"]).then_inc(r_in, 16)

                def load(buf, c, quad):
                    if not (isinstance(c, int) and c < 4):
                        wait_apart(sp, tok_out[buf], quad * (16 * CC))
                    load_chunk(sp, xn2_d, c, buf, 0, tok_in[buf])
                    load_chunk(sp, h2_d, c, buf, D + 2, tok_in[buf])

                chunks(sp, load)

            @block.gpsimd
            def _(pool):
                pool.wait_ge(placed, 1)

                def send(buf, c, quad):
                    if not (isinstance(c, int) and c < 4):
                        wait_apart(pool, tok_out[buf], quad * (16 * CC))
                    send_chunk(pool, c, buf, 0, xc_d, RC, CT * ROWS, idx_ready, c + 1,
                               tok_in[buf], quad * 32 + 32 * len(chunk_rows(c)), tok_out[buf])

                chunks(pool, send)
                for buf, e in enumerate(tok_out):
                    pool.wait_ge(e, uses(buf) * 16 * CC)

            @block.scalar
            def _(act):
                nc.scalar.wait_ge(z_ready, 1)
                nc.scalar.activation(ez[:], z[:], ACT.Exp).then_inc(e_ready, 1)

            @block.tensor
            def _(pe):
                pe.wait_ge(r_in, 48)
                flat_logits = logits[:].rearrange("e b s -> e (b s)")
                for c in range(COLS):
                    n, at = P if c < COLS - 1 else LASTN, c % HALF * NE
                    mm = pe.transpose((in_col, of_col)[c // HALF][0:n, at:at + NE], flat_logits[:, c * P:c * P + n], eye[0:NE, 0:NE])
                mm.then_inc(turned_in, 1)
                pe.wait_ge(ranks_in, 1)
                pe.matmul(in_col[:, 0:NX * COLS], before[:], flat(OH[:, 0]), start=True, stop=True)
                pe.matmul(of_col[:, 0:NX * COLS], ones[:], flat(OH[:, 0]), start=True, stop=True).then_inc(ranks_out, 1)

            @block.vector
            def _(dve):
                last = lambda x: bc(x.rearrange("p c (s a) -> p c s a", a=1), [P, COLS, 2, NX])
                order = bc(C["rank"].rearrange("p (a b e) -> p a b e", a=1, b=1), [P, COLS, 2, NX])
                for x, value in ((ones, 1.0), (T, 0.0), (step, 1.0)):
                    done(dve.memset(x[:], value))
                for x in base:
                    done(dve.memset(x[:], 0.0))
                dve.wait_ge(r_in, 48)
                done(dve.memset(by_token[:, COLS - 1, :], 0.0))
                dve.wait_ge(turned_in, 1)
                n = COLS - 1 - HALF
                full = lambda x: x.rearrange("p c e -> p (c e)")
                dve.tensor_copy(full(by_token[:, 0:HALF, :]), in_col[:, 0:HALF * NE])
                dve.tensor_copy(full(by_token[:, HALF:COLS - 1, :]), of_col[:, 0:n * NE])
                done(dve.tensor_copy(by_token[0:LASTN, COLS - 1, :], of_col[0:LASTN, n * NE:(n + 1) * NE]))
                lg = by_token[:].rearrange("p c (s e) -> p c s e", s=2)
                done(dve.tensor_reduce(mx[:], lg, AX.X, ALU.max))
                dve.tensor_tensor(z[:], lg, last(mx), ALU.subtract).then_inc(z_ready, 1)
                dve.wait_ge(e_ready, 1)
                done(dve.tensor_reduce(total[:], ez[:], AX.X, ALU.add))
                done(dve.reciprocal(mx[:], total[:]))
                done(dve.tensor_tensor(ez[:], ez[:], last(mx), ALU.mult))
                done(dve.tensor_reduce(pmax[:], ez[:], AX.X, ALU.max))
                done(dve.tensor_tensor(z[:], ez[:], last(pmax), ALU.is_equal))
                done(dve.tensor_tensor(z[:], z[:], order, ALU.mult))
                done(dve.tensor_reduce(total[:], z[:], AX.X, ALU.max))
                done(dve.tensor_tensor(OH[:].rearrange("p s e c -> p c s e"), last(total), order, ALU.is_equal))
                done(dve.tensor_tensor(OH[:, 0], OH[:, 0], by_c(C["valid"]), ALU.mult))
                dve.sem_inc(ranks_in, 1)
                done(dve.tensor_tensor(OH[:, 1], OH[:, 1], by_c(C["valid"]), ALU.mult))
                done(dve.tensor_tensor(key[:], OH[:, 0], by_c(pmax[:, :, 0]), ALU.mult))
                done(dve.reciprocal(mx[:], pmax[:]))
                done(dve.tensor_tensor(meta[:, :, :, 0].rearrange("p s c -> p c s"), pmax[:], mx[:], ALU.mult))
                for kind in range(2):
                    done(dve.tensor_copy(meta[:, kind, :, 1], C["ids"]))
                for f in column_ranks(0) + place(0, 0, CT):
                    f()
                done(dve.tensor_copy(pos[:, 0, :], posf[:]))
                dve.sem_inc(placed, 1)

        w_in = sems("w_in")
        rows_in = sems("rows_in")
        ids_ready = sem("ids_ready")
        base_in = sems("base_in")
        xt_filled, xh_ready, xt_ready = sem("xt_filled"), sem("xh_ready"), sem("xt_ready")
        wh_ready, wl_ready = sem("wh_ready"), sem("wl_ready")
        h_filled, g_ready = sem("h_filled"), sem("g_ready")
        y_filled, yb_ready, y_ready = sem("y_filled"), sem("yb_ready"), sem("y_ready")
        y_out = sems("y_out")
        spread_in = sems("spread_in")
        spread_out = sems("spread_out")
        spread_ready = sem("spread_ready")
        block = ctx.enter_context(nc.Block())

        def spread_chunks(t):
            for u in range(2):
                c = (t.quad - SPREAD) * (2 * DEPTH) + 2 * t.i + u
                if c < CHUNKS:
                    yield c, c % 4, c // 4

        out_rows = out.rearrange("b s d -> (b s) d")
        unique_rows = (TILES - CT) * ROWS

        def load_end(eng):
            if eng is not nc.vector:
                eng.wait_ge(placed, 2)
            return eng.value_load(end_tile[0:1, 0:1], min_val=0, max_val=TILES)

        def halves(w, half):
            return w[:, 0:2 * FF].rearrange("p (c h f) -> p c h f", c=2, h=2)[:, :, half, :]

        @block.sync
        def _(sp):
            def body(t):
                if t.at_least(DEPTH):
                    wait_apart(sp, y_ready, t.n - (DEPTH - 1))
                if t.unique:
                    if t.number == CT:
                        for buf, e in enumerate(spread_out):
                            sp.wait_ge(e, uses(buf) * 16 * CC)
                    sp.dma_start(X[t.i][:, :, 0:RU], xu_d[bass.ds((t.n - CT) * ROWS, ROWS), :].rearrange("(t p) d -> p t d", p=P)
                                 ).then_inc(rows_in[t.i], 16)
                else:
                    sp.dma_start(X[t.i][:], xc_d[bass.ds(t.n * ROWS, ROWS), :].rearrange("(t p) d -> p t d", p=P)).then_inc(rows_in[t.i], 16)
                row = sp.value_load(wrow[0:1, bass.ds(t.n, 1)], min_val=0, max_val=(2 * NX - 1) * P)
                sp.dma_start(W[t.i][:, :], A["experts"][bass.ds(row, P), :]).then_inc(w_in[t.i], 16)
                if t.spread:
                    for c, buf, use in spread_chunks(t):
                        if use:
                            wait_apart(sp, spread_out[buf], use * (16 * CC))
                        load_chunk(sp, xn2_d, c, buf, 0, spread_in[buf])

            tiles(sp, body, load_end)

        @block.gpsimd
        def _(pool):
            def send(t):
                for k in range(ROWS // P):
                    pool.indirect_dma_start(out_rows, bass.IndirectOffsetOnAxis(ids[t.i][:, k:k + 1], 0), Y[t.i][:, k, :],
                                            None, bounds_check=N - 1, oob_is_err=False).then_inc(y_out[t.i], 16)

            def numbers(t):
                if t.at_least(DEPTH):
                    wait_apart(pool, y_out[t.i], t.quad * 32)
                wait_apart(pool, rows_in[t.i], t.quad * 16 + 16)
                pool.tensor_copy(ids[t.i][:], X[t.i][:, :, D + 1]).then_inc(ids_ready, 1)
                if t.unique:
                    wait_apart(pool, ids_ready, t.n + 1)
                    if t.number == CT:
                        for n in range(SWITCH * DEPTH, CT):
                            wait_apart(pool, y_ready, n + 1)
                            send(Tile(SWITCH, n % DEPTH))
                        for i, e in enumerate(y_out):
                            pool.wait_ge(e, len(range(i, CT, DEPTH)) * 32)
                    for k in range(ROWS // P):
                        pool.indirect_dma_start(base[t.i][:, k, :], None, out_rows, bass.IndirectOffsetOnAxis(ids[t.i][:, k:k + 1], 0),
                                                bounds_check=N - 1, oob_is_err=False).then_inc(base_in[t.i], 16)

            def spread(t):
                for c, buf, use in spread_chunks(t):
                    if use:
                        wait_apart(pool, spread_out[buf], use * (16 * CC))
                    send_chunk(pool, c, buf, 1, xu_d, RU, unique_rows, spread_ready, c + 1,
                               spread_in[buf], use * 16 + 16 * len(chunk_rows(c)), spread_out[buf])

            def body(t):
                if t.number is not None and t.number >= DEPTH or t.number is None and not t.unique:
                    wait_apart(pool, y_ready, t.n - (DEPTH - 1))
                    send(Tile(t.quad - 1, t.i))
                if t.i >= 2 or t.at_least(2) and not (t.number is None and t.unique):
                    numbers(t.before(2))
                if t.number == SPREAD * DEPTH:
                    pool.wait_ge(placed, 2)
                if t.spread:
                    spread(t)
                if t.closes:
                    numbers(t.before(1))
                    numbers(t)
                    for i in range(DEPTH):
                        if t.number is None or i >= CT % DEPTH:
                            wait_apart(pool, y_ready, t.quad * DEPTH + (i + 1))
                            send(Tile(t.quad, i))

            tiles(pool, body, load_end)
            stored = pool.value_load(end_stored[0:1, 0:1], min_val=32, max_val=32 * TILES // DEPTH)
            for e in y_out:
                pool.wait_ge(e, stored)

        @block.tensor
        def _(pe):
            def turn(t):
                pe.wait_ge(rows_in[t.i], t.quad * 16 + 16)
                if t.at_least(1):
                    pe.wait_ge(xt_ready, t.n)
                for c in range(2):
                    for k in range(ROWS // P):
                        mm = pe.transpose(xt_ps[0:KC, c * ROWS + k * P:c * ROWS + (k + 1) * P],
                                          X[t.i][:, k, c * KC:(c + 1) * KC], eye[:])
                mm.then_inc(xt_filled, 1)

            def up(t, chunks):
                for f in chunks:
                    if not (t.number == 0 and f < 3):
                        pe.wait_ge(g_ready, t.n * FC + (f - 2))
                    products = [(w, x, c) for c in range(2) for w, x in ((Wh, XTh), (Wh, XTl), (Wl, XTh))]
                    for k, (w, x, c) in enumerate(products):
                        mm = pe.matmul(h_ps[f % 3][:, 0:ROWS], w[t.par][:, c * FF + f * P:c * FF + (f + 1) * P],
                                       x[t.par][:, c, :], start=(k == 0), stop=(k == len(products) - 1))
                    mm.then_inc(h_filled, 1)

            def down(t):
                pe.wait_ge(g_ready, t.n * FC + FC)
                if t.at_least(1):
                    pe.wait_ge(y_ready, t.n)
                for k in range(ROWS // P):
                    for f in range(FC):
                        mm = pe.matmul(y_ps[:, k * D:(k + 1) * D], Gl[t.par][:, f, k * P:(k + 1) * P],
                                       W[t.i][:, W2O + f * D:W2O + (f + 1) * D], start=(f == 0), stop=(f == FC - 1))
                mm.then_inc(y_filled, 1)

            def ranks(k, src):
                pe.wait_ge(ranks_in, k + 1)
                pe.matmul(in_col[:, 0:NX * COLS], before[:], flat(src), start=True, stop=True)
                pe.matmul(of_col[:, 0:NX * COLS], ones[:], flat(src), start=True, stop=True).then_inc(ranks_out, 1)

            def count(n):
                pe.wait_ge(part_ready, n + 1)
                pe.matmul(cnt_ps[:, 0:NX], ones[:], part[:], start=True, stop=True).then_inc(counted, 1)

            def body(t):
                if t.opens:
                    turn(t)
                if not t.closes:
                    turn(t.next())
                pe.wait_ge(w_in[t.i], t.quad * 16 + 16)
                pe.wait_ge(xt_ready, t.n + 1)
                pe.wait_ge(wl_ready, t.n * 2 + 1)
                up(t, range(3))
                pe.wait_ge(wl_ready, t.n * 2 + 2)
                up(t, range(3, FC))
                if t.search or t.number == SETTLE * DEPTH:
                    count(t.n * 2)
                if not t.opens:
                    down(t.before(1))
                if t.search:
                    count(t.n * 2 + 1)
                if t.number == SETTLE * DEPTH:
                    ranks(1, tie)
                if t.number == SETTLE * DEPTH + 1:
                    ranks(2, OH[:, 1])
                if t.closes:
                    down(t)

            tiles(pe, body, load_end)

        @block.scalar
        def _(act):
            act = nc.scalar

            def split(t, half):
                if t.at_least(2):
                    act.wait_ge(h_filled, (t.n - 1) * FC)
                act.wait_ge(w_in[t.i], t.quad * 16 + 16)
                act.activation(halves(Wh[t.par], half), halves(W[t.i][0:KC, W1O:W2O], half), ACT.Copy).then_inc(wh_ready, 1)

            def body(t):
                if t.opens:
                    split(t, 0)
                    split(t, 1)
                act.wait_ge(w_in[t.i], t.quad * 16 + 16)
                if t.at_least(2):
                    act.wait_ge(y_filled, t.n - 1)
                for f in range(FC):
                    act.wait_ge(h_filled, t.n * FC + f + 1)
                    act.activation(Gl[t.par][:, f, :], h_ps[f % 3][:, 0:ROWS], ACT.Gelu,
                                   bias=W[t.i][:, B1O + f:B1O + f + 1]).then_inc(g_ready, 1)
                    if not t.closes and f in (2, 5):
                        split(t.next(), f // 3)

            tiles(act, body, load_end)

        @block.vector
        def _(dve):
            nonlocal made

            def turned(t):
                dve.wait_ge(xt_filled, t.n + 1)
                if t.at_least(2):
                    dve.wait_ge(h_filled, (t.n - 1) * FC)
                xt = xt_ps[0:KC, :].rearrange("p (c t) -> p c t", c=2)
                dve.tensor_copy(XTh[t.par][:], xt).then_inc(xh_ready, 1)
                dve.wait_ge(xh_ready, t.n + 1)
                dve.tensor_tensor(XTl[t.par][:], xt, XTh[t.par][:], ALU.subtract).then_inc(xt_ready, 1)

            def split(t, half):
                dve.wait_ge(wh_ready, t.n * 2 + (half + 1))
                dve.tensor_tensor(halves(Wl[t.par], half), halves(W[t.i][0:KC, W1O:W2O], half), halves(Wh[t.par], half),
                                  ALU.subtract).then_inc(wl_ready, 1)

            def finish(t):
                dve.wait_ge(y_filled, t.n + 1)
                b2 = W[t.i][:, B2O:B2O + D].rearrange("p (a d) -> p a d", a=1).broadcast_to([P, ROWS // P, D])
                dve.tensor_tensor(Yb[:], y_ps[:, 0:ROWS // P * D].rearrange("p (t d) -> p t d", d=D), b2, ALU.add).then_inc(yb_ready, 1)
                dve.wait_ge(ids_ready, t.n + 1)
                if t.at_least(DEPTH):
                    dve.wait_ge(y_out[t.i], t.quad * 32)
                if t.unique:
                    first = SWITCH + (t.i < CT % DEPTH)
                    dve.wait_ge(base_in[t.i], (t.quad - first) * 32 + 32)
                dve.wait_ge(yb_ready, t.n + 1)
                for k in range(ROWS // P):
                    more_ = base[t.i][:, k, :] if t.unique else X[t.i][:, k, D + 2:RC]
                    ins = dve.scalar_tensor_tensor(Y[t.i][:, k, :], Yb[:, k, :], X[t.i][:, k, D:D + 1], more_, ALU.mult, ALU.add)
                ins.then_inc(y_ready, 1)

            start = made

            def test(k, step0):
                dve.tensor_scalar(cand[:], T[:], step[:, 0:1], None, ALU.add).then_inc(v, 1)
                dve.wait_ge(v, step0 + 1)
                dve.tensor_tensor(flag[:], key[:], by_e(cand[:]), ALU.is_ge).then_inc(v, 1)
                dve.wait_ge(v, step0 + 2)
                dve.tensor_reduce(part[:], flag[:], AX.X, ALU.add).then_inc(part_ready, 1)

            def take(k, step0):
                dve.wait_ge(counted, k + 1)
                dve.tensor_scalar(gain[:], cnt_ps[:, 0:NX], float(CAP), step[:, 0:1], ALU.is_ge, ALU.mult).then_inc(v, 1)
                dve.wait_ge(v, step0 + 3)
                dve.tensor_scalar(step[:], step[:], 0.5, None, ALU.mult).then_inc(v, 1)
                dve.tensor_tensor(T[:], T[:], gain[:], ALU.add).then_inc(v, 1)
                dve.wait_ge(v, step0 + 5)

            def ties():
                done(dve.tensor_tensor(flag[:], key[:], by_e(T[:]), ALU.is_gt))
                dve.tensor_reduce(part[:], flag[:], AX.X, ALU.add).then_inc(part_ready, 1)
                done(dve.tensor_tensor(tie[:], key[:], by_e(T[:]), ALU.is_equal))
                done(dve.tensor_tensor(tie[:], tie[:], OH[:, 0], ALU.mult))
                dve.sem_inc(ranks_in, 1)

            def drops():
                dve.wait_ge(counted, 2 * DEPTH * SEARCH + 1)
                done(dve.tensor_scalar(need[:], cnt_ps[:, 0:NX], -1.0, float(CAP), ALU.mult, ALU.add))
                for f in column_ranks(1):
                    f()
                done(dve.tensor_tensor(rk[:], rk[:], by_e(need[:]), ALU.is_ge))
                done(dve.tensor_tensor(rk[:], rk[:], tie[:], ALU.mult))
                done(dve.tensor_tensor(flag[:], key[:], by_e(T[:]), ALU.is_lt))
                done(dve.tensor_tensor(flag[:], flag[:], OH[:, 0], ALU.mult))
                done(dve.tensor_tensor(flag[:], flag[:], rk[:], ALU.add))
                done(dve.tensor_reduce(drop[:], over_e(flag[:]), AX.X, ALU.add))
                done(dve.tensor_tensor(OH[:, 1], OH[:, 1], by_c(drop[:]), ALU.mult))
                dve.sem_inc(ranks_in, 1)

            unique_place = column_ranks(2) + place(1, CT, TILES) + [
                lambda: done(dve.tensor_scalar(drop[:], drop[:], -float(unique_rows), float(unique_rows), ALU.mult, ALU.add)),
                lambda: done(dve.tensor_tensor(pos[:, 1, :], posf[:], drop[:], ALU.add)),
                lambda: dve.sem_inc(placed, 1)]

            def body(t):
                nonlocal made
                if t.opens:
                    turned(t)
                    split(t, 0)
                    split(t, 1)
                if not t.closes:
                    turned(t.next())
                if t.search:
                    if t.number != 0:
                        take(t.n * 2 - 1, t.n * 10 + (start - 5))
                    test(t.n * 2, t.n * 10 + start)
                if not t.closes:
                    split(t.next(), 0)
                if t.search:
                    take(t.n * 2, t.n * 10 + start)
                    test(t.n * 2 + 1, t.n * 10 + (start + 5))
                if t.number == SETTLE * DEPTH:
                    take(t.n * 2 - 1, t.n * 10 + (start - 5))
                    made = start + 10 * t.n
                    ties()
                if t.number == SETTLE * DEPTH + 1:
                    drops()
                if t.number == SETTLE * DEPTH + 2:
                    for f in unique_place[:8]:
                        f()
                if t.number == SETTLE * DEPTH + 3:
                    for f in unique_place[8:]:
                        f()
                if not t.closes:
                    split(t.next(), 1)
                if not t.opens:
                    finish(t.before(1))
                if t.closes:
                    finish(t)

            tiles(dve, body, load_end)


def build(nc, A, out):
    ctx = ExitStack()
    with ctx:
        def sb(name, shape, dt=F32):
            return ctx.enter_context(nc.sbuf_tensor(name, shape, dt))

        logits = sb("logits", [NE, B, S])
        h2_d = nc.dram_tensor("h2_d", [B, S, D], F32).ap()
        xn2_d = nc.dram_tensor("xn2_d", [B, S, D], F32).ap()
        xc_d = nc.dram_tensor("xc_d", [CT * ROWS, RC], F32).ap()
        xu_d = nc.dram_tensor("xu_d", [(TILES - CT) * ROWS, RU], F32).ap()
        attention(nc, A, logits, h2_d, xn2_d, xc_d, xu_d)
        experts(nc, A, logits, h2_d, xn2_d, xc_d, xu_d, out)
    return nc


IN_NAMES = ["xT", "txt", "ident", "masks", "cosw", "sinw", "base", "biasb", "w_emb", "w_qkv", "w_o", "w_r", "rconsts", "before", "experts"]


def layout(I):
    a = {k: np.asarray(v) for k, v in I.items()}
    side, pp = 14, 16
    x = a["x"].reshape(B, side, pp, side, pp, 3).transpose(0, 5, 2, 4, 1, 3).reshape(B, EC, P, NPATCH)
    xT = np.zeros((B, P, EC, NPATCH + 1), np.float32)
    xT[:, :, :, 1:] = x.transpose(0, 2, 1, 3)
    o = {"xT": xT, "txt": a["txt"]}
    o["ident"] = np.eye(P, dtype=np.float32)
    i = np.arange(P)
    later = np.where(i[None, :] > i[:, None], BIG, 0.0)
    o["masks"] = np.stack([later, later.T], 1).astype(np.float32)
    inv = (1.0 / np.float32(10000.0) ** (np.arange(D // 2, dtype=np.float32) * np.float32(2.0) / np.float32(D))).astype(np.float32)
    ang = (np.arange(TT * P, dtype=np.float32)[:, None] * inv[None, :]).astype(np.float32)
    cos = np.repeat(np.cos(ang).astype(np.float32), 2, 1)
    sin = np.repeat(np.sin(ang).astype(np.float32), 2, 1) * np.tile(np.float32([-1, 1]), D // 2)
    tiles = lambda t: np.ascontiguousarray(np.tile(t, (1, 2)).reshape(TT, P, 2 * D).transpose(1, 0, 2)).astype(np.float32)
    o["cosw"], o["sinw"] = tiles(cos), tiles(sin)
    pos = np.zeros((2 * P, D), np.float32)
    pos[:NPATCH + 1] = a["L0_tok_pos_embed"][0]
    bias = np.tile(a["L0_tok_b"], (2 * P, 1))
    bias[0] = a["L0_tok_cls_token"][0, 0]
    o["base"] = np.ascontiguousarray(pos.reshape(2, P, D).transpose(1, 0, 2))
    o["biasb"] = np.ascontiguousarray(bias.reshape(2, P, D).transpose(1, 0, 2))
    o["w_emb"] = np.ascontiguousarray(a["L0_tok_W"].T.reshape(EC, P, D).transpose(1, 0, 2))

    def chunks(w, bias):
        c = np.zeros((KC + 1, 2, w.shape[1]), np.float32)
        c[:KC, 0], c[:KC, 1], c[KC, 0] = w[:KC], w[KC:], bias
        return c

    o["w_qkv"] = chunks(np.concatenate([a[f"L0_attn_W{k}"] for k in "qkv"], 1), np.concatenate([a[f"L0_attn_b{k}"] for k in "qkv"]))
    o["w_o"] = chunks(a["L0_attn_Wo"], a["L0_attn_bo"])
    o["w_r"] = chunks(np.concatenate([a["L0_ffn_Wsc"], a["L0_ffn_Wsu"]], 1), np.concatenate([a["L0_ffn_bsc"], a["L0_ffn_bsu"]]))
    lane, col = np.arange(P)[:, None], np.arange(COLS)[None, :]
    c = dict(valid=(P * col + lane < N), ids=P * col + lane, seg=np.tile(col > 0, (P, NX)), rank=np.tile(NX - np.arange(NX), (P, 1)),
             kth=np.tile(ROWS * np.arange(KTH), (P, 1)), tile=np.tile(np.arange(TILES), (P, 1)), lane=lane, one=np.ones((P, NX)))
    o["rconsts"] = np.concatenate([c[k].astype(np.float32) for k in CONSTS], 1)
    o["before"] = (lane < np.arange(P)[None, :]).astype(np.float32)
    w = np.zeros((2, NX, P, WCOLS), np.float32)
    for i, kind in enumerate("cu"):
        w[i, :, :KC, W1O:W2O] = a[f"L0_ffn_W1{kind}"].reshape(NX, 2, KC, FF).transpose(0, 2, 1, 3).reshape(NX, KC, 2 * FF)
        w[i, :, :, W2O:B1O] = a[f"L0_ffn_W2{kind}"].reshape(NX, FC, P, D).transpose(0, 2, 1, 3).reshape(NX, P, FC * D)
        w[i, :, :, B1O:B2O] = a[f"L0_ffn_b1{kind}"].reshape(NX, FC, P).transpose(0, 2, 1)
        w[i, :, :, B2O:] = a[f"L0_ffn_b2{kind}"][:, None, :]
    o["experts"] = w.reshape(2 * NX * P, WCOLS)
    return o


def kernel(**inputs):
    import concourse.bacc as _bacc
    from concourse.bass_utils import run_bass_kernel_spmd as _run

    nc = _bacc.Bacc("TRN2", target_bir_lowering=False, num_devices=1)
    arrays, aps = {}, {}
    for name, array in layout(inputs).items():
        arrays[f"in_{name}_dram"] = np.ascontiguousarray(array)
        aps[name] = nc.dram_tensor(f"in_{name}_dram", array.shape, mybir.dt.from_np(array.dtype), kind="ExternalInput").ap()
    out = nc.dram_tensor("out_0_dram", (B, S, D), F32, kind="ExternalOutput").ap()
    build(nc, aps, out)
    r = _run(nc, [arrays], core_ids=[0])
    return r.results[0]["out_0_dram"]
```
